# Optimizing a Trainium2 kernel written in Bass

```python
import numpy as np
import jax
import jax.numpy as jnp

def _softmax(x, axis=-1):
    return jax.nn.softmax(x, axis=axis)

def _gelu(x):
    return jax.nn.gelu(x, approximate=True)

def _silu(x):
    return jax.nn.silu(x)

def _sigmoid(x):
    return jax.nn.sigmoid(x)

def _layernorm(x, axis=-1, eps=1e-05):
    m = jnp.mean(x, axis=axis, keepdims=True)
    v = jnp.var(x, axis=axis, keepdims=True)
    return (x - m) / jnp.sqrt(v + eps)

def _scatter_add(tgt, idx, src, axis=0):
    return tgt.at[idx].add(src)

def _segment_sum(src, seg, n):
    return jax.ops.segment_sum(src, seg, n)
kernel_name = 'mk_lm_tower_d1_tok_ids256_r4_76e77f'

def setup_inputs(seed: int=0):
    np.random.seed(seed)
    _w = jnp.asarray

    def _rec_inputs():
        import jax
        import jax.numpy as jnp
        _rk = jax.random.key(seed)
        x = jax.random.randint(jax.random.fold_in(_rk, 1), (32, 256), 0, 64, jnp.int32)
        return x
    x = _rec_inputs()

    def _L0_tok_setup():
        import jax, jax.numpy as jnp
        import numpy as np
        V, C, D, N_ROUNDS, WIN = (64, 8, 128, 3, 4)
        B, T = (16, 2048)
        EPS = 1e-05

        def _ln(x, g, b):
            mu = jnp.mean(x, axis=-1, keepdims=True)
            var = jnp.mean((x - mu) ** 2, axis=-1, keepdims=True)
            return (x - mu) * jax.lax.rsqrt(var + EPS) * g + b

        def _mlp2(x, w1, b1, w2, b2):
            return jax.nn.gelu(x @ w1 + b1, approximate=False) @ w2 + b2
        key = jax.random.key(seed)
        ks = iter(jax.random.split(key, 32))
        nrm = lambda shp, s: jax.random.normal(next(ks), shp, jnp.float32) * s
        inp = {'x': jax.random.randint(next(ks), (B, T), 0, V, dtype=jnp.int32), 'emb': nrm((V, D), 0.02), 'pos': nrm((C, D), 0.02), 'lw1': nrm((D, 2 * D), 0.05), 'lb1': jnp.zeros((2 * D,)), 'lw2': nrm((2 * D, D), 0.05), 'lb2': jnp.zeros((D,)), 'lln_g': jnp.ones((D,)), 'lln_b': jnp.zeros((D,)), 'pool_w': nrm((D, D), 0.05), 'pool_b': jnp.zeros((D,)), 'msg_w1': nrm((2 * D, D), 0.05), 'msg_b1': jnp.zeros((D,)), 'msg_w2': nrm((D, D), 0.05), 'msg_b2': jnp.zeros((D,)), 'upd_w1': nrm((2 * D, D), 0.05), 'upd_b1': jnp.zeros((D,)), 'upd_w2': nrm((D, D), 0.05), 'upd_b2': jnp.zeros((D,)), 'mln_g': jnp.ones((D,)), 'mln_b': jnp.zeros((D,)), 'bc_w': nrm((D, D), 0.05), 'bc_b': jnp.zeros((D,)), 'fln_g': jnp.ones((D,)), 'fln_b': jnp.zeros((D,)), 'head_w': nrm((D, V), 0.05)}
        return inp
    _L0_tok_all = _L0_tok_setup()
    _L0_tok_in = {k: v for k, v in _L0_tok_all.items() if k in ('emb', 'pos', 'lw1', 'lb1', 'lw2', 'lb2', 'lln_g', 'lln_b', 'pool_w', 'pool_b', 'msg_w1', 'msg_b1', 'msg_w2', 'msg_b2', 'upd_w1', 'upd_b1', 'upd_w2', 'upd_b2', 'mln_g', 'mln_b', 'bc_w', 'bc_b', 'fln_g', 'fln_b', 'head_w')}
    del _L0_tok_all

    def _L0_attn_setup():
        import jax, jax.numpy as jnp
        import numpy as np
        import math
        CHUNK = 128

        def _build_slopes(n):

            def p2(n):
                start = 2.0 ** (-2.0 ** (-(math.log2(n) - 3)))
                return [start ** (i + 1) for i in range(n)]
            if math.log2(n).is_integer():
                s = p2(n)
            else:
                c = 2 ** math.floor(math.log2(n))
                s = p2(c) + p2(2 * c)[0::2][:n - c]
            return np.asarray(s, dtype=np.float32)

        def _lightning_attn(q, k, v, slopes):
            b, h, l, d = q.shape
            n = l // CHUNK
            s = slopes.reshape(h, 1, 1)
            pos = jnp.arange(CHUNK, dtype=q.dtype)
            diff = pos[:, None] - pos[None, :]
            mask = jnp.where(diff >= 0, jnp.exp(-s * diff), 0.0)[None]
            q_dec = jnp.exp(-slopes[:, None] * pos)[None, :, :, None]
            k_dec = jnp.exp(-slopes[:, None] * (CHUNK - pos))[None, :, :, None]
            blk = jnp.exp(-slopes * CHUNK).reshape(1, h, 1, 1)
            qc = q.reshape(b, h, n, CHUNK, d).transpose(2, 0, 1, 3, 4)
            kc = k.reshape(b, h, n, CHUNK, d).transpose(2, 0, 1, 3, 4)
            vc = v.reshape(b, h, n, CHUNK, d).transpose(2, 0, 1, 3, 4)

            def step(S, xs):
                qi, ki, vi = xs
                scores = jnp.einsum('bhcd,bhed->bhce', qi, ki) * mask
                intra = jnp.einsum('bhce,bhed->bhcd', scores, vi)
                inter = jnp.einsum('bhcd,bhde->bhce', qi * q_dec, S)
                S_new = blk * S + jnp.einsum('bhcd,bhce->bhde', ki * k_dec, vi)
                return (S_new, intra + inter)
            S0 = jnp.zeros((b, h, d, d), q.dtype)
            _, o = jax.lax.scan(step, S0, (qc, kc, vc))
            return o.transpose(1, 2, 0, 3, 4).reshape(b, h, l, d)
        key = jax.random.key(seed)
        k1, k2, k3 = jax.random.split(key, 3)
        b, l, c, h = (8, 4096, 64, 8)
        x = jax.random.normal(k1, (b, l, c), dtype=jnp.float32)
        w_qkv = jax.random.normal(k2, (c, 3 * c), dtype=jnp.float32) * 0.02
        w_proj = jax.random.normal(k3, (c, c), dtype=jnp.float32) * 0.02
        b_proj = jnp.zeros((c,), dtype=jnp.float32)
        slopes = jnp.asarray(_build_slopes(h))
        return {'x': x, 'w_qkv': w_qkv, 'w_proj': w_proj, 'b_proj': b_proj, 'slopes': slopes}
    _L0_attn_all = _L0_attn_setup()
    _L0_attn_in = {k: v for k, v in _L0_attn_all.items() if k in ('w_qkv', 'w_proj', 'b_proj', 'slopes')}
    del _L0_attn_all

    def _L0_ffn_setup():
        import jax, jax.numpy as jnp
        import numpy as np
        B, S, D, F, E, K = (8, 512, 64, 256, 8, 2)
        key = jax.random.key(seed)
        ks = jax.random.split(key, 10)
        s = 0.02
        return {'x': jax.random.normal(ks[0], (B, S, D), dtype=jnp.float32), 'Wr': jax.random.normal(ks[1], (D, E), dtype=jnp.float32) * s, 'W1s': jax.random.normal(ks[2], (D, F), dtype=jnp.float32) * s, 'b1s': jnp.zeros((F,), dtype=jnp.float32), 'W2s': jax.random.normal(ks[3], (F, D), dtype=jnp.float32) * s, 'b2s': jnp.zeros((D,), dtype=jnp.float32), 'W1p': jax.random.normal(ks[4], (E, D, F), dtype=jnp.float32) * s, 'b1p': jnp.zeros((E, F), dtype=jnp.float32), 'W2p': jax.random.normal(ks[5], (E, F, D), dtype=jnp.float32) * s, 'b2p': jnp.zeros((E, D), dtype=jnp.float32)}
    _L0_ffn_all = _L0_ffn_setup()
    _L0_ffn_in = {k: v for k, v in _L0_ffn_all.items() if k in ('Wr', 'W1s', 'b1s', 'W2s', 'b2s', 'W1p', 'b1p', 'W2p', 'b2p')}
    del _L0_ffn_all
    return {'x': x, 'L0_tok_emb': _L0_tok_in['emb'], 'L0_tok_pos': _L0_tok_in['pos'], 'L0_tok_lw1': _L0_tok_in['lw1'], 'L0_tok_lb1': _L0_tok_in['lb1'], 'L0_tok_lw2': _L0_tok_in['lw2'], 'L0_tok_lb2': _L0_tok_in['lb2'], 'L0_tok_lln_g': _L0_tok_in['lln_g'], 'L0_tok_lln_b': _L0_tok_in['lln_b'], 'L0_tok_pool_w': _L0_tok_in['pool_w'], 'L0_tok_pool_b': _L0_tok_in['pool_b'], 'L0_tok_msg_w1': _L0_tok_in['msg_w1'], 'L0_tok_msg_b1': _L0_tok_in['msg_b1'], 'L0_tok_msg_w2': _L0_tok_in['msg_w2'], 'L0_tok_msg_b2': _L0_tok_in['msg_b2'], 'L0_tok_upd_w1': _L0_tok_in['upd_w1'], 'L0_tok_upd_b1': _L0_tok_in['upd_b1'], 'L0_tok_upd_w2': _L0_tok_in['upd_w2'], 'L0_tok_upd_b2': _L0_tok_in['upd_b2'], 'L0_tok_mln_g': _L0_tok_in['mln_g'], 'L0_tok_mln_b': _L0_tok_in['mln_b'], 'L0_tok_bc_w': _L0_tok_in['bc_w'], 'L0_tok_bc_b': _L0_tok_in['bc_b'], 'L0_tok_fln_g': _L0_tok_in['fln_g'], 'L0_tok_fln_b': _L0_tok_in['fln_b'], 'L0_tok_head_w': _L0_tok_in['head_w'], 'L0_attn_w_qkv': _L0_attn_in['w_qkv'], 'L0_attn_w_proj': _L0_attn_in['w_proj'], 'L0_attn_b_proj': _L0_attn_in['b_proj'], 'L0_attn_slopes': _L0_attn_in['slopes'], 'L0_ffn_Wr': _L0_ffn_in['Wr'], 'L0_ffn_W1s': _L0_ffn_in['W1s'], 'L0_ffn_b1s': _L0_ffn_in['b1s'], 'L0_ffn_W2s': _L0_ffn_in['W2s'], 'L0_ffn_b2s': _L0_ffn_in['b2s'], 'L0_ffn_W1p': _L0_ffn_in['W1p'], 'L0_ffn_b1p': _L0_ffn_in['b1p'], 'L0_ffn_W2p': _L0_ffn_in['W2p'], 'L0_ffn_b2p': _L0_ffn_in['b2p']}

def reference(x, L0_tok_emb, L0_tok_pos, L0_tok_lw1, L0_tok_lb1, L0_tok_lw2, L0_tok_lb2, L0_tok_lln_g, L0_tok_lln_b, L0_tok_pool_w, L0_tok_pool_b, L0_tok_msg_w1, L0_tok_msg_b1, L0_tok_msg_w2, L0_tok_msg_b2, L0_tok_upd_w1, L0_tok_upd_b1, L0_tok_upd_w2, L0_tok_upd_b2, L0_tok_mln_g, L0_tok_mln_b, L0_tok_bc_w, L0_tok_bc_b, L0_tok_fln_g, L0_tok_fln_b, L0_tok_head_w, L0_attn_w_qkv, L0_attn_w_proj, L0_attn_b_proj, L0_attn_slopes, L0_ffn_Wr, L0_ffn_W1s, L0_ffn_b1s, L0_ffn_W2s, L0_ffn_b2s, L0_ffn_W1p, L0_ffn_b1p, L0_ffn_W2p, L0_ffn_b2p):
    import jax
    import jax.numpy as jnp

    def _L0_tok_ref(x, emb, pos, lw1, lb1, lw2, lb2, lln_g, lln_b, pool_w, pool_b, msg_w1, msg_b1, msg_w2, msg_b2, upd_w1, upd_b1, upd_w2, upd_b2, mln_g, mln_b, bc_w, bc_b, fln_g, fln_b, head_w):
        import jax, jax.numpy as jnp
        import numpy as np
        V, C, D, N_ROUNDS, WIN = (64, 8, 128, 3, 4)
        B, T = (16, 2048)
        EPS = 1e-05

        def _ln(x, g, b):
            mu = jnp.mean(x, axis=-1, keepdims=True)
            var = jnp.mean((x - mu) ** 2, axis=-1, keepdims=True)
            return (x - mu) * jax.lax.rsqrt(var + EPS) * g + b

        def _mlp2(x, w1, b1, w2, b2):
            return jax.nn.gelu(x @ w1 + b1, approximate=False) @ w2 + b2
        Bv, Tv = x.shape
        pad = -Tv % C
        padded_T = Tv + pad
        n_chunks = padded_T // C
        x_pad = jnp.pad(x, ((0, 0), (0, pad)))
        chunks = x_pad.reshape(Bv, n_chunks, C)
        h = emb[chunks] + pos[None, None, :, :]
        local = h + _mlp2(_ln(h, lln_g, lln_b), lw1, lb1, lw2, lb2)
        summ = local.mean(axis=2) @ pool_w + pool_b
        i = jnp.arange(n_chunks)[:, None]
        d = jnp.arange(WIN + 1)[None, :]
        idx = jnp.clip(i - d, 0, None)
        valid = (i - d >= 0).astype(summ.dtype)
        count = valid.sum(axis=1)
        hmsg = summ
        for _ in range(N_ROUNDS):
            nbr = hmsg[:, idx]
            self_e = jnp.broadcast_to(hmsg[:, :, None, :], nbr.shape)
            msgs = _mlp2(jnp.concatenate([self_e, nbr], -1), msg_w1, msg_b1, msg_w2, msg_b2)
            agg = (msgs * valid[None, :, :, None]).sum(axis=2) / count[None, :, None]
            upd = _mlp2(jnp.concatenate([hmsg, agg], -1), upd_w1, upd_b1, upd_w2, upd_b2)
            hmsg = _ln(hmsg + upd, mln_g, mln_b)
        bc = hmsg @ bc_w + bc_b
        combined = (local + bc[:, :, None, :]).reshape(Bv, padded_T, D)[:, :Tv, :]
        logits = _ln(combined, fln_g, fln_b) @ head_w
        return logits

    def _L0_attn_ref(x, w_qkv, w_proj, b_proj, slopes):
        import jax, jax.numpy as jnp
        import numpy as np
        import math
        CHUNK = 128

        def _build_slopes(n):

            def p2(n):
                start = 2.0 ** (-2.0 ** (-(math.log2(n) - 3)))
                return [start ** (i + 1) for i in range(n)]
            if math.log2(n).is_integer():
                s = p2(n)
            else:
                c = 2 ** math.floor(math.log2(n))
                s = p2(c) + p2(2 * c)[0::2][:n - c]
            return np.asarray(s, dtype=np.float32)

        def _lightning_attn(q, k, v, slopes):
            b, h, l, d = q.shape
            n = l // CHUNK
            s = slopes.reshape(h, 1, 1)
            pos = jnp.arange(CHUNK, dtype=q.dtype)
            diff = pos[:, None] - pos[None, :]
            mask = jnp.where(diff >= 0, jnp.exp(-s * diff), 0.0)[None]
            q_dec = jnp.exp(-slopes[:, None] * pos)[None, :, :, None]
            k_dec = jnp.exp(-slopes[:, None] * (CHUNK - pos))[None, :, :, None]
            blk = jnp.exp(-slopes * CHUNK).reshape(1, h, 1, 1)
            qc = q.reshape(b, h, n, CHUNK, d).transpose(2, 0, 1, 3, 4)
            kc = k.reshape(b, h, n, CHUNK, d).transpose(2, 0, 1, 3, 4)
            vc = v.reshape(b, h, n, CHUNK, d).transpose(2, 0, 1, 3, 4)

            def step(S, xs):
                qi, ki, vi = xs
                scores = jnp.einsum('bhcd,bhed->bhce', qi, ki) * mask
                intra = jnp.einsum('bhce,bhed->bhcd', scores, vi)
                inter = jnp.einsum('bhcd,bhde->bhce', qi * q_dec, S)
                S_new = blk * S + jnp.einsum('bhcd,bhce->bhde', ki * k_dec, vi)
                return (S_new, intra + inter)
            S0 = jnp.zeros((b, h, d, d), q.dtype)
            _, o = jax.lax.scan(step, S0, (qc, kc, vc))
            return o.transpose(1, 2, 0, 3, 4).reshape(b, h, l, d)
        b, l, c = x.shape
        h = slopes.shape[0]
        d = c // h
        scale = d ** (-0.5)
        qkv = (x @ w_qkv).reshape(b, l, 3, h, d)
        q = qkv[:, :, 0].transpose(0, 2, 1, 3) * scale
        k = qkv[:, :, 1].transpose(0, 2, 1, 3)
        v = qkv[:, :, 2].transpose(0, 2, 1, 3)
        o = _lightning_attn(q, k, v, slopes)
        out = o.transpose(0, 2, 1, 3).reshape(b, l, c) @ w_proj + b_proj
        return out

    def _L0_ffn_ref(x, Wr, W1s, b1s, W2s, b2s, W1p, b1p, W2p, b2p):
        import jax, jax.numpy as jnp
        import numpy as np
        B, S, D, F, E, K = (8, 512, 64, 256, 8, 2)
        gelu = lambda t: jax.nn.gelu(t, approximate=False)
        shared = gelu(x @ W1s + b1s) @ W2s + b2s
        rw = jax.nn.softmax(x @ Wr, axis=-1)
        topw, topi = jax.lax.top_k(rw, K)
        topw = topw / jnp.sum(topw, axis=-1, keepdims=True)
        mask = jnp.sum(jax.nn.one_hot(topi, E, dtype=topw.dtype) * topw[..., None], axis=-2)
        h = gelu(jnp.einsum('bsd,edf->bsef', x, W1p) + b1p)
        priv = jnp.einsum('bsef,efd->bsed', h, W2p) + b2p
        routed = jnp.einsum('bsed,bse->bsd', priv, mask)
        return shared + routed
    h = _L0_tok_ref(x, L0_tok_emb, L0_tok_pos, L0_tok_lw1, L0_tok_lb1, L0_tok_lw2, L0_tok_lb2, L0_tok_lln_g, L0_tok_lln_b, L0_tok_pool_w, L0_tok_pool_b, L0_tok_msg_w1, L0_tok_msg_b1, L0_tok_msg_w2, L0_tok_msg_b2, L0_tok_upd_w1, L0_tok_upd_b1, L0_tok_upd_w2, L0_tok_upd_b2, L0_tok_mln_g, L0_tok_mln_b, L0_tok_bc_w, L0_tok_bc_b, L0_tok_fln_g, L0_tok_fln_b, L0_tok_head_w)
    h = h + _L0_attn_ref(_layernorm(h, axis=-1), L0_attn_w_qkv, L0_attn_w_proj, L0_attn_b_proj, L0_attn_slopes)
    h = h + _L0_ffn_ref(_layernorm(h, axis=-1), L0_ffn_Wr, L0_ffn_W1s, L0_ffn_b1s, L0_ffn_W2s, L0_ffn_b2s, L0_ffn_W1p, L0_ffn_b1p, L0_ffn_W2p, L0_ffn_b2p)
    return h

_drawn_inputs = setup_inputs


def setup_inputs(seed=0):
    import zlib

    import numpy as np

    out = dict(_drawn_inputs(seed))
    spreads = {'L0_tok_lb1': (0.0, 0.1),
     'L0_tok_lb2': (0.0, 0.1),
     'L0_tok_lln_g': (1.0, 0.2),
     'L0_tok_lln_b': (0.0, 0.1),
     'L0_tok_pool_b': (0.0, 0.1),
     'L0_tok_msg_b1': (0.0, 0.382),
     'L0_tok_msg_b2': (0.0, 0.1),
     'L0_tok_upd_b1': (0.0, 0.1),
     'L0_tok_upd_b2': (0.0, 0.1),
     'L0_tok_mln_g': (1.0, 0.2),
     'L0_tok_mln_b': (0.0, 0.1),
     'L0_tok_bc_b': (0.0, 0.1),
     'L0_tok_fln_g': (1.0, 0.2),
     'L0_tok_fln_b': (0.0, 0.1),
     'L0_attn_b_proj': (0.0, 0.1),
     'L0_ffn_b1s': (0.0, 0.296),
     'L0_ffn_b2s': (0.0, 0.1),
     'L0_ffn_b1p': (0.0, 0.42),
     'L0_ffn_b2p': (0.0, 0.1)}
    factors = {}
    for name, (base, spread) in spreads.items():
        noise = np.random.default_rng([zlib.crc32(name.encode()), seed]).standard_normal(out[name].shape)
        drawn = base * np.exp(spread * noise) if base else spread * noise
        out[name] = jnp.asarray(drawn.astype(out[name].dtype))
    for name, factor in factors.items():
        out[name] = (out[name] * factor).astype(out[name].dtype)
    return out
```

```python
from contextlib import ExitStack

import concourse.bass as bass
from concourse import mybir
from concourse.alu_op_type import AluOpType as ALU

ACT = mybir.ActivationFunctionType
F32 = mybir.dt.float32
F16 = mybir.dt.float16
BF16 = mybir.dt.bfloat16
I32 = mybir.dt.int32
AX_X = mybir.AxisListType.X

P = 128
VOCAB, POS, DT, ROUNDS, WIN = 64, 8, 128, 3, 4
NB, SEQ = 32, 256
CPB = SEQ // POS
NCHUNK = NB * CPB
HALF = NCHUNK // 2
HB = HALF // CPB
D, H, DH = 64, 8, 8
CH = 128
F, E = 256, 8
NT1 = 2 * (E + 1)
EPS = 1e-5
PER_QUAD = 54
SW = 64.0
NQ = NCHUNK // P
QT = P * POS
TAB = DT + D
TABP = TAB + DT

C_ID, C_CEN, C_DIFF, C_CAUS, C_II, C_BLK = 0, 128, 256, 384, 512, 576
C_THR, C_LOW, C_COL, C_INV, C_NEGC, C_END = 640, 648, 712, 720, 752, 880
W_Q, W_K, W_V, W_KC, W_QC, W_P, W_R, W_END = 0, 256, 512, 576, 640, 704, 768, 776
T_L1, T_L2, T_MA, T_MB, T_M2, T_UA, T_UB, T_U2 = 0, 256, 512, 640, 768, 896, 1024, 1152
T_PW, T_BC, T_BCT, T_HW, T_END = 1280, 1408, 1536, 1664, 1728
(B_L1, B_L2, B_LG, B_LB, B_PB, B_M1, B_M2, B_U1, B_MG, B_MB, B_BC, B_FG, B_FB, B_END) = (
    0, 2, 3, 4, 5, 6, 7, 8, 9, 10, 11, 12, 13, 14)


class Steps:

    def __init__(self, eng, sem):
        self.eng, self.sem, self.origin, self.k = eng, sem, 0, 0

    def step(self, ins):
        ins.then_inc(self.sem, 1)
        self.k += 1

    def settle(self):
        self.eng.wait_ge(self.sem, self.origin + self.k)

    def enter(self, i, first, per):
        self.start = self.origin + self.k
        self.per = per
        self.origin, self.k = self.start + (i - first) * per, 0

    def leave(self, times):
        assert self.k == self.per, ("steps in the loop's body", self.k)
        self.origin, self.k = self.start + times * self.per, 0


def build(nc, ids, emb, pos, consts, towerw, towerb, updb2, attnw, bproj, slopes, w1, b1, w2, b2, out):
    mask_rows = nc.dram_tensor("mask_rows", [NQ, E * POS, P], F32).ap()
    out_v = out.rearrange("b (j c) d -> (b j) (c d)", c=POS)

    with ExitStack() as ctx:
        def sb(name, shape, dt=F32):
            return ctx.enter_context(nc.sbuf_tensor(name, shape, dt))

        PS = ctx.enter_context(nc.psum_tensor("PS", [P, 8, 512], F32))
        BANK_A, BANK_T, BANK_Q, BANK_O = 4, 5, 6, 7

        cst = sb("cst", [P, C_END])
        ident = cst[:, C_ID:C_ID + P]
        identb = sb("identb", [P, P], BF16)
        identh = sb("identh", [P, P], F16)
        pair_sum = sb("pair_sum", [P, D], F16)
        tw = sb("tw", [P, T_END])
        tb = sb("tb", [P, B_END])
        updb2_bc = sb("updb2_bc", [P, DT])
        bproj_bc = sb("bproj_bc", [P, D])
        slope_bc = sb("slope_bc", [P, H])
        slope_row = sb("slope_row", [P, H, DH])
        neg_slope = sb("neg_slope", [P, H])
        slope_col = sb("slope_col", [D, 1])
        wa = sb("wa", [P, W_END])
        wa_hi = sb("wa_hi", [P, W_END], F16)
        wa_lo = sb("wa_lo", [P, W_END], F16)
        w1_hi = sb("w1_hi", [P, NT1, P], F16)
        w1_lo = sb("w1_lo", [P, NT1, P], F16)
        w2_sb = sb("w2_sb", [P, NT1, D])
        b1_sb = sb("b1_sb", [P, NT1])
        b2_sb = sb("b2_sb", [P, 1 + E // 2])
        minus_half = sb("minus_half", [P, POS])

        slab2 = sb("slab2", [P, POS * NCHUNK // 2])
        onehot = slab2[:, :].bitcast(BF16).rearrange("p (c n) -> p c n", c=POS)
        embt = sb("embt", [P, DT])
        postab = sb("postab", [P, 4, DT])
        htab = sb("htab", [P, 4, DT])
        table = sb("table", [P, POS, TABP], BF16)
        table3 = sb("table3", [P, POS, TABP], BF16)
        bcparts = sb("bcparts", [P, 3, NQ, TAB], BF16)
        rt = sb("rt", [P, TAB])
        bx = sb("bx", [P, TAB])
        gh = sb("gh", [P, D])
        fb_bc = sb("fb_bc", [P, P])
        hb = sb("hb", [P, D])
        hT = sb("hT", [P, 2, HALF])
        slab = sb("slab", [P, 10240])
        w1_raw = slab[:, 10240 - NT1 * P:10240]
        pre = slab[:, 0:2 * (WIN + 1) * HALF].rearrange("p (f d n) -> p f d n", f=2, d=WIN + 1)
        slab3 = sb("slab3", [P, 12 * HALF])

        def part3(k, n, dt=F32):
            x = slab3[:, k * HALF:(k + n) * HALF]
            return x if dt is F32 else x.bitcast(dt)

        lnT, g1 = part3(0, 1), part3(1, 2).rearrange("p (f n) -> p f n", f=2)
        xt = part3(3, 1).rearrange("p (t n) -> p t n", t=4)
        locd = part3(4, 2).rearrange("p (c k v) -> p c k v", c=POS, k=2)
        locdb = part3(6, 2).rearrange("p (c k v) -> p c k v", c=POS, k=2)
        tab_top = sb("tab_top", [P, 2, TABP], BF16)
        tab_rest = sb("tab_rest", [P, TABP])
        a_sb = part3(8, 2).rearrange("p (f n) -> p f n", f=2)
        msum = part3(10, 2).rearrange("p (f n) -> p f n", f=2)
        agg_sb = a_sb
        gu_sb = msum
        rtok = lnT.rearrange("p (t n) -> p t n", t=4), g1[:, 0, :].rearrange("p (t n) -> p t n", t=4)
        bc_rest = slab[:, 0:NQ * TAB]
        ids_stage = slab[:, 0:4 * NCHUNK].bitcast(I32).rearrange("p (k n) -> p k n", k=2)
        psT16 = PS[:, BANK_T, :].bitcast(F16)
        GR = 6
        gring = slab[:, 0:GR * QT].rearrange("p (s n) -> p s n", s=GR)
        mb = slab[:, GR * QT:GR * QT + 4 * QT].rearrange("p (s n) -> p s n", s=4)

        h_res = sb("h_res", [P, NQ * POS * D])
        xs1 = sb("xs1", [P, QT], F16)
        xs2 = sb("xs2", [P, NQ * QT], F16)
        u_sb = part3(3, 1).rearrange("p (c n) -> p c n", c=POS)
        xn = part3(1, 1).rearrange("p (c n) -> p c n", c=POS)
        xhl = part3(4, 1, F16).rearrange("p (c n) -> p c n", c=POS)
        xn2 = part3(2, 1).rearrange("p (c n) -> p c n", c=POS)
        xhl2 = part3(5, 1, F16).rearrange("p (c n) -> p c n", c=POS)
        q32 = slab[:, 4 * QT:5 * QT].bitcast(F16).rearrange("p (g n) -> p g n", g=2)
        k32 = slab[:, 5 * QT:6 * QT].bitcast(F16).rearrange("p (g n) -> p g n", g=2)
        qk_hi = sb("qk_hi", [P, 4, 512], F16)
        vx = sb("vx", [P, POS, 2, 160])
        vdec = sb("vdec", [P, 4, D])
        ktok = sb("ktok", [P, 4, D])
        sbd = sb("sbd", [P, 4, D])
        qdec = sb("qdec", [P, 4, CH])
        probs = slab[:, 0:4 * QT].rearrange("p (s j n) -> p s j n", s=2, j=4)
        decay = sb("decay", [P, 4, 2, CH])
        kdec = sb("kdec", [P, D])
        dec = sb("dec", [D, CH])
        ostk = part3(8, 1, F16)
        st = {n: sb(f"st_{n}", [P, POS, 6]) for n in ("t", "f", "a", "c")}
        stx = {n: sb(f"stx_{n}", [P, 6, POS]) for n in ("t", "f", "a", "c")}
        rstd = {n: sb(f"rstd_{n}", [P, POS]) for n in ("t", "f", "a", "c")}
        rmax = sb("rmax", [P, 4, POS])
        rlog = sb("rlog", [P, POS, E])
        rexp = sb("rexp", [P, POS, E])
        rw = sb("rw", [P, POS, E])
        rge = part3(6, 1).rearrange("p (c e j) -> p c e j", c=POS, e=E)
        rdf = part3(7, 1).rearrange("p (c e j) -> p c e j", c=POS, e=E)
        rank = sb("rank", [P, POS, E])
        mtok = sb("mtok", [P, P])
        mT = sb("mT", [D, P])
        yacc = slab2[:, 0:QT]
        ytmp = slab2[:, QT:2 * QT]
        y_hi = slab2[:, 2 * QT:5 * QT // 2].bitcast(F16)
        y_lo = slab2[:, 5 * QT // 2:3 * QT].bitcast(F16)
        obuf = sb("obuf", [P, POS * D])

        SEMS = {}

        def s(name):
            if name not in SEMS:
                SEMS[name] = ctx.enter_context(nc.semaphore(name))
            return SEMS[name]

        block = ctx.enter_context(nc.Block())

        @block.sync
        def _(sp):
            for k in range(2):
                sp.dma_start(embt[64 * k:64 * k + 64, :], emb).then_inc(s("ld_emb"), 16)
            for c in range(POS):
                sp.dma_start(postab[64 * (c % 2):64 * (c % 2) + 64, c // 2, :],
                             pos[c, :].partition_broadcast(64)).then_inc(s("ld_emb"), 16)
            sp.dma_start(tb[:, :], towerb).then_inc(s("ld_tow"), 16)
            sp.dma_start(tw[:, :], towerw).then_inc(s("ld_tow"), 16)
            for k in range(4):
                if k >= 2:
                    sp.wait_ge(s("onehot_ready"), k - 1)
                sp.dma_start(ids_stage[:, k % 2, :],
                             ids[2 * k * NCHUNK:2 * (k + 1) * NCHUNK].partition_broadcast(P)
                             ).then_inc(s(f"ld_ids{k}"), 16)
            sp.dma_start(updb2_bc[:, :], updb2.partition_broadcast(P)).then_inc(s("ld_rows"), 16)
            sp.dma_start(bproj_bc[:, :], bproj.partition_broadcast(P)).then_inc(s("ld_rows"), 16)
            sp.dma_start(w2_sb[:, :, :], w2.rearrange("p (t n) -> p t n", t=NT1)).then_inc(s("ld_ffn"), 16)
            sp.dma_start(b1_sb[:, :], b1).then_inc(s("ld_ffn"), 16)
            sp.dma_start(b2_sb[:, :], b2).then_inc(s("ld_ffn"), 16)
            with sp.Fori(0, NQ) as q:
                sp.wait_ge(s("mT_ready"), q + 1)
                sp.dma_start(mask_rows[bass.ds(q, 1)].rearrange("q r p -> (q r) p"), mT[:, :]
                             ).then_inc(s("m_stored"), 16)

            def load_masks(q, free):
                sp.wait_ge(s("m_stored"), q * 16 + 16)
                for pr in range(E // 2):
                    if free is not None:
                        sp.wait_ge(s("m_used"), free + pr)
                    for k in range(2):
                        e = 2 * pr + k
                        sp.dma_start(
                            mb[64 * k:64 * k + 64, pr:pr + 1, :],
                            mask_rows[bass.ds(q, 1), e * POS:(e + 1) * POS, :].rearrange("q r p -> q (r p)")
                            .partition_broadcast(64)).then_inc(s(f"m_loaded{pr}"), 16)

            sp.wait_ge(s("w1_ready"), 1)
            load_masks(0, None)
            with sp.Fori(1, NQ) as q:
                load_masks(q, q * 4 - 3)
            sp.wait_ge(s("out_done"), 16 * NQ)

        @block.tensor
        def _(pe):
            def mm(o, lhsT, rhs, start=True, stop=True):
                return nc.tensor.matmul(o, lhsT, rhs, start=start, stop=stop, skip_group_check=True)

            pe.wait_ge(s("xt_ready"), 4)
            for k in range(4):
                i = nc.tensor.transpose(PS[:, 0, k * P:(k + 1) * P], xt[:, k, :], ident)
            i.then_inc(s("xtT"), 1)
            pe.wait_ge(s("ld_tow"), 32)
            pe.wait_ge(s("lnT_ready"), 1)
            for f in range(2):
                mm(PS[:, 1 + f, :], tw[:, T_L1 + f * P:T_L1 + (f + 1) * P], lnT[:, :]).then_inc(s("mlp1"), 1)
            for f in range(2):
                pe.wait_ge(s("g1_ready"), f + 1)
                mm(PS[:, 3, :], tw[:, T_L2 + f * P:T_L2 + (f + 1) * P], g1[:, f, :], start=f == 0, stop=False)
            for k in range(4):
                i = mm(PS[:, 3, k * P:(k + 1) * P], htab[:, k, :], ident, start=False, stop=True)
            i.then_inc(s("mlp2"), 1)
            pe.wait_ge(s("gh_ready"), 1)
            mm(PS[:, 4, 0:D], cst[:, C_CEN:C_CEN + P], gh[:, :]).then_inc(s("ghc"), 1)
            pe.wait_ge(s("rt_ready"), 1)
            mm(PS[:, 4, 64:64 + D], fb_bc[:, :], tw[:, T_HW:T_HW + D]).then_inc(s("hb_mm"), 1)
            pe.wait_ge(s("hb_ready"), 1)
            mm(PS[:, 4, 128:128 + D], tw[:, T_BCT:T_BCT + P], rt[:, DT:TAB]).then_inc(s("bx_mm"), 1)
            pe.wait_ge(s("locb_ready"), 1)
            for c in range(POS):
                if c >= 2:
                    pe.wait_ge(s("tab_ready"), c - 1)
                mm(PS[:, 5 + c % 2, 0:TAB], locdb[:, c, :, :], rt[:, :])
                mm(PS[:, 5 + c % 2, TAB:TABP], locd[:, c, :, :], tw[:, T_PW:T_PW + P]).then_inc(s("tab_mm"), 1)
            pe.wait_ge(s("tab_ready"), POS)
            pe.wait_ge(s("onehot_ready"), 4)
            for f in range(2):
                for c in range(POS):
                    oh = onehot[:, c, f * HALF:(f + 1) * HALF]
                    mm(PS[:, 4 * f, :], table[:, c, TAB:TABP], oh, start=c == 0, stop=False)
                    i = mm(PS[:, 4 * f, :], table3[:, c, TAB:TABP], oh, start=False, stop=c == POS - 1)
                i.then_inc(s("summ"), 1)
            for r in range(ROUNDS):
                for f in range(2):
                    k = 2 * r + f + 1
                    pe.wait_ge(s("h_ready"), k)
                    mm(PS[:, 4 * f, :], tw[:, T_MA:T_MA + P], hT[:, f, :])
                    mm(PS[:, 4 * f + 1, :], tw[:, T_MB:T_MB + P], hT[:, f, :]).then_inc(s("t_ab"), 1)
                for f in range(2):
                    k = 2 * r + f + 1
                    pe.wait_ge(s("t_sum"), k)
                    mm(PS[:, 4 * f + 2, :], tw[:, T_M2:T_M2 + P], msum[:, f, :]).then_inc(s("t_agg"), 1)
                    mm(PS[:, 4 * f + 3, :], tw[:, T_UA:T_UA + P], hT[:, f, :], start=True, stop=False)
                for f in range(2):
                    pe.wait_ge(s("t_aggs"), 2 * r + f + 1)
                    mm(PS[:, 4 * f + 3, :], tw[:, T_UB:T_UB + P], agg_sb[:, f, :], start=False, stop=True
                       ).then_inc(s("t_u"), 1)
                for f in range(2):
                    pe.wait_ge(s("t_gu"), 2 * r + f + 1)
                    for t in range(4):
                        o = PS[:, 4 * f, t * P:(t + 1) * P]
                        mm(o, gu_sb[:, f, t * P:(t + 1) * P], tw[:, T_U2:T_U2 + P], start=True, stop=False)
                        i = mm(o, hT[:, f, t * P:(t + 1) * P], ident, start=False, stop=True)
                    i.then_inc(s("t_r"), 1)
                for f in range(2):
                    pe.wait_ge(s("t_xc"), 4 * (2 * r + f + 1))
                    for t in range(4):
                        i = nc.tensor.transpose(PS[:, 4 * f + 1, t * P:(t + 1) * P], rtok[f][:, t, :], ident)
                    i.then_inc(s("t_T"), 1)
            pe.wait_ge(s("h_ready"), 2 * ROUNDS + 2)
            pe.wait_ge(s("bx_ready"), 1)
            for q in range(NQ):
                o = PS[:, q // 2, (q % 2) * TAB:(q % 2 + 1) * TAB]
                i = mm(o, hT[:, q // 4, (q % 4) * P:(q % 4 + 1) * P], bx[:, :])
            i.then_inc(s("bc_mm"), 1)

            def a_rows(q, pair, free):
                bank = BANK_A if pair % 2 == 0 else BANK_Q
                if pair >= 2:
                    pe.wait_ge(s("a_ucopy"), q * 4 + pair - 1)
                elif free is not None:
                    pe.wait_ge(s(free[0]), free[1])
                for c in (2 * pair, 2 * pair + 1):
                    o = PS[:, bank, (c % 2) * TAB:(c % 2 + 1) * TAB]
                    oh = onehot[:, c:c + 1, bass.ds(q * P, P)]
                    for part in range(3):
                        mm(o, identb[:, :], bcparts[:, part:part + 1, bass.ds(q, 1), :], start=part == 0, stop=False)
                    mm(o, oh, table[:, c, 0:TAB], start=False, stop=False)
                    i = mm(o, oh, table3[:, c, 0:TAB], start=False, stop=True)
                i.then_inc(s("a_mm"), 1)

            def a_transposes(q):
                pe.wait_ge(s("a_lo"), q + 1)
                pe.wait_ge(s("a_hi"), q + 1)
                for c in range(POS):
                    i = nc.tensor.transpose(psT16[:, c * P:(c + 1) * P], xhl[:, c, :], identh[:, :])
                i.then_inc(s("a_T"), 1)

            def c_transposes(q):
                pe.wait_ge(s("c_lo"), q + 1)
                pe.wait_ge(s("c_hi"), q + 1)
                for c in range(POS):
                    i = nc.tensor.transpose(psT16[:, c * P:(c + 1) * P], xhl2[:, c, :], identh[:, :])
                i.then_inc(s("c_T"), 1)

            def c_router(q, pairs_done):
                pe.wait_ge(s("xs2_ready"), q + 1)
                pe.wait_ge(s("a_ucopy"), pairs_done)
                for c in range(POS):
                    x = xs2[:, bass.ds(q * QT + c * P, P)]
                    o = PS[:, BANK_A, c * E:(c + 1) * E]
                    mm(o, x, wa_hi[:, W_R:W_R + E], start=True, stop=False)
                    i = mm(o, x, wa_lo[:, W_R:W_R + E], start=False, stop=True)
                i.then_inc(s("r_mm"), 1)

            def c_mask_transpose(q):
                pe.wait_ge(s("m_ready"), q + 1)
                nc.tensor.transpose(PS[:, BANK_T, 0:P], mtok[:, :], ident).then_inc(s("m_T"), 1)

            def b_queries_keys(q, uses):
                for u in uses:
                    w, g, half = (W_Q, W_K)[u // 4], u // 2 % 2, u % 2
                    if u >= 4:
                        pe.wait_ge(s("qk_split"), q * 8 + u - 3)
                    elif not isinstance(q, int) or q > 0:
                        pe.wait_ge(s("mask_done"), q * 16 - 3 + u)
                    x = xs1[:, half * 512:(half + 1) * 512]
                    mm(PS[:, u % 4, :], wa_hi[:, w + g * P:w + (g + 1) * P], x, start=True, stop=False)
                    mm(PS[:, u % 4, :], wa_lo[:, w + g * P:w + (g + 1) * P], x, start=False, stop=True
                       ).then_inc(s("qk_mm"), 1)

            def b_values(q):
                pe.wait_ge(s("a_ucopy"), q * 4 + 4)
                for n in range(8):
                    o = PS[:, BANK_Q, n * D:(n + 1) * D]
                    x = xs1[:, n * CH:(n + 1) * CH]
                    mm(o, x, wa_hi[:, W_V:W_V + D], start=True, stop=False)
                    i = mm(o, x, wa_lo[:, W_V:W_V + D], start=False, stop=True)
                i.then_inc(s("v_mm"), 1)
                if not isinstance(q, int) or q > 1:
                    pe.wait_ge(s("r_log"), q - 1)
                for b in range(4):
                    o = PS[:, BANK_A, b * D:(b + 1) * D]
                    x = xs1[:, 2 * b * CH:(2 * b + 1) * CH]
                    mm(o, x, wa_hi[:, W_KC:W_KC + D], start=True, stop=False)
                    i = mm(o, x, wa_lo[:, W_KC:W_KC + D], start=False, stop=True)
                i.then_inc(s("ktok_mm"), 1)
                x = xs1[:, :].rearrange("p (b a n) -> p b a n", b=4, a=2)[:, :, 1, :]
                mm(PS[0:D, BANK_T, :], wa_hi[:, W_QC:W_QC + D], x, start=True, stop=False)
                mm(PS[0:D, BANK_T, :], wa_lo[:, W_QC:W_QC + D], x, start=False, stop=True).then_inc(s("qc_mm"), 1)

            def b_state(q):
                pe.wait_ge(s("ktok_ready"), q + 1)
                pe.wait_ge(s("vdec_ready"), q + 1)
                for b in range(4):
                    i = mm(PS[0:D, BANK_A, 256 + b * D:256 + (b + 1) * D], ktok[:, b, :], vdec[:, b, :])
                i.then_inc(s("kv_mm"), 1)

            def b_scores(q, n):
                b = n // 2
                for j in (2 * (n % 2), 2 * (n % 2) + 1):
                    if not isinstance(q, int) or 16 * q + 4 * b + j - 3 > 0:
                        pe.wait_ge(s("mask_done"), q * 16 + 4 * b + j - 3)
                    for a in range(2):
                        chunk = slice((2 * b + a) * CH, (2 * b + a + 1) * CH)
                        for g in range(2):
                            i = mm(PS[:, j, (2 * a + g) * CH:(2 * a + g + 1) * CH],
                                   k32[32 * j:32 * j + 32, g, chunk], q32[32 * j:32 * j + 32, g, chunk])
                    i.then_inc(s("scores"), 1)

            def b_outputs(q, b):
                pe.wait_ge(s("mask_done"), q * 16 + 4 * b + 4)
                if b == 0:
                    pe.wait_ge(s("sbd_ready"), q + 1)
                    pe.wait_ge(s("qdec_ready"), q + 1)
                cols = slice(b * CH, (b + 1) * CH)
                mm(PS[64:128, BANK_O, cols], sbd[:, b, :], qdec[:, b, :], start=True, stop=False)
                for j in range(4):
                    for a in range(2):
                        for g in range(2):
                            n = 2 * b + a
                            r0 = 64 * a + 32 * g
                            i = mm(PS[r0:r0 + 32, BANK_O, cols], vx[:, n, g, 32 * j:32 * j + 32],
                                   probs[:, b % 2, j, (2 * a + g) * CH:(2 * a + g + 1) * CH],
                                   start=(a == 0 and j == 0), stop=j == 3)
                i.then_inc(s("pv_done"), 1)

            def b_project(q):
                pe.wait_ge(s("olo_ready"), q * 2 + 2)
                for c in range(POS):
                    o = PS[:, BANK_O, c * D:(c + 1) * D]
                    x = ostk[:, c:QT:POS]
                    mm(o, x, wa_hi[:, W_P:W_P + D], start=True, stop=False)
                    i = mm(o, x, wa_lo[:, W_P:W_P + D], start=False, stop=True)
                i.then_inc(s("proj_mm"), 1)

            def quad(q, has_a, has_c):
                for n in range(8):
                    if n == 0:
                        pe.wait_ge(s("qk_split"), q * 8 + 8)
                    b_scores(q, n)
                    if n == 0 and has_a:
                        a_rows(q + 1, 0, ("sbd_ready", q + 1))
                    if n == 1 and has_a:
                        a_rows(q + 1, 1, ("vdec_ready", q + 1))
                    if n == 2 and has_a:
                        a_rows(q + 1, 2, None)
                    if n == 3 and has_a:
                        a_rows(q + 1, 3, None)
                    if n == 3 and has_c:
                        if not isinstance(q, int) or q > 1:
                            pe.wait_ge(s("mT_ready"), q - 1)
                        pe.wait_ge(s("qdec_ready"), q + 1)
                        c_transposes(q - 1)
                    if n == 5 and has_c:
                        c_router(q - 1, pairs_done(q, has_a))
                    if n % 2 == 0 and n > 0:
                        b_outputs(q, n // 2 - 1)
                    if n == 7 and has_a:
                        if has_c:
                            pe.wait_ge(s("xs2_ready"), q)
                        a_transposes(q + 1)
                if has_a:
                    pe.wait_ge(s("xs1_ready"), q + 2)
                    b_queries_keys(q + 1, (0, 1, 2, 3))
                b_outputs(q, 3)
                if has_a:
                    b_queries_keys(q + 1, (4, 5, 6, 7))
                    b_values(q + 1)
                b_project(q)
                if has_a:
                    b_state(q + 1)
                    pe.wait_ge(s("qdec_ready"), q + 2)
                if has_c:
                    c_mask_transpose(q - 1)

            def pairs_done(q, has_a):
                return (q + 2) * 4 if has_a else 4 * NQ

            pe.wait_ge(s("identb_ready"), 2)
            pe.wait_ge(s("bc_ready"), 1)
            for pair in range(4):
                a_rows(0, pair, None)
            a_transposes(0)
            pe.wait_ge(s("wa_ready"), 1)
            pe.wait_ge(s("zero_ready"), 4)
            pe.wait_ge(s("xs1_ready"), 1)
            b_queries_keys(0, range(8))
            b_values(0)
            b_state(0)
            quad(0, True, False)
            with pe.Fori(1, NQ - 1) as q:
                quad(q, True, True)
            quad(NQ - 1, False, True)
            pe.wait_ge(s("mT_ready"), NQ - 1)
            c_transposes(NQ - 1)
            c_router(NQ - 1, 4 * NQ)
            c_mask_transpose(NQ - 1)

            def l1(q, t):
                if not isinstance(q, int) or q > 0 or t >= 2:
                    pe.wait_ge(s("gelu_done"), q * NT1 + t - 1)
                for w, first in ((w1_hi, True), (w1_lo, False)):
                    for half in range(2):
                        i = mm(PS[:, 2 * (t % 2) + half, :], w[:, t, :],
                               xs2[:, bass.ds(q * QT + half * 512, 512)], start=first, stop=not first)
                i.then_inc(s("l1_done"), 1)

            def l2(q, u):
                unit = (u + 1) // 2
                first = u == 0 or u % 2 == 1
                last = u % 2 == 0
                banks = 4 + 2 * (unit % 2)
                if first:
                    need = {0: 0, 1: -1, 2: 1, 3: 2, 4: 3}[unit]
                    if not isinstance(q, int) or 5 * q + need > 0:
                        pe.wait_ge(s("y_used"), q * 5 + need)
                    if unit == 2 and (not isinstance(q, int) or q > 0):
                        pe.wait_ge(s("f_used"), q)
                pe.wait_ge(s("gelu_done"), q * NT1 + 2 * u + 2)
                for half in range(2):
                    for k in range(2):
                        i = mm(PS[64 * k:64 * k + 64, banks + half, :], w2_sb[:, 2 * u + k, :],
                               gring[:, (2 * u + k) % GR, half * 512:(half + 1) * 512], start=first, stop=last)
                i.then_inc(s("l2_done"), 1)

            def fold(q):
                pe.wait_ge(s("ylo_ready"), q + 1)
                for c in range(POS):
                    o = PS[:, 4, c * D:(c + 1) * D]
                    mm(o, y_hi[:, c * P:(c + 1) * P], pair_sum[:, :], start=True, stop=False)
                    i = mm(o, y_lo[:, c * P:(c + 1) * P], pair_sum[:, :], start=False, stop=True)
                i.then_inc(s("f_mm"), 1)

            def ffn(q, has_fold):
                l1(q, 0)
                l1(q, 1)
                for u in range(NT1 // 2):
                    if u + 1 < NT1 // 2:
                        l1(q, 2 * u + 2)
                        l1(q, 2 * u + 3)
                    l2(q, u)
                    if u == 2 and has_fold:
                        pe.wait_ge(s("y_used"), q * 5 + 1)
                        fold(q - 1)

            pe.wait_ge(s("w1_ready"), 1)
            pe.wait_ge(s("ld_ffn"), 48)
            pe.wait_ge(s("mT_ready"), NQ)
            ffn(0, False)
            with pe.Fori(1, NQ) as q:
                ffn(q, True)
            pe.wait_ge(s("y_used"), 5 * NQ)
            fold(NQ - 1)

        @block.scalar
        def _(act):
            def a(o, i, f=ACT.Identity, **kw):
                return nc.scalar.activation(o, i, f, **kw)

            act.dma_start(cst[:, :], consts).then_inc(s("ld_cst"), 16)
            act.dma_start(slope_bc[:, :], slopes.partition_broadcast(P)).then_inc(s("ld_slope"), 16)
            act.dma_start(slope_col[:, :], bass.AP(tensor=slopes.tensor, offset=slopes.offset,
                                                   ap=[[1, H], [0, DH], [1, 1]])).then_inc(s("ld_slope"), 16)
            act.dma_start(wa[:, :], attnw).then_inc(s("ld_attn"), 16)
            act.dma_start(w1_raw, w1).then_inc(s("ld_w1"), 16)
            act.wait_ge(s("slope_ready"), 2)
            for j in range(4):
                for g in range(2):
                    a(decay[:, j, g, :], cst[:, C_DIFF:C_DIFF + P], ACT.Exp,
                      scale=neg_slope[:, 4 * g + j:4 * g + j + 1]).then_inc(s("decay_raw"), 1)
            a(kdec[:, :], slope_row[:, :, :], ACT.Exp, scale=cst[:, C_COL + 4:C_COL + 5]).then_inc(s("kdec_ready"), 1)
            a(dec[:, :], cst[0:D, C_NEGC:C_NEGC + CH], ACT.Exp, scale=slope_col[:, :]).then_inc(s("dec_raw"), 1)
            act.wait_ge(s("ld_tow"), 32)
            act.wait_ge(s("xtT"), 1)
            a(lnT[:, :], PS[:, 0, :], bias=tb[:, B_LB:B_LB + 1], scale=tb[:, B_LG:B_LG + 1]).then_inc(s("lnT_ready"), 1)
            for f in range(2):
                act.wait_ge(s("mlp1"), f + 1)
                a(g1[:, f, :], PS[:, 1 + f, :], ACT.Gelu, bias=tb[:, B_L1 + f:B_L1 + f + 1]).then_inc(s("g1_ready"), 1)
            act.wait_ge(s("mlp2"), 1)
            a(locd[:, :, :, :], PS[:, 3, :].rearrange("p (c o v) -> p c o v", o=1, v=VOCAB)
              .broadcast_to([P, POS, 2, VOCAB]), bias=tb[:, B_L2:B_L2 + 1]).then_inc(s("loc_ready"), 1)
            act.wait_ge(s("ghc"), 1)
            a(rt[:, DT:TAB], PS[:, 4, 0:D]).then_inc(s("rt_ready"), 1)
            act.wait_ge(s("hb_mm"), 1)
            a(hb[:, :], PS[:, 4, 64:64 + D]).then_inc(s("hb_ready"), 1)
            act.wait_ge(s("bx_mm"), 1)
            a(bx[:, DT:TAB], PS[:, 4, 128:128 + D]).then_inc(s("bx_ready"), 1)
            for c in range(POS):
                act.wait_ge(s("tab_mm"), c + 1)
                if c >= 2:
                    act.wait_ge(s("tab_ready"), c - 1)
                a(tab_top[:, c % 2, :], PS[:, 5 + c % 2, 0:TABP], ACT.Copy).then_inc(s("tab_hi"), 1)
            for f in range(2):
                act.wait_ge(s("summ"), f + 1)
                a(hT[:, f, :], PS[:, 4 * f, :], bias=tb[:, B_PB:B_PB + 1], scale=1.0 / POS).then_inc(s("h_ready"), 1)
            for r in range(ROUNDS):
                for f in range(2):
                    act.wait_ge(s("t_ab"), 2 * r + f + 1)
                    a(a_sb[:, f, :], PS[:, 4 * f, :], bias=tb[:, B_M1:B_M1 + 1]).then_inc(s("t_a"), 1)
                for f in range(2):
                    for d in range(WIN + 1):
                        act.wait_ge(s("t_pre"), 5 * (2 * r + f) + d + 1)
                        v = pre[:, f, d, :].rearrange("p (b n) -> p b n", b=HB)[:, :, d:CPB]
                        a(v, v, ACT.Gelu).then_inc(s("t_g"), 1)
                for f in range(2):
                    act.wait_ge(s("t_agg"), 2 * r + f + 1)
                    a(agg_sb[:, f, :], PS[:, 4 * f + 2, :], bias=tb[:, B_M2:B_M2 + 1]).then_inc(s("t_aggs"), 1)
                for f in range(2):
                    act.wait_ge(s("t_u"), 2 * r + f + 1)
                    a(gu_sb[:, f, :], PS[:, 4 * f + 3, :], ACT.Gelu, bias=tb[:, B_U1:B_U1 + 1]).then_inc(s("t_gu"), 1)
                for f in range(2):
                    act.wait_ge(s("t_T"), 2 * r + f + 1)
                    a(hT[:, f, :], PS[:, 4 * f + 1, :], bias=tb[:, B_MB:B_MB + 1], scale=tb[:, B_MG:B_MG + 1]
                      ).then_inc(s("h_ready"), 1)
            act.wait_ge(s("bc_mm"), 1)
            a(bcparts[:, 0, :, :].rearrange("p (k a) n -> p k (a n)", k=4), PS[:, 0:4, 0:2 * TAB], ACT.Copy
              ).then_inc(s("bc_hi"), 1)

            def a_copies(q, pairs):
                for c2 in pairs:
                    act.wait_ge(s("a_stat"), q * 4 + c2 + 1)
                    if c2 == 0 and (not isinstance(q, int) or q > 0):
                        act.wait_ge(s("a_u_used"), q)
                    src = PS[:, BANK_A if c2 % 2 == 0 else BANK_Q, 0:2 * TAB].rearrange("p (c n) -> p c n", c=2)[:, :, DT:TAB]
                    a(u_sb[:, 2 * c2:2 * c2 + 2, :], src, ACT.Copy).then_inc(s("a_ucopy"), 1)

            def a_high(q):
                act.wait_ge(s("a_xn"), q + 1)
                if not isinstance(q, int) or q > 0:
                    act.wait_ge(s("a_T"), q)
                a(xhl[:, :, 0:D], xn[:, :, :], ACT.Copy).then_inc(s("a_hi"), 1)

            def a_evacuate(q):
                act.wait_ge(s("a_T"), q + 1)
                if not isinstance(q, int) or q > 0:
                    act.wait_ge(s("qc_mm"), q)
                    act.wait_ge(s("ktok_mm"), q)
                a(xs1[:, :].rearrange("p (n c) -> p c n", c=POS), psT16.rearrange("p (c n) -> p c n", c=POS),
                  ACT.Copy).then_inc(s("xs1_ready"), 1)

            def c_high(q):
                act.wait_ge(s("c_xn"), q + 1)
                if not isinstance(q, int) or q > 0:
                    act.wait_ge(s("c_T"), q)
                a(xhl2[:, :, 0:D], xn2[:, :, :], ACT.Copy).then_inc(s("c_hi"), 1)

            def c_evacuate(q):
                act.wait_ge(s("c_T"), q + 1)
                a(xs2[:, bass.ds(q * QT, QT)], psT16, ACT.Copy).then_inc(s("xs2_ready"), 1)

            def c_exp(q):
                act.wait_ge(s("r_log"), q + 1)
                a(rexp[:, :, :], rlog[:, :, :], ACT.Exp, scale=1.0 / SW).then_inc(s("r_exp"), 1)

            def c_mask_copy(q):
                act.wait_ge(s("m_T"), q + 1)
                if not isinstance(q, int) or q > 0:
                    act.wait_ge(s("m_stored"), q * 16)
                a(mT[:, :], PS[0:D, BANK_T, 0:P], ACT.Copy).then_inc(s("mT_ready"), 1)

            def b_high(q, uses):
                for u in uses:
                    act.wait_ge(s("qk_mm"), q * 8 + u + 1)
                    if not isinstance(q, int) or q > 0 or u >= 4:
                        act.wait_ge(s("qk_split"), q * 8 + u - 3)
                    a(qk_hi[:, u % 4, :], PS[:, u % 4, :], ACT.Copy).then_inc(s("qk_hi_ready"), 1)

            def b_value_copies(q):
                act.wait_ge(s("v_mm"), q + 1)
                if not isinstance(q, int) or q > 0:
                    act.wait_ge(s("pv_done"), q * 4)
                pv = PS[:, BANK_Q, :].rearrange("p (n g j d) -> p n g j d", n=8, g=2, j=4)
                for g in range(2):
                    a(vx[:, :, g, :].rearrange("p n (j w) -> p n j w", w=40)[:, :, :, 0:DH], pv[:, :, g, :, :],
                      ACT.Copy).then_inc(s("vx_ready"), 1)
                act.wait_ge(s("ktok_mm"), q + 1)
                a(ktok[:, :, :], PS[:, BANK_A, 0:4 * D].rearrange("p (b n) -> p b n", b=4), ACT.Copy
                  ).then_inc(s("ktok_ready"), 1)

            def b_output_high(q):
                act.wait_ge(s("pv_done"), q * 4 + 4)
                if not isinstance(q, int) or q > 0:
                    act.wait_ge(s("proj_mm"), q)
                for k in range(2):
                    a(ostk[0:D, :].rearrange("p (b a n) -> p b a n", b=4, a=2)[:, :, k, :],
                      PS[64 * k:64 * k + 64, BANK_O, :].rearrange("p (b n) -> p b n", b=4), ACT.Copy
                      ).then_inc(s("ohi_ready"), 1)

            def quad(q, has_a, has_c):
                for n in range(8):
                    if 1 <= n <= 4 and has_a:
                        a_copies(q + 1, (n - 1,))
                    if n == 2 and has_c:
                        c_high(q - 1)
                    if n == 4 and has_c:
                        c_evacuate(q - 1)
                    if n == 6 and has_a:
                        a_high(q + 1)
                    if n == 6 and has_c:
                        c_exp(q - 1)
                    if n == 7 and has_a:
                        a_evacuate(q + 1)
                if has_a:
                    b_high(q + 1, (0, 1, 2, 3))
                b_output_high(q)
                if has_a:
                    b_high(q + 1, (4, 5, 6, 7))
                    b_value_copies(q + 1)
                if has_c:
                    c_mask_copy(q - 1)

            a_copies(0, (0, 1, 2, 3))
            a_high(0)
            a_evacuate(0)
            b_high(0, range(8))
            b_value_copies(0)
            quad(0, True, False)
            with act.Fori(1, NQ - 1) as q:
                quad(q, True, True)
            quad(NQ - 1, False, True)
            c_high(NQ - 1)
            c_evacuate(NQ - 1)
            c_exp(NQ - 1)
            c_mask_copy(NQ - 1)

            def y_high(q):
                act.wait_ge(s("y_acc"), q + 1)
                if not isinstance(q, int) or q > 0:
                    act.wait_ge(s("f_mm"), q)
                a(y_hi[:, :], yacc[:, :], ACT.Copy).then_inc(s("yhi_ready"), 1)

            def store(q):
                act.wait_ge(s("f_used"), q + 1)
                act.dma_start(out_v[bass.ds(q * P, P), :], obuf[:, :]).then_inc(s("out_done"), 16)

            def ffn(q, has_fold):
                for t in range(NT1):
                    act.wait_ge(s("l1_done"), q * NT1 + t + 1)
                    u = t // 2
                    if not isinstance(q, int) or 9 * q + u - 2 > 0:
                        act.wait_ge(s("l2_done"), q * 9 + u - 2)
                    a(gring[:, t % GR, :], PS[:, 2 * (t % 2):2 * (t % 2) + 2, :], ACT.Gelu,
                      bias=b1_sb[:, t:t + 1], scale=1.0 / SW).then_inc(s("gelu_done"), 1)
                    if t == 4 and has_fold:
                        y_high(q - 1)
                    if t == 9 and has_fold:
                        store(q - 1)

            act.wait_ge(s("ld_ffn"), 48)
            ffn(0, False)
            with act.Fori(1, NQ) as q:
                ffn(q, True)
            y_high(NQ - 1)
            store(NQ - 1)

        @block.vector
        def _(dve):
            v = nc.vector
            ch = Steps(dve, s("dve_step"))
            tt = v.tensor_tensor

            def stats_tail(n, key, width):
                e, x = st[key], stx[key]
                ch.step(tt(x[:, 0, 0:n], e[:, 0:n, 1], e[:, 0:n, 4], ALU.subtract))
                ch.step(tt(x[:, 1, 0:n], e[:, 0:n, 2], e[:, 0:n, 5], ALU.add))
                ch.step(tt(x[:, 2, 0:n], e[:, 0:n, 1], e[:, 0:n, 4], ALU.add))
                ch.settle()
                ch.step(tt(x[:, 3, 0:n], x[:, 0, 0:n], x[:, 0, 0:n], ALU.mult))
                ch.step(v.tensor_scalar(x[:, 5, 0:n], x[:, 2, 0:n], 0.5, None, ALU.mult))
                ch.settle()
                ch.step(v.scalar_tensor_tensor(x[:, 0, 0:n], x[:, 3, 0:n], width / 4.0, x[:, 1, 0:n],
                                               ALU.mult, ALU.add))
                ch.settle()
                v.tensor_scalar(x[:, 4, 0:n], x[:, 0, 0:n], 1.0 / width, EPS, ALU.mult, ALU.add
                                ).then_inc(s("stats_" + key), 1)

            dve.wait_ge(s("ld_cst"), 16)
            v.tensor_copy(identb[:, :], ident).then_inc(s("identb_ready"), 1)
            v.tensor_copy(identh[:, :], ident).then_inc(s("identb_ready"), 1)
            dve.wait_ge(s("ld_slope"), 32)
            v.tensor_copy(slope_row[:, :, :], slope_bc[:, :].rearrange("p (h o) -> p h o", o=1)
                          .broadcast_to([P, H, DH])).then_inc(s("slope_ready"), 1)
            v.tensor_scalar(neg_slope[:, :], slope_bc[:, :], -1.0, None, ALU.mult).then_inc(s("slope_ready"), 1)
            v.tensor_copy(rt[:, 0:DT], ident).then_inc(s("rt_id"), 1)
            v.tensor_copy(pair_sum[:, :], cst[:, C_II:C_II + D]).then_inc(s("zero_ready"), 1)
            v.memset(vx[:, :, :, :], 0.0).then_inc(s("zero_ready"), 1)
            v.memset(mtok[:, :], 0.0).then_inc(s("zero_ready"), 1)
            v.memset(sbd[:, :, :], 0.0).then_inc(s("zero_ready"), 1)
            ch.step(v.memset(qdec[64:128, :, :], 0.0))
            ch.step(v.memset(table3[:, :, :], 0.0))
            dve.wait_ge(s("ld_emb"), 160)
            for k in range(4):
                tt(htab[:, k, :], embt[:, :], postab[:, k, :], ALU.add).then_inc(s("htab_ready"), 1)
            dve.wait_ge(s("htab_ready"), 4)
            for k in range(4):
                ch.step(v.bn_stats(st["t"][:, k, :], htab[:, k, :]))
            ch.settle()
            stats_tail(4, "t", DT)
            dve.wait_ge(s("rstd_t"), 1)
            for k in range(4):
                v.tensor_scalar(xt[:, k, :], htab[:, k, :], stx["t"][:, 5, k:k + 1], rstd["t"][:, k:k + 1],
                                ALU.subtract, ALU.mult).then_inc(s("xt_ready"), 1)
            dve.wait_ge(s("ld_tow"), 32)
            ch.step(v.tensor_copy(fb_bc[:, :], tb[:, B_FB:B_FB + 1].broadcast_to([P, P])))
            ch.step(v.tensor_copy(bx[:, 0:DT], tw[:, T_BC:T_BC + DT]))
            ch.settle()
            v.tensor_scalar(gh[:, :], tw[:, T_HW:T_HW + D], tb[:, B_FG:B_FG + 1], None, ALU.mult
                            ).then_inc(s("gh_ready"), 1)
            for k in range(4):
                dve.wait_ge(s(f"ld_ids{k}"), 16)
                v.tensor_scalar(onehot[:, 2 * k:2 * k + 2, :], ids_stage[:, k % 2, :],
                                cst[:, C_COL:C_COL + 1], None, ALU.is_equal).then_inc(s("onehot_ready"), 1)
            dve.wait_ge(s("loc_ready"), 1)
            v.tensor_scalar(locdb[:, :, :, :], locd[:, :, :, :], tb[:, B_BC:B_BC + 1], None, ALU.add
                            ).then_inc(s("locb_ready"), 1)
            for c in range(POS):
                dve.wait_ge(s("tab_hi"), c + 1)
                top, acc = tab_top[:, c % 2, :], PS[:, 5 + c % 2, 0:TABP]
                ch.step(v.scalar_tensor_tensor(table[:, c, :], top, cst[:, C_COL + 3:C_COL + 4], acc,
                                               ALU.mult, ALU.add))
                ch.step(tt(tab_rest[:, :], acc, top, ALU.subtract))
                ch.settle()
                v.scalar_tensor_tensor(table3[64:128, c, :], table[64:128, c, :], -1.0, tab_rest[64:128, :],
                                       ALU.mult, ALU.add).then_inc(s("tab_ready"), 1)
                dve.wait_ge(s("tab_ready"), c + 1)
            dve.wait_ge(s("decay_raw"), 8)
            tt(decay[:, :, :, :].rearrange("p j g c -> p (j g) c"), decay[:, :, :, :].rearrange("p j g c -> p (j g) c"),
               cst[:, C_CAUS:C_CAUS + CH].rearrange("p (o c) -> p o c", o=1).broadcast_to([P, H, CH]), ALU.mult
               ).then_inc(s("decay_ready"), 1)
            dve.wait_ge(s("dec_raw"), 1)
            v.tensor_scalar(dec[:, :], dec[:, :], DH ** -0.5 / SW ** 2, None, ALU.mult).then_inc(s("decay_ready"), 1)
            inv = cst[:, C_INV:C_INV + CPB].rearrange("p (o n) -> p o n", o=1).broadcast_to([P, HB, CPB])
            dve.wait_ge(s("ld_rows"), 32)

            def seqs(x):
                return x.rearrange("p (b n) -> p b n", b=HB)

            for f in range(2):
                for d in range(1, WIN + 1):
                    ch.step(v.memset(seqs(pre[:, f, d, :])[:, :, 0:d], 0.0))
            for r in range(ROUNDS):
                for f in range(2):
                    dve.wait_ge(s("t_a"), 2 * r + f + 1)
                    for d in range(WIN + 1):
                        tt(seqs(pre[:, f, d, :])[:, :, d:CPB], seqs(PS[:, 4 * f + 1, :])[:, :, 0:CPB - d],
                           seqs(a_sb[:, f, :])[:, :, d:CPB], ALU.add).then_inc(s("t_pre"), 1)
                for f in range(2):
                    base = 5 * (2 * r + f)
                    dve.wait_ge(s("t_g"), base + 2)
                    ch.step(tt(msum[:, f, :], pre[:, f, 0, :], pre[:, f, 1, :], ALU.add))
                    for d in range(2, WIN + 1):
                        dve.wait_ge(s("t_g"), base + d + 1)
                        ch.settle()
                        ch.step(tt(msum[:, f, :], msum[:, f, :], pre[:, f, d, :], ALU.add))
                    ch.settle()
                    tt(seqs(msum[:, f, :]), seqs(msum[:, f, :]), inv, ALU.mult).then_inc(s("t_sum"), 1)
                for f in range(2):
                    dve.wait_ge(s("t_r"), 2 * r + f + 1)
                    x = rtok[f]
                    ch.step(tt(x, PS[:, 4 * f, :].rearrange("p (t n) -> p t n", t=4),
                               updb2_bc[:, :].rearrange("p (o n) -> p o n", o=1).broadcast_to([P, 4, DT]), ALU.add))
                    ch.settle()
                    for t in range(4):
                        ch.step(v.bn_stats(st["t"][:, 4 * f + t, :], x[:, t, :]))
                ch.settle()
                stats_tail(8, "t", DT)
                dve.wait_ge(s("rstd_t"), r + 2)
                for f in range(2):
                    for t in range(4):
                        k = 4 * f + t
                        v.tensor_scalar(rtok[f][:, t, :], rtok[f][:, t, :], stx["t"][:, 5, k:k + 1],
                                        rstd["t"][:, k:k + 1], ALU.subtract, ALU.mult).then_inc(s("t_xc"), 1)
            dve.wait_ge(s("bc_hi"), 1)
            acc = PS[:, 0:4, 0:2 * TAB]

            def parts(k):
                return bcparts[:, k, :, :].rearrange("p (k a) n -> p k (a n)", k=4)

            rest = bc_rest.rearrange("p (k n) -> p k n", k=4)
            ch.step(tt(rest, acc, parts(0), ALU.subtract))
            ch.settle()
            ch.step(v.tensor_copy(parts(1), rest))
            ch.settle()
            tt(parts(2), rest, parts(1), ALU.subtract).then_inc(s("bc_ready"), 1)
            dve.wait_ge(s("hb_ready"), 1)
            dve.wait_ge(s("kdec_ready"), 1)

            def bc_d(x, width):
                return x.rearrange("p (c o) -> p c o", o=1).broadcast_to([P, POS, width])

            def bc_row(x):
                return x.rearrange("p (o n) -> p o n", o=1).broadcast_to([P, POS, D])

            def a_stats(q, pairs):
                for c2 in pairs:
                    dve.wait_ge(s("a_mm"), q * 4 + c2 + 1)
                    for c in (2 * c2, 2 * c2 + 1):
                        bank = BANK_A if c2 % 2 == 0 else BANK_Q
                        i = v.bn_stats(st["f"][:, c, :], PS[:, bank, (c % 2) * TAB:(c % 2) * TAB + DT])
                        if c % 2 == 0:
                            ch.step(i)
                    i.then_inc(s("a_stat"), 1)
                if pairs[-1] == 3:
                    dve.wait_ge(s("a_stat"), q * 4 + 4)
                    stats_tail(8, "f", DT)

            def a_hidden(q):
                hq = h_res[:, bass.ds(q * POS * D, POS * D)].rearrange("p (c n) -> p c n", c=POS)
                dve.wait_ge(s("rstd_f"), q + 1)
                dve.wait_ge(s("a_ucopy"), q * 4 + 4)
                tt(xn[:, :, :], u_sb[:, :, :], bc_d(rstd["f"][:, :], D), ALU.mult).then_inc(s("a_u_used"), 1)
                dve.wait_ge(s("a_u_used"), q + 1)
                ch.step(tt(hq, xn[:, :, :], bc_row(hb[:, :]), ALU.add))
                ch.settle()
                for c in (1, 2, 3, 4, 5, 6, 7, 0):
                    ch.step(v.bn_stats(st["a"][:, c, :], h_res[:, bass.ds(q * POS * D + c * D, D)]))
                ch.settle()
                stats_tail(8, "a", D)

            def normalize(q, key, x, x_hl, hi_ready):
                hq = h_res[:, bass.ds(q * POS * D, POS * D)].rearrange("p (c n) -> p c n", c=POS)
                dve.wait_ge(s("rstd_" + key), q + 1)
                ch.step(tt(x[:, :, :], hq, bc_d(stx[key][:, 5, :], D), ALU.subtract))
                ch.settle()
                if not isinstance(q, int) or q > 0:
                    dve.wait_ge(s(key + "_hi"), q)
                tt(x[:, :, :], x[:, :, :], bc_d(rstd[key][:, :], D), ALU.mult).then_inc(s(key + "_xn"), 1)
                dve.wait_ge(s(key + "_hi"), q + 1)
                tt(x_hl[:, :, D:2 * D], x[:, :, :], x_hl[:, :, 0:D], ALU.subtract).then_inc(s(key + "_lo"), 1)

            def c_stats(q):
                if not isinstance(q, int) or q >= 0:
                    dve.wait_ge(s("h2_done"), q + 1)
                for c in (1, 2, 3, 4, 5, 6, 7, 0):
                    ch.step(v.bn_stats(st["c"][:, c, :], h_res[:, bass.ds(q * POS * D + c * D, D)]))
                ch.settle()
                stats_tail(8, "c", D)

            def c_logits(q):
                dve.wait_ge(s("r_mm"), q + 1)
                ps = PS[:, BANK_A, 0:POS * E].rearrange("p (c e) -> p c e", c=POS)
                ch.step(v.tensor_reduce(rmax[:, 0, :], ps, op=ALU.max, axis=AX_X))
                ch.settle()
                tt(rlog[:, :, :], ps, bc_d(rmax[:, 0, :], E), ALU.subtract).then_inc(s("r_log"), 1)

            def c_top2(q):
                dve.wait_ge(s("r_exp"), q + 1)
                ch.step(v.tensor_reduce(rmax[:, 1, :], rexp[:, :, :], op=ALU.add, axis=AX_X))
                ch.settle()
                ch.step(v.reciprocal(rmax[:, 2, :], rmax[:, 1, :]))
                ch.settle()
                ch.step(tt(rw[:, :, :], rexp[:, :, :], bc_d(rmax[:, 2, :], E), ALU.mult))
                ch.settle()
                wj = rw[:, :, :].rearrange("p c (o j) -> p c o j", o=1).broadcast_to([P, POS, E, E])
                we = rw[:, :, :].rearrange("p c (e o) -> p c e o", o=1).broadcast_to([P, POS, E, E])
                low = cst[:, C_LOW:C_LOW + E * E].rearrange("p (o n) -> p o n", o=1).broadcast_to([P, POS, E * E])
                ch.step(tt(rge[:, :, :, :], wj, we, ALU.is_ge))
                ch.settle()
                flat = rge[:, :, :, :].rearrange("p c e j -> p c (e j)")
                ch.step(tt(flat, flat, low, ALU.mult))
                ch.settle()
                ch.step(tt(rdf[:, :, :, :], rge[:, :, :, :], rge[:, :, :, :].rearrange("p c e j -> p c j e"),
                           ALU.subtract))
                ch.settle()
                ch.step(v.tensor_reduce(rank[:, :, :], rdf[:, :, :, :], op=ALU.add, axis=AX_X))
                ch.settle()
                thr = cst[:, C_THR:C_THR + E].rearrange("p (o n) -> p o n", o=1).broadcast_to([P, POS, E])
                ch.step(tt(rank[:, :, :], rank[:, :, :], thr, ALU.is_lt))
                ch.settle()
                ch.step(tt(rw[:, :, :], rw[:, :, :], rank[:, :, :], ALU.mult))
                ch.settle()
                ch.step(v.tensor_reduce(rmax[:, 1, :], rw[:, :, :], op=ALU.add, axis=AX_X))
                ch.settle()
                ch.step(v.reciprocal(rmax[:, 3, :], rmax[:, 1, :]))
                ch.settle()
                if not isinstance(q, int) or q > 0:
                    dve.wait_ge(s("m_T"), q)
                tt(mtok[:, 0:POS * E].rearrange("p (e c) -> p c e", e=E), rw[:, :, :], bc_d(rmax[:, 3, :], E),
                   ALU.mult).then_inc(s("m_ready"), 1)

            def b_split(q, uses):
                for u in uses:
                    dst, g, half = (q32, k32)[u // 4], u // 2 % 2, u % 2
                    dve.wait_ge(s("qk_hi_ready"), q * 8 + u + 1)
                    if u == 0 and (not isinstance(q, int) or q > 0):
                        dve.wait_ge(s("scores"), q * 16)
                    v.scalar_tensor_tensor(
                        dst[:, g, half * 512:(half + 1) * 512], qk_hi[:, u % 4, :],
                        cst[:, C_COL + 1 + u // 4:C_COL + 2 + u // 4], PS[:, u % 4, :], ALU.mult, ALU.add
                    ).then_inc(s("qk_split"), 1)

            def b_decayed_values(q):
                dve.wait_ge(s("vx_ready"), q * 2 + 2)
                if not isinstance(q, int) or q > 0:
                    dve.wait_ge(s("kv_mm"), q)
                pv = PS[:, BANK_Q, :].rearrange("p (b a n) -> p b a n", b=4, a=2)[:, :, 0, :]
                tt(vdec[:, :, :], pv, kdec[:, :].rearrange("p (o n) -> p o n", o=1).broadcast_to([P, 4, D]),
                   ALU.mult).then_inc(s("vdec_ready"), 1)

            def b_decayed_queries(q):
                dve.wait_ge(s("qc_mm"), q + 1)
                if not isinstance(q, int) or q > 0:
                    dve.wait_ge(s("pv_done"), q * 4)
                tt(qdec[0:D, :, :], PS[0:D, BANK_T, :].rearrange("p (b n) -> p b n", b=4),
                   dec[:, :].rearrange("p (o n) -> p o n", o=1).broadcast_to([D, 4, CH]), ALU.mult
                   ).then_inc(s("qdec_ready"), 1)

            def b_masked_state(q):
                dve.wait_ge(s("kv_mm"), q + 1)
                tt(sbd[0:D, :, :], PS[0:D, BANK_A, 256:512].rearrange("p (b n) -> p b n", b=4),
                   cst[0:D, C_BLK:C_BLK + D].rearrange("p (o n) -> p o n", o=1).broadcast_to([D, 4, D]), ALU.mult
                   ).then_inc(s("sbd_ready"), 1)

            def b_mask(q, n):
                b = n // 2
                for j in (2 * (n % 2), 2 * (n % 2) + 1):
                    dve.wait_ge(s("scores"), q * 16 + 4 * b + j + 1)
                    if j == 0 and (not isinstance(q, int) or 4 * q + b - 1 > 0):
                        dve.wait_ge(s("pv_done"), q * 4 + b - 1)
                    tt(probs[:, b % 2, j, :].rearrange("p (a n) -> p a n", a=2),
                       PS[:, j, :].rearrange("p (a n) -> p a n", a=2),
                       decay[:, j, :, :].rearrange("p (o g) c -> p o (g c)", o=1).broadcast_to([P, 2, 2 * CH]),
                       ALU.mult).then_inc(s("mask_done"), 1)

            def b_output_low(q):
                for k in range(2):
                    dve.wait_ge(s("ohi_ready"), q * 2 + k + 1)
                    hi = ostk[0:D, :].rearrange("p (b a n) -> p b a n", b=4, a=2)[:, :, k, :]
                    lo = ostk[D:P, :].rearrange("p (b a n) -> p b a n", b=4, a=2)[:, :, k, :]
                    tt(lo, PS[64 * k:64 * k + 64, BANK_O, :].rearrange("p (b n) -> p b n", b=4), hi, ALU.subtract
                       ).then_inc(s("olo_ready"), 1)

            def b_residual(q):
                hq = h_res[:, bass.ds(q * POS * D, POS * D)]
                dve.wait_ge(s("proj_mm"), q + 1)
                ch.step(v.scalar_tensor_tensor(hq, PS[:, BANK_O, :], SW ** -2, hq, ALU.mult, ALU.add))
                ch.settle()
                hq3 = hq.rearrange("p (c n) -> p c n", c=POS)
                tt(hq3, hq3, bc_row(bproj_bc[:, :]), ALU.add).then_inc(s("h2_done"), 1)

            def quad(q, has_a, has_c):
                for n in range(8):
                    b_mask(q, n)
                    if n == 0 and has_c:
                        c_stats(q - 1)
                    if 1 <= n <= 4 and has_a:
                        a_stats(q + 1, (n - 1,))
                    if n == 2 and has_c:
                        normalize(q - 1, "c", xn2, xhl2, "c_hi")
                    if n == 5 and has_a:
                        a_hidden(q + 1)
                    if n == 6 and has_a:
                        normalize(q + 1, "a", xn, xhl, "a_hi")
                    if n == 6 and has_c:
                        c_logits(q - 1)
                    if n == 7 and has_c:
                        c_top2(q - 1)
                if has_a:
                    b_split(q + 1, (0, 1, 2, 3))
                b_output_low(q)
                if has_a:
                    b_split(q + 1, (4, 5, 6, 7))
                    b_decayed_values(q + 1)
                b_residual(q)
                if has_a:
                    b_decayed_queries(q + 1)
                    b_masked_state(q + 1)

            a_stats(0, (0, 1, 2, 3))
            a_hidden(0)
            normalize(0, "a", xn, xhl, "a_hi")
            dve.wait_ge(s("decay_ready"), 2)
            b_split(0, range(8))
            b_decayed_values(0)
            b_decayed_queries(0)
            b_masked_state(0)
            quad(0, True, False)
            with dve.Fori(1, NQ - 1) as q:
                ch.enter(q, 1, PER_QUAD)
                quad(q, True, True)
            ch.leave(NQ - 2)
            quad(NQ - 1, False, True)
            c_stats(NQ - 1)
            normalize(NQ - 1, "c", xn2, xhl2, "c_hi")
            c_logits(NQ - 1)
            c_top2(NQ - 1)

            def use_unit(q, unit):
                acc = PS[:, 4 + 2 * (unit % 2):6 + 2 * (unit % 2), :]
                dve.wait_ge(s("l2_done"), q * 9 + 2 * unit + 1)
                y2 = yacc[:, :].rearrange("p (k n) -> p k n", k=2)
                if unit == 0:
                    if not isinstance(q, int) or q > 0:
                        dve.wait_ge(s("ylo_ready"), q)
                    v.tensor_scalar(y2, acc, b2_sb[:, 0:1], None, ALU.add).then_inc(s("y_used"), 1)
                    return
                pr = unit - 1
                dve.wait_ge(s(f"m_loaded{pr}"), q * 32 + 32)
                v.scalar_tensor_tensor(ytmp[:, :].rearrange("p (k n) -> p k n", k=2), acc, b2_sb[:, unit:unit + 1],
                                       mb[:, pr, :].rearrange("p (k n) -> p k n", k=2), ALU.add, ALU.mult
                                       ).then_inc(s("y_used"), 1)
                dve.wait_ge(s("y_used"), q * 5 + unit + 1)
                tt(yacc[:, :], yacc[:, :], ytmp[:, :], ALU.add).then_inc(s("m_used"), 1)
                dve.wait_ge(s("m_used"), q * 4 + unit)

            def y_low(q):
                dve.wait_ge(s("yhi_ready"), q + 1)
                if not isinstance(q, int) or q > 0:
                    dve.wait_ge(s("f_mm"), q)
                tt(y_lo[:, :], yacc[:, :], y_hi[:, :], ALU.subtract).then_inc(s("ylo_ready"), 1)

            def finish(q):
                dve.wait_ge(s("f_mm"), q + 1)
                if not isinstance(q, int) or q > 0:
                    dve.wait_ge(s("out_done"), q * 16)
                tt(obuf[:, :], PS[:, 4, :], h_res[:, bass.ds(q * POS * D, POS * D)], ALU.add).then_inc(s("f_used"), 1)

            def ffn(q, has_fold):
                if has_fold:
                    y_low(q - 1)
                use_unit(q, 0)
                use_unit(q, 1)
                if has_fold:
                    finish(q - 1)
                for unit in range(2, 5):
                    use_unit(q, unit)
                v.tensor_copy(rmax[:, 0, :], rmax[:, 0, :]).then_inc(s("y_acc"), 1)

            dve.wait_ge(s("ld_ffn"), 48)
            ffn(0, False)
            with dve.Fori(1, NQ) as q:
                ffn(q, True)
            y_low(NQ - 1)
            finish(NQ - 1)

        @block.gpsimd
        def _(pool):
            g = nc.gpsimd
            chp = Steps(pool, s("pool_step"))
            g.memset(minus_half[:, :], -0.5).then_inc(s("half_ready"), 1)
            pool.wait_ge(s("half_ready"), 1)

            def power(key, count, n=POS):
                pool.wait_ge(s("stats_" + key), count)
                g.tensor_tensor(rstd[key][:, 0:n], stx[key][:, 4, 0:n], minus_half[:, 0:n], ALU.pow
                                ).then_inc(s("rstd_" + key), 1)

            power("t", 1, 4)

            def split(raw, hi, lo, ready):
                chp.step(g.tensor_scalar(raw, raw, SW, 0.0, ALU.mult, ALU.add))
                chp.settle()
                chp.step(g.tensor_copy(hi, raw))
                chp.settle()
                g.tensor_tensor(lo, raw, hi, ALU.subtract).then_inc(s(ready), 1)

            pool.wait_ge(s("ld_attn"), 16)
            split(wa[:, :], wa_hi[:, :], wa_lo[:, :], "wa_ready")
            pool.wait_ge(s("ld_w1"), 16)
            split(w1_raw.rearrange("p (t n) -> p t n", t=NT1), w1_hi[:, :, :], w1_lo[:, :, :], "w1_ready")
            for r in range(ROUNDS):
                power("t", r + 2)
            power("f", 1)
            power("a", 1)

            def quad(q, has_a, has_c):
                if has_c:
                    power("c", q)
                if has_a:
                    power("f", q + 2)
                    power("a", q + 2)

            quad(0, True, False)
            with pool.Fori(1, NQ - 1) as q:
                quad(q, True, True)
            quad(NQ - 1, False, True)
            power("c", NQ)


_INS = ["ids", "emb", "pos", "consts", "towerw", "towerb", "updb2", "attnw", "bproj", "slopes", "w1", "b1", "w2", "b2"]


def shape_constants():
    import numpy as np
    c = np.zeros((P, C_END), np.float32)
    c[:, C_ID:C_ID + P] = np.eye(P)
    c[:, C_CEN:C_CEN + P] = np.eye(P) - 1.0 / DT
    e, t = np.arange(CH)[:, None], np.arange(CH)[None, :]
    c[:, C_DIFF:C_DIFF + CH] = np.maximum(t - e, 0)
    c[:, C_CAUS:C_CAUS + CH] = (t >= e) * (DH ** -0.5 / SW ** 2)
    c[:, C_II:C_II + D] = np.vstack([np.eye(D), np.eye(D)])
    hd = np.arange(D) // DH
    c[0:D, C_BLK:C_BLK + D] = hd[:, None] == hd[None, :]
    j = np.arange(E)
    c[:, C_THR:C_THR + E] = 2.0 - (E - 1 - j)
    c[:, C_LOW:C_LOW + E * E] = (j[None, :] < j[:, None]).reshape(-1)
    p = np.arange(P)
    c[:, C_COL] = p % VOCAB
    c[:, C_COL + 1] = -1.0 * (p // 16 % 2)
    c[:, C_COL + 2] = -1.0 * (p // 8 % 2)
    c[:, C_COL + 3] = -1.0 * (p // 64)
    c[:, C_COL + 4] = -1.0 * (CH - p)
    c[:, C_INV:C_INV + CPB] = 1.0 / np.minimum(np.arange(CPB) + 1, WIN + 1)
    c[:, C_NEGC:C_NEGC + CH] = -np.arange(CH)
    return c


def laid_out(inputs):
    import numpy as np

    a = {k: np.asarray(v) for k, v in inputs.items()}
    t = {k[7:]: v for k, v in a.items() if k.startswith("L0_tok_")}
    w = {k[8:]: v for k, v in a.items() if k.startswith("L0_attn_")}
    m = {k[7:]: v for k, v in a.items() if k.startswith("L0_ffn_")}

    def tiles(x, n):
        return np.concatenate([x[P * i:P * (i + 1)] for i in range(n)], axis=1)

    def col(x):
        return x.reshape(-1, P).T

    def slots(x):
        return np.repeat(x.reshape(D, H, 1, DH), 4, axis=2).reshape(D, H * 4 * DH)

    wq, wk, wv = (w["w_qkv"][:, k * D:(k + 1) * D] for k in range(3))
    attnw = np.concatenate([slots(wq), slots(wk), wv, wk, wq, w["w_proj"], m["Wr"]], axis=1)
    w1t = [m["W1s"][:, :P], m["W1s"][:, P:]]
    b1t = [m["b1s"][:P], m["b1s"][P:]]
    w2t = [m["W2s"][:P], m["W2s"][P:]]
    for pr in range(E // 2):
        for f in range(2):
            for e in (2 * pr, 2 * pr + 1):
                w1t.append(m["W1p"][e][:, f * P:(f + 1) * P])
                b1t.append(m["b1p"][e][f * P:(f + 1) * P])
                w2t.append(m["W2p"][e][f * P:(f + 1) * P])
    w1 = np.concatenate(w1t, axis=1)
    zero = np.zeros_like(m["b2s"])
    arrays = {
        "ids": a["x"].reshape(NCHUNK, POS).T.reshape(-1),
        "emb": t["emb"], "pos": t["pos"], "consts": shape_constants(),
        "towerw": np.concatenate([t["lw1"], tiles(t["lw2"], 2), tiles(t["msg_w1"], 2), t["msg_w2"],
                                  tiles(t["upd_w1"], 2), t["upd_w2"], t["pool_w"], t["bc_w"], t["bc_w"].T,
                                  t["head_w"]], axis=1),
        "towerb": np.concatenate([col(t[k]) for k in (
            "lb1", "lb2", "lln_g", "lln_b", "pool_b", "msg_b1", "msg_b2", "upd_b1", "mln_g", "mln_b", "bc_b",
            "fln_g", "fln_b")], axis=1),
        "updb2": t["upd_b2"], "attnw": np.concatenate([attnw, attnw], axis=0), "bproj": w["b_proj"],
        "slopes": w["slopes"], "w1": np.concatenate([w1, w1], axis=0), "b1": np.stack(b1t, axis=1),
        "w2": np.concatenate(w2t, axis=1),
        "b2": np.stack([np.concatenate([m["b2s"], zero])] +
                       [m["b2p"][2 * pr:2 * pr + 2].reshape(-1) for pr in range(E // 2)], axis=1),
    }
    return {name: np.ascontiguousarray(arrays[name]) for name in _INS}


def kernel(**inputs):
    import concourse.bacc as bacc
    from concourse.bass_utils import run_bass_kernel_spmd

    arrays = laid_out(inputs)
    nc = bacc.Bacc("TRN2", target_bir_lowering=False, num_devices=1)
    args = {}
    for name in _INS:
        args[name] = nc.dram_tensor(f"in_{name}", arrays[name].shape, mybir.dt.from_np(arrays[name].dtype),
                                    kind="ExternalInput").ap()
    args["out"] = nc.dram_tensor("out_0", (NB, SEQ, D), F32, kind="ExternalOutput").ap()
    build(nc, **args)
    r = run_bass_kernel_spmd(nc, [{f"in_{k}": v for k, v in arrays.items()}], core_ids=[0])
    return r.results[0]["out_0"]
```

```python
from contextlib import ExitStack

import concourse.bass as bass
from concourse import mybir
from concourse.alu_op_type import AluOpType as ALU

ACT = mybir.ActivationFunctionType
F32 = mybir.dt.float32
F16 = mybir.dt.float16
BF16 = mybir.dt.bfloat16
I32 = mybir.dt.int32
AX_X = mybir.AxisListType.X

P = 128
VOCAB, POS, DT, ROUNDS, WIN = 64, 8, 128, 3, 4
NB, SEQ = 32, 256
CPB = SEQ // POS
NCHUNK = NB * CPB
HALF = NCHUNK // 2
HB = HALF // CPB
D, H, DH = 64, 8, 8
CH = 128
F, E = 256, 8
NT1 = 2 * (E + 1)
EPS = 1e-5
PER_QUAD = 47
POOL_PER_QUAD = 3
SW = 64.0
NQ = NCHUNK // P
QT = P * POS
TAB = DT + D
TABP = TAB + DT

C_ID, C_CEN, C_DIFF, C_CAUS, C_II, C_BLK = 0, 128, 256, 384, 512, 576
C_THR, C_LOW, C_COL, C_INV, C_NEGC, C_END = 640, 648, 712, 720, 752, 880
W_Q, W_K, W_V, W_KC, W_QC, W_P, W_R, W_END = 0, 256, 512, 576, 640, 704, 768, 776
T_L1, T_L2, T_MA, T_MB, T_M2, T_UA, T_UB, T_U2 = 0, 256, 512, 640, 768, 896, 1024, 1152
T_PW, T_BC, T_BCT, T_HW, T_END = 1280, 1408, 1536, 1664, 1728
(B_L1, B_L2, B_LG, B_LB, B_PB, B_M1, B_M2, B_U1, B_MG, B_MB, B_BC, B_FG, B_FB, B_END) = (
    0, 2, 3, 4, 5, 6, 7, 8, 9, 10, 11, 12, 13, 14)


class Steps:

    def __init__(self, eng, sem):
        self.eng, self.sem, self.origin, self.k = eng, sem, 0, 0

    def step(self, ins):
        ins.then_inc(self.sem, 1)
        self.k += 1

    def settle(self):
        self.eng.wait_ge(self.sem, self.origin + self.k)

    def enter(self, i, first, per):
        self.start = self.origin + self.k
        self.per = per
        self.origin, self.k = self.start + (i - first) * per, 0

    def leave(self, times):
        assert self.k == self.per, ("steps in the loop's body", self.k)
        self.origin, self.k = self.start + times * self.per, 0


def build(nc, ids, emb, pos, consts, towerw, towerb, updb2, attnw, bproj, slopes, w1, b1, w2, b2, out):
    mask_rows = nc.dram_tensor("mask_rows", [NQ, E * POS, P], F32).ap()
    out_v = out.rearrange("b (j c) d -> (b j) (c d)", c=POS)

    with ExitStack() as ctx:
        def sb(name, shape, dt=F32):
            return ctx.enter_context(nc.sbuf_tensor(name, shape, dt))

        PS = ctx.enter_context(nc.psum_tensor("PS", [P, 8, 512], F32))
        BANK_A, BANK_T, BANK_Q, BANK_O = 4, 5, 6, 7

        cst = sb("cst", [P, C_END])
        ident = cst[:, C_ID:C_ID + P]
        identb = sb("identb", [P, P], BF16)
        identh = sb("identh", [P, P], F16)
        pair_sum = sb("pair_sum", [P, D], F16)
        tw = sb("tw", [P, T_END])
        tb = sb("tb", [P, B_END])
        updb2_bc = sb("updb2_bc", [P, DT])
        bproj_bc = sb("bproj_bc", [P, D])
        slope_bc = sb("slope_bc", [P, H])
        slope_row = sb("slope_row", [P, H, DH])
        neg_slope = sb("neg_slope", [P, H])
        slope_col = sb("slope_col", [D, 1])
        wa = sb("wa", [P, W_END])
        wa_hi = sb("wa_hi", [P, W_END], F16)
        wa_lo = sb("wa_lo", [P, W_END], F16)
        w1_hi = sb("w1_hi", [P, NT1, P], F16)
        w1_lo = sb("w1_lo", [P, NT1, P], F16)
        w2_sb = sb("w2_sb", [P, NT1, D])
        b1_sb = sb("b1_sb", [P, NT1])
        b2_sb = sb("b2_sb", [P, 1 + E // 2])
        minus_half = sb("minus_half", [P, POS])

        slab2 = sb("slab2", [P, POS * NCHUNK // 2])
        onehot = slab2[:, :].bitcast(BF16).rearrange("p (c n) -> p c n", c=POS)
        embt = sb("embt", [P, DT])
        postab = sb("postab", [P, 4, DT])
        htab = sb("htab", [P, 4, DT])
        table = sb("table", [P, POS, TABP], BF16)
        table3 = sb("table3", [P, POS, TABP], BF16)
        bcparts = sb("bcparts", [P, 3, NQ, TAB], BF16)
        rt = sb("rt", [P, TAB])
        bx = sb("bx", [P, TAB])
        gh = sb("gh", [P, D])
        fb_bc = sb("fb_bc", [P, P])
        hb = sb("hb", [P, D])
        hT = sb("hT", [P, 2, HALF])
        slab = sb("slab", [P, 10240])
        w1_raw = slab[:, 10240 - NT1 * P:10240]
        pre = slab[:, 0:2 * (WIN + 1) * HALF].rearrange("p (f d n) -> p f d n", f=2, d=WIN + 1)
        slab3 = sb("slab3", [P, 12 * HALF])

        def part3(k, n, dt=F32):
            x = slab3[:, k * HALF:(k + n) * HALF]
            return x if dt is F32 else x.bitcast(dt)

        lnT, g1 = part3(0, 1), part3(1, 2).rearrange("p (f n) -> p f n", f=2)
        xt = part3(3, 1).rearrange("p (t n) -> p t n", t=4)
        locd = part3(4, 2).rearrange("p (c k v) -> p c k v", c=POS, k=2)
        locdb = part3(6, 2).rearrange("p (c k v) -> p c k v", c=POS, k=2)
        tab_top = sb("tab_top", [P, 2, TABP], BF16)
        tab_rest = sb("tab_rest", [P, TABP])
        a_sb = part3(8, 2).rearrange("p (f n) -> p f n", f=2)
        msum = part3(10, 2).rearrange("p (f n) -> p f n", f=2)
        agg_sb = a_sb
        gu_sb = msum
        rtok = lnT.rearrange("p (t n) -> p t n", t=4), g1[:, 0, :].rearrange("p (t n) -> p t n", t=4)
        bc_rest = slab[:, 0:NQ * TAB]
        ids_stage = slab[:, 0:4 * NCHUNK].bitcast(I32).rearrange("p (k n) -> p k n", k=2)
        psT16 = PS[:, BANK_T, :].bitcast(F16)
        GR = 6
        gring = slab[:, 0:GR * QT].rearrange("p (s n) -> p s n", s=GR)
        mb = slab[:, GR * QT:GR * QT + 4 * QT].rearrange("p (s n) -> p s n", s=4)

        h_res = sb("h_res", [P, NQ * POS * D])
        xs1 = sb("xs1", [P, QT], F16)
        xs2 = sb("xs2", [P, NQ * QT], F16)
        u_sb = part3(3, 1).rearrange("p (c n) -> p c n", c=POS)
        xn = part3(1, 1).rearrange("p (c n) -> p c n", c=POS)
        xhl = part3(4, 1, F16).rearrange("p (c n) -> p c n", c=POS)
        xn2 = part3(2, 1).rearrange("p (c n) -> p c n", c=POS)
        xhl2 = part3(5, 1, F16).rearrange("p (c n) -> p c n", c=POS)
        q32 = slab[:, 4 * QT:5 * QT].bitcast(F16).rearrange("p (g n) -> p g n", g=2)
        k32 = slab[:, 5 * QT:6 * QT].bitcast(F16).rearrange("p (g n) -> p g n", g=2)
        qk_hi = sb("qk_hi", [P, 4, 512], F16)
        vx = sb("vx", [P, POS, 2, 160])
        vdec = sb("vdec", [P, 4, D])
        ktok = sb("ktok", [P, 4, D])
        sbd = sb("sbd", [P, 4, D])
        qdec = sb("qdec", [P, 4, CH])
        probs = slab[:, 0:4 * QT].rearrange("p (s j n) -> p s j n", s=2, j=4)
        decay = sb("decay", [P, 4, 2, CH])
        kdec = sb("kdec", [P, D])
        dec = sb("dec", [D, CH])
        ostk = part3(8, 1, F16)
        st = {n: sb(f"st_{n}", [P, POS, 6]) for n in ("t", "f", "a", "c")}
        stx = {n: sb(f"stx_{n}", [P, 6, POS]) for n in ("t", "f", "a", "c")}
        rstd = {n: sb(f"rstd_{n}", [P, POS]) for n in ("t", "f", "a", "c")}
        rmax = sb("rmax", [P, 4, POS])
        rlog = sb("rlog", [P, POS, E])
        rexp = sb("rexp", [P, POS, E])
        rw = sb("rw", [P, POS, E])
        rge = part3(6, 1).rearrange("p (c e j) -> p c e j", c=POS, e=E)
        rdf = part3(7, 1).rearrange("p (c e j) -> p c e j", c=POS, e=E)
        rank = sb("rank", [P, POS, E])
        mtok = sb("mtok", [P, P])
        mT = sb("mT", [D, P])
        yacc = slab2[:, 0:QT]
        ytmp = slab2[:, QT:2 * QT]
        y_hi = slab2[:, 2 * QT:5 * QT // 2].bitcast(F16)
        y_lo = slab2[:, 5 * QT // 2:3 * QT].bitcast(F16)
        obuf = sb("obuf", [P, POS * D])

        SEMS = {}

        def s(name):
            if name not in SEMS:
                SEMS[name] = ctx.enter_context(nc.semaphore(name))
            return SEMS[name]

        block = ctx.enter_context(nc.Block())

        @block.sync
        def _(sp):
            for k in range(2):
                sp.dma_start(embt[64 * k:64 * k + 64, :], emb).then_inc(s("ld_emb"), 16)
            for c in range(POS):
                sp.dma_start(postab[64 * (c % 2):64 * (c % 2) + 64, c // 2, :],
                             pos[c, :].partition_broadcast(64)).then_inc(s("ld_emb"), 16)
            sp.dma_start(tb[:, :], towerb).then_inc(s("ld_tow"), 16)
            sp.dma_start(tw[:, :], towerw).then_inc(s("ld_tow"), 16)
            for k in range(4):
                if k >= 2:
                    sp.wait_ge(s("onehot_ready"), k - 1)
                sp.dma_start(ids_stage[:, k % 2, :],
                             ids[2 * k * NCHUNK:2 * (k + 1) * NCHUNK].partition_broadcast(P)
                             ).then_inc(s(f"ld_ids{k}"), 16)
            sp.dma_start(updb2_bc[:, :], updb2.partition_broadcast(P)).then_inc(s("ld_rows"), 16)
            sp.dma_start(bproj_bc[:, :], bproj.partition_broadcast(P)).then_inc(s("ld_rows"), 16)
            sp.dma_start(w2_sb[:, :, :], w2.rearrange("p (t n) -> p t n", t=NT1)).then_inc(s("ld_ffn"), 16)
            sp.dma_start(b1_sb[:, :], b1).then_inc(s("ld_ffn"), 16)
            sp.dma_start(b2_sb[:, :], b2).then_inc(s("ld_ffn"), 16)
            with sp.Fori(0, NQ) as q:
                sp.wait_ge(s("mT_ready"), q + 1)
                sp.dma_start(mask_rows[bass.ds(q, 1)].rearrange("q r p -> (q r) p"), mT[:, :]
                             ).then_inc(s("m_stored"), 16)

            def load_masks(q, free):
                sp.wait_ge(s("m_stored"), q * 16 + 16)
                for pr in range(E // 2):
                    if free is not None:
                        sp.wait_ge(s("m_used"), free + pr)
                    for k in range(2):
                        e = 2 * pr + k
                        sp.dma_start(
                            mb[64 * k:64 * k + 64, pr:pr + 1, :],
                            mask_rows[bass.ds(q, 1), e * POS:(e + 1) * POS, :].rearrange("q r p -> q (r p)")
                            .partition_broadcast(64)).then_inc(s(f"m_loaded{pr}"), 16)

            sp.wait_ge(s("w1_ready"), 1)
            load_masks(0, None)
            with sp.Fori(1, NQ) as q:
                load_masks(q, q * 4 - 3)
            sp.wait_ge(s("out_done"), 16 * NQ)

        @block.tensor
        def _(pe):
            def mm(o, lhsT, rhs, start=True, stop=True):
                return nc.tensor.matmul(o, lhsT, rhs, start=start, stop=stop, skip_group_check=True)

            pe.wait_ge(s("xt_ready"), 4)
            for k in range(4):
                i = nc.tensor.transpose(PS[:, 0, k * P:(k + 1) * P], xt[:, k, :], ident)
            i.then_inc(s("xtT"), 1)
            pe.wait_ge(s("ld_tow"), 32)
            pe.wait_ge(s("lnT_ready"), 1)
            for f in range(2):
                mm(PS[:, 1 + f, :], tw[:, T_L1 + f * P:T_L1 + (f + 1) * P], lnT[:, :]).then_inc(s("mlp1"), 1)
            for f in range(2):
                pe.wait_ge(s("g1_ready"), f + 1)
                mm(PS[:, 3, :], tw[:, T_L2 + f * P:T_L2 + (f + 1) * P], g1[:, f, :], start=f == 0, stop=False)
            for k in range(4):
                i = mm(PS[:, 3, k * P:(k + 1) * P], htab[:, k, :], ident, start=False, stop=True)
            i.then_inc(s("mlp2"), 1)
            pe.wait_ge(s("gh_ready"), 1)
            mm(PS[:, 4, 0:D], cst[:, C_CEN:C_CEN + P], gh[:, :]).then_inc(s("ghc"), 1)
            pe.wait_ge(s("rt_ready"), 1)
            mm(PS[:, 4, 64:64 + D], fb_bc[:, :], tw[:, T_HW:T_HW + D]).then_inc(s("hb_mm"), 1)
            pe.wait_ge(s("hb_ready"), 1)
            mm(PS[:, 4, 128:128 + D], tw[:, T_BCT:T_BCT + P], rt[:, DT:TAB]).then_inc(s("bx_mm"), 1)
            pe.wait_ge(s("locb_ready"), 1)
            for c in range(POS):
                if c >= 2:
                    pe.wait_ge(s("tab_ready"), c - 1)
                mm(PS[:, 5 + c % 2, 0:TAB], locdb[:, c, :, :], rt[:, :])
                mm(PS[:, 5 + c % 2, TAB:TABP], locd[:, c, :, :], tw[:, T_PW:T_PW + P]).then_inc(s("tab_mm"), 1)
            pe.wait_ge(s("tab_ready"), POS)
            pe.wait_ge(s("onehot_ready"), 4)
            for f in range(2):
                for c in range(POS):
                    oh = onehot[:, c, f * HALF:(f + 1) * HALF]
                    mm(PS[:, 4 * f, :], table[:, c, TAB:TABP], oh, start=c == 0, stop=False)
                    i = mm(PS[:, 4 * f, :], table3[:, c, TAB:TABP], oh, start=False, stop=c == POS - 1)
                i.then_inc(s("summ"), 1)
            for r in range(ROUNDS):
                for f in range(2):
                    k = 2 * r + f + 1
                    pe.wait_ge(s("h_ready"), k)
                    mm(PS[:, 4 * f, :], tw[:, T_MA:T_MA + P], hT[:, f, :])
                    mm(PS[:, 4 * f + 1, :], tw[:, T_MB:T_MB + P], hT[:, f, :]).then_inc(s("t_ab"), 1)
                for f in range(2):
                    k = 2 * r + f + 1
                    pe.wait_ge(s("t_sum"), k)
                    mm(PS[:, 4 * f + 2, :], tw[:, T_M2:T_M2 + P], msum[:, f, :]).then_inc(s("t_agg"), 1)
                    mm(PS[:, 4 * f + 3, :], tw[:, T_UA:T_UA + P], hT[:, f, :], start=True, stop=False)
                for f in range(2):
                    pe.wait_ge(s("t_aggs"), 2 * r + f + 1)
                    mm(PS[:, 4 * f + 3, :], tw[:, T_UB:T_UB + P], agg_sb[:, f, :], start=False, stop=True
                       ).then_inc(s("t_u"), 1)
                for f in range(2):
                    pe.wait_ge(s("t_gu"), 2 * r + f + 1)
                    for t in range(4):
                        o = PS[:, 4 * f, t * P:(t + 1) * P]
                        mm(o, gu_sb[:, f, t * P:(t + 1) * P], tw[:, T_U2:T_U2 + P], start=True, stop=False)
                        i = mm(o, hT[:, f, t * P:(t + 1) * P], ident, start=False, stop=True)
                    i.then_inc(s("t_r"), 1)
                for f in range(2):
                    pe.wait_ge(s("t_xc"), 4 * (2 * r + f + 1))
                    for t in range(4):
                        i = nc.tensor.transpose(PS[:, 4 * f + 1, t * P:(t + 1) * P], rtok[f][:, t, :], ident)
                    i.then_inc(s("t_T"), 1)
            pe.wait_ge(s("h_ready"), 2 * ROUNDS + 2)
            pe.wait_ge(s("bx_ready"), 1)
            for q in range(NQ):
                o = PS[:, q // 2, (q % 2) * TAB:(q % 2 + 1) * TAB]
                i = mm(o, hT[:, q // 4, (q % 4) * P:(q % 4 + 1) * P], bx[:, :])
            i.then_inc(s("bc_mm"), 1)

            def a_rows(q, pair, free):
                bank = BANK_A if pair % 2 == 0 else BANK_Q
                if pair >= 2:
                    pe.wait_ge(s("a_ucopy"), q * 4 + pair - 1)
                elif free is not None:
                    pe.wait_ge(s(free[0]), free[1])
                for c in (2 * pair, 2 * pair + 1):
                    o = PS[:, bank, (c % 2) * TAB:(c % 2 + 1) * TAB]
                    oh = onehot[:, c:c + 1, bass.ds(q * P, P)]
                    for part in range(3):
                        mm(o, identb[:, :], bcparts[:, part:part + 1, bass.ds(q, 1), :], start=part == 0, stop=False)
                    mm(o, oh, table[:, c, 0:TAB], start=False, stop=False)
                    i = mm(o, oh, table3[:, c, 0:TAB], start=False, stop=True)
                i.then_inc(s("a_mm"), 1)

            def a_transposes(q):
                pe.wait_ge(s("a_lo"), q + 1)
                pe.wait_ge(s("a_hi"), q + 1)
                for c in range(POS):
                    i = nc.tensor.transpose(psT16[:, c * P:(c + 1) * P], xhl[:, c, :], identh[:, :])
                i.then_inc(s("a_T"), 1)

            def c_transposes(q):
                pe.wait_ge(s("c_lo"), q + 1)
                pe.wait_ge(s("c_hi"), q + 1)
                for c in range(POS):
                    i = nc.tensor.transpose(psT16[:, c * P:(c + 1) * P], xhl2[:, c, :], identh[:, :])
                i.then_inc(s("c_T"), 1)

            def c_router(q):
                pe.wait_ge(s("xs2_ready"), q + 1)
                for c in range(POS):
                    x = xs2[:, bass.ds(q * QT + c * P, P)]
                    o = PS[:, BANK_T, c * E:(c + 1) * E]
                    mm(o, x, wa_hi[:, W_R:W_R + E], start=True, stop=False)
                    i = mm(o, x, wa_lo[:, W_R:W_R + E], start=False, stop=True)
                i.then_inc(s("r_mm"), 1)

            def c_mask_transpose(q):
                pe.wait_ge(s("m_ready"), q + 1)
                nc.tensor.transpose(PS[:, BANK_T, 0:P], mtok[:, :], ident).then_inc(s("m_T"), 1)

            def b_queries_keys(q, uses):
                for u in uses:
                    w, g, half = (W_Q, W_K)[u // 4], u // 2 % 2, u % 2
                    if u >= 4:
                        pe.wait_ge(s("qk_split"), q * 8 + u - 3)
                    elif not isinstance(q, int) or q > 0:
                        pe.wait_ge(s("mask_done"), q * 16 - 3 + u)
                    x = xs1[:, half * 512:(half + 1) * 512]
                    mm(PS[:, u % 4, :], wa_hi[:, w + g * P:w + (g + 1) * P], x, start=True, stop=False)
                    mm(PS[:, u % 4, :], wa_lo[:, w + g * P:w + (g + 1) * P], x, start=False, stop=True
                       ).then_inc(s("qk_mm"), 1)

            def b_values(q):
                pe.wait_ge(s("a_ucopy"), q * 4 + 8 if not isinstance(q, int) else min(q * 4 + 8, 4 * NQ))
                for n in range(8):
                    o = PS[:, BANK_Q, n * D:(n + 1) * D]
                    x = xs1[:, n * CH:(n + 1) * CH]
                    mm(o, x, wa_hi[:, W_V:W_V + D], start=True, stop=False)
                    i = mm(o, x, wa_lo[:, W_V:W_V + D], start=False, stop=True)
                i.then_inc(s("v_mm"), 1)
                for b in range(4):
                    o = PS[:, BANK_A, b * D:(b + 1) * D]
                    x = xs1[:, 2 * b * CH:(2 * b + 1) * CH]
                    mm(o, x, wa_hi[:, W_KC:W_KC + D], start=True, stop=False)
                    i = mm(o, x, wa_lo[:, W_KC:W_KC + D], start=False, stop=True)
                i.then_inc(s("ktok_mm"), 1)

            def b_chunk_queries(q):
                x = xs1[:, :].rearrange("p (b a n) -> p b a n", b=4, a=2)[:, :, 1, :]
                mm(PS[0:D, BANK_T, :], wa_hi[:, W_QC:W_QC + D], x, start=True, stop=False)
                mm(PS[0:D, BANK_T, :], wa_lo[:, W_QC:W_QC + D], x, start=False, stop=True).then_inc(s("qc_mm"), 1)

            def b_state(q):
                pe.wait_ge(s("ktok_ready"), q + 1)
                pe.wait_ge(s("vdec_ready"), q + 1)
                for b in range(4):
                    i = mm(PS[0:D, BANK_A, 256 + b * D:256 + (b + 1) * D], ktok[:, b, :], vdec[:, b, :])
                i.then_inc(s("kv_mm"), 1)

            def b_scores(q, n):
                b = n // 2
                for j in (2 * (n % 2), 2 * (n % 2) + 1):
                    if not isinstance(q, int) or 16 * q + 4 * b + j - 3 > 0:
                        pe.wait_ge(s("mask_done"), q * 16 + 4 * b + j - 3)
                    for a in range(2):
                        chunk = slice((2 * b + a) * CH, (2 * b + a + 1) * CH)
                        for g in range(2):
                            i = mm(PS[:, j, (2 * a + g) * CH:(2 * a + g + 1) * CH],
                                   k32[32 * j:32 * j + 32, g, chunk], q32[32 * j:32 * j + 32, g, chunk])
                    i.then_inc(s("scores"), 1)

            def b_outputs(q, b):
                pe.wait_ge(s("mask_done"), q * 16 + 4 * b + 4)
                if b == 0:
                    pe.wait_ge(s("sbd_ready"), q + 1)
                    pe.wait_ge(s("qdec_ready"), q + 1)
                cols = slice(b * CH, (b + 1) * CH)
                mm(PS[64:128, BANK_O, cols], sbd[:, b, :], qdec[:, b, :], start=True, stop=False)
                for j in range(4):
                    for a in range(2):
                        for g in range(2):
                            n = 2 * b + a
                            r0 = 64 * a + 32 * g
                            i = mm(PS[r0:r0 + 32, BANK_O, cols], vx[:, n, g, 32 * j:32 * j + 32],
                                   probs[:, b % 2, j, (2 * a + g) * CH:(2 * a + g + 1) * CH],
                                   start=(a == 0 and j == 0), stop=j == 3)
                i.then_inc(s("pv_done"), 1)

            def b_project(q):
                pe.wait_ge(s("olo_ready"), q * 2 + 2)
                for c in range(POS):
                    o = PS[:, BANK_O, c * D:(c + 1) * D]
                    x = ostk[:, c:QT:POS]
                    mm(o, x, wa_hi[:, W_P:W_P + D], start=True, stop=False)
                    i = mm(o, x, wa_lo[:, W_P:W_P + D], start=False, stop=True)
                i.then_inc(s("proj_mm"), 1)

            def quad(q, has_n, has_a, has_c):
                pe.wait_ge(s("qk_split"), q * 8 + 8)
                for n in range(8):
                    if n == 0:
                        b_scores(q, 0)
                    if n < 7:
                        b_scores(q, n + 1)
                    if n == 0:
                        b_state(q)
                    if n in (2, 4, 6):
                        b_outputs(q, n // 2 - 1)
                    if n == 1 and has_a:
                        a_rows(q + 2, 0, ("sbd_ready", q + 1))
                        a_rows(q + 2, 1, ("vdec_ready", q + 1))
                    if n == 1:
                        pe.wait_ge(s("qdec_ready"), q + 1)
                        if has_n:
                            a_transposes(q + 1)
                    if n == 3 and has_c:
                        if has_n:
                            pe.wait_ge(s("xs1_ready"), q + 2)
                        c_transposes(q - 1)
                    if n in (3, 4) and has_a:
                        a_rows(q + 2, n - 1, None)
                    if n == 4 and has_c:
                        c_router(q - 1)
                if has_n:
                    pe.wait_ge(s("xs1_ready"), q + 2)
                    b_queries_keys(q + 1, (0, 1, 2, 3))
                b_outputs(q, 3)
                if has_n:
                    b_queries_keys(q + 1, (4, 5, 6, 7))
                    b_values(q + 1)
                if has_c:
                    pe.wait_ge(s("r_log"), q)
                    c_mask_transpose(q - 1)
                b_project(q)
                if has_n:
                    if has_c:
                        pe.wait_ge(s("mT_ready"), q)
                    b_chunk_queries(q + 1)

            pe.wait_ge(s("identb_ready"), 2)
            pe.wait_ge(s("bc_ready"), 1)
            for pair in range(4):
                a_rows(0, pair, None)
            for pair in range(4):
                a_rows(1, pair, ("a_ucopy", 3 + pair))
            a_transposes(0)
            pe.wait_ge(s("wa_ready"), 1)
            pe.wait_ge(s("zero_ready"), 4)
            pe.wait_ge(s("xs1_ready"), 1)
            b_queries_keys(0, range(8))
            b_values(0)
            b_chunk_queries(0)
            quad(0, True, True, False)
            with pe.Fori(1, NQ - 2) as q:
                quad(q, True, True, True)
            quad(NQ - 2, True, False, True)
            quad(NQ - 1, False, False, True)
            pe.wait_ge(s("mT_ready"), NQ - 1)

            def l1(q, t):
                if not isinstance(q, int) or q > 0 or t >= 2:
                    pe.wait_ge(s("gelu_done"), q * NT1 + t - 1)
                for w, first in ((w1_hi, True), (w1_lo, False)):
                    for half in range(2):
                        i = mm(PS[:, 2 * (t % 2) + half, :], w[:, t, :],
                               xs2[:, bass.ds(q * QT + half * 512, 512)], start=first, stop=not first)
                i.then_inc(s("l1_done"), 1)

            def l2(q, u):
                unit = (u + 1) // 2
                first = u == 0 or u % 2 == 1
                last = u % 2 == 0
                banks = BANK_Q - 2 * (unit % 2)
                if first:
                    need = {0: 0, 1: -1, 2: 1, 3: 2, 4: 3}[unit]
                    if not isinstance(q, int) or 5 * q + need > 0:
                        pe.wait_ge(s("y_used"), q * 5 + need)
                    if unit == 2 and (not isinstance(q, int) or q > 0):
                        pe.wait_ge(s("f_used"), q)
                pe.wait_ge(s("gelu_done"), q * NT1 + 2 * u + 2)
                for half in range(2):
                    for k in range(2):
                        i = mm(PS[64 * k:64 * k + 64, banks + half, :], w2_sb[:, 2 * u + k, :],
                               gring[:, (2 * u + k) % GR, half * 512:(half + 1) * 512], start=first, stop=last)
                i.then_inc(s("l2_done"), 1)

            def fold(q):
                pe.wait_ge(s("ylo_ready"), q + 1)
                for c in range(POS):
                    o = PS[:, BANK_Q, c * D:(c + 1) * D]
                    mm(o, y_hi[:, c * P:(c + 1) * P], pair_sum[:, :], start=True, stop=False)
                    i = mm(o, y_lo[:, c * P:(c + 1) * P], pair_sum[:, :], start=False, stop=True)
                i.then_inc(s("f_mm"), 1)

            def ffn(q, has_fold, has_next):
                for u in range(NT1 // 2):
                    if u + 1 < NT1 // 2:
                        l1(q, 2 * u + 2)
                        l1(q, 2 * u + 3)
                    elif has_next:
                        l1(q + 1, 0)
                        l1(q + 1, 1)
                    l2(q, u)
                    if u == 1 and has_fold:
                        pe.wait_ge(s("y_used"), q * 5 + 1)
                        fold(q - 1)

            pe.wait_ge(s("w1_ready"), 1)
            pe.wait_ge(s("mask_done"), 16 * NQ)
            l1(0, 0)
            l1(0, 1)
            c_transposes(NQ - 1)
            l1(0, 2)
            c_router(NQ - 1)
            l1(0, 3)
            pe.wait_ge(s("ld_ffn"), 48)
            pe.wait_ge(s("h2_done"), NQ)
            l2(0, 0)
            for t in range(4, 8):
                l1(0, t)
            pe.wait_ge(s("r_log"), NQ)
            c_mask_transpose(NQ - 1)
            pe.wait_ge(s("mT_ready"), NQ)
            l2(0, 1)
            l2(0, 2)
            for u in range(3, NT1 // 2):
                if u + 1 < NT1 // 2:
                    l1(0, 2 * u + 2)
                    l1(0, 2 * u + 3)
                else:
                    l1(1, 0)
                    l1(1, 1)
                l2(0, u)
            with pe.Fori(1, NQ - 1) as q:
                ffn(q, True, True)
            ffn(NQ - 1, True, False)
            pe.wait_ge(s("y_used"), 5 * NQ)
            fold(NQ - 1)

        @block.scalar
        def _(act):
            def a(o, i, f=ACT.Identity, **kw):
                return nc.scalar.activation(o, i, f, **kw)

            act.dma_start(cst[:, :], consts).then_inc(s("ld_cst"), 16)
            act.dma_start(slope_bc[:, :], slopes.partition_broadcast(P)).then_inc(s("ld_slope"), 16)
            act.dma_start(slope_col[:, :], bass.AP(tensor=slopes.tensor, offset=slopes.offset,
                                                   ap=[[1, H], [0, DH], [1, 1]])).then_inc(s("ld_slope"), 16)
            act.dma_start(wa[:, :], attnw).then_inc(s("ld_attn"), 16)
            act.dma_start(w1_raw, w1).then_inc(s("ld_w1"), 16)
            act.wait_ge(s("slope_ready"), 2)
            for j in range(4):
                for g in range(2):
                    a(decay[:, j, g, :], cst[:, C_DIFF:C_DIFF + P], ACT.Exp,
                      scale=neg_slope[:, 4 * g + j:4 * g + j + 1]).then_inc(s("decay_raw"), 1)
            a(kdec[:, :], slope_row[:, :, :], ACT.Exp, scale=cst[:, C_COL + 4:C_COL + 5]).then_inc(s("kdec_ready"), 1)
            a(dec[:, :], cst[0:D, C_NEGC:C_NEGC + CH], ACT.Exp, scale=slope_col[:, :]).then_inc(s("dec_raw"), 1)
            act.wait_ge(s("ld_tow"), 32)
            act.wait_ge(s("xtT"), 1)
            a(lnT[:, :], PS[:, 0, :], bias=tb[:, B_LB:B_LB + 1], scale=tb[:, B_LG:B_LG + 1]).then_inc(s("lnT_ready"), 1)
            for f in range(2):
                act.wait_ge(s("mlp1"), f + 1)
                a(g1[:, f, :], PS[:, 1 + f, :], ACT.Gelu, bias=tb[:, B_L1 + f:B_L1 + f + 1]).then_inc(s("g1_ready"), 1)
            act.wait_ge(s("mlp2"), 1)
            a(locd[:, :, :, :], PS[:, 3, :].rearrange("p (c o v) -> p c o v", o=1, v=VOCAB)
              .broadcast_to([P, POS, 2, VOCAB]), bias=tb[:, B_L2:B_L2 + 1]).then_inc(s("loc_ready"), 1)
            act.wait_ge(s("ghc"), 1)
            a(rt[:, DT:TAB], PS[:, 4, 0:D]).then_inc(s("rt_ready"), 1)
            act.wait_ge(s("hb_mm"), 1)
            a(hb[:, :], PS[:, 4, 64:64 + D]).then_inc(s("hb_ready"), 1)
            act.wait_ge(s("bx_mm"), 1)
            a(bx[:, DT:TAB], PS[:, 4, 128:128 + D]).then_inc(s("bx_ready"), 1)
            for c in range(POS):
                act.wait_ge(s("tab_mm"), c + 1)
                if c >= 2:
                    act.wait_ge(s("tab_ready"), c - 1)
                a(tab_top[:, c % 2, :], PS[:, 5 + c % 2, 0:TABP], ACT.Copy).then_inc(s("tab_hi"), 1)
            for f in range(2):
                act.wait_ge(s("summ"), f + 1)
                a(hT[:, f, :], PS[:, 4 * f, :], bias=tb[:, B_PB:B_PB + 1], scale=1.0 / POS).then_inc(s("h_ready"), 1)
            for r in range(ROUNDS):
                for f in range(2):
                    act.wait_ge(s("t_ab"), 2 * r + f + 1)
                    a(a_sb[:, f, :], PS[:, 4 * f, :], bias=tb[:, B_M1:B_M1 + 1]).then_inc(s("t_a"), 1)
                for f in range(2):
                    for d in range(WIN + 1):
                        act.wait_ge(s("t_pre"), 5 * (2 * r + f) + d + 1)
                        v = pre[:, f, d, :].rearrange("p (b n) -> p b n", b=HB)[:, :, d:CPB]
                        a(v, v, ACT.Gelu).then_inc(s("t_g"), 1)
                for f in range(2):
                    act.wait_ge(s("t_agg"), 2 * r + f + 1)
                    a(agg_sb[:, f, :], PS[:, 4 * f + 2, :], bias=tb[:, B_M2:B_M2 + 1]).then_inc(s("t_aggs"), 1)
                for f in range(2):
                    act.wait_ge(s("t_u"), 2 * r + f + 1)
                    a(gu_sb[:, f, :], PS[:, 4 * f + 3, :], ACT.Gelu, bias=tb[:, B_U1:B_U1 + 1]).then_inc(s("t_gu"), 1)
                for f in range(2):
                    act.wait_ge(s("t_T"), 2 * r + f + 1)
                    a(hT[:, f, :], PS[:, 4 * f + 1, :], bias=tb[:, B_MB:B_MB + 1], scale=tb[:, B_MG:B_MG + 1]
                      ).then_inc(s("h_ready"), 1)
            act.wait_ge(s("bc_mm"), 1)
            a(bcparts[:, 0, :, :].rearrange("p (k a) n -> p k (a n)", k=4), PS[:, 0:4, 0:2 * TAB], ACT.Copy
              ).then_inc(s("bc_hi"), 1)

            def a_copies(q, pairs):
                for c2 in pairs:
                    act.wait_ge(s("a_stat"), q * 4 + c2 + 1)
                    if c2 == 0 and (not isinstance(q, int) or q > 0):
                        act.wait_ge(s("a_u_used"), q)
                    src = PS[:, BANK_A if c2 % 2 == 0 else BANK_Q, 0:2 * TAB].rearrange("p (c n) -> p c n", c=2)[:, :, DT:TAB]
                    a(u_sb[:, 2 * c2:2 * c2 + 2, :], src, ACT.Copy).then_inc(s("a_ucopy"), 1)

            def a_high(q):
                act.wait_ge(s("a_xn"), q + 1)
                if not isinstance(q, int) or q > 0:
                    act.wait_ge(s("a_T"), q)
                a(xhl[:, :, 0:D], xn[:, :, :], ACT.Copy).then_inc(s("a_hi"), 1)

            def a_evacuate(q):
                act.wait_ge(s("a_T"), q + 1)
                if not isinstance(q, int) or q > 0:
                    act.wait_ge(s("qc_mm"), q)
                    act.wait_ge(s("ktok_mm"), q)
                a(xs1[:, :].rearrange("p (n c) -> p c n", c=POS), psT16.rearrange("p (c n) -> p c n", c=POS),
                  ACT.Copy).then_inc(s("xs1_ready"), 1)

            def c_high(q):
                act.wait_ge(s("c_xn"), q + 1)
                if not isinstance(q, int) or q > 0:
                    act.wait_ge(s("c_T"), q)
                a(xhl2[:, :, 0:D], xn2[:, :, :], ACT.Copy).then_inc(s("c_hi"), 1)

            def c_evacuate(q):
                act.wait_ge(s("c_T"), q + 1)
                a(xs2[:, bass.ds(q * QT, QT)], psT16, ACT.Copy).then_inc(s("xs2_ready"), 1)

            def c_exp(q):
                act.wait_ge(s("r_log"), q + 1)
                a(rexp[:, :, :], rlog[:, :, :], ACT.Exp, scale=1.0 / SW).then_inc(s("r_exp"), 1)

            def c_mask_copy(q):
                act.wait_ge(s("m_T"), q + 1)
                if not isinstance(q, int) or q > 0:
                    act.wait_ge(s("m_stored"), q * 16)
                a(mT[:, :], PS[0:D, BANK_T, 0:P], ACT.Copy).then_inc(s("mT_ready"), 1)

            def b_high(q, uses):
                for u in uses:
                    act.wait_ge(s("qk_mm"), q * 8 + u + 1)
                    if not isinstance(q, int) or q > 0 or u >= 4:
                        act.wait_ge(s("qk_split"), q * 8 + u - 3)
                    a(qk_hi[:, u % 4, :], PS[:, u % 4, :], ACT.Copy).then_inc(s("qk_hi_ready"), 1)

            def b_value_copies(q):
                act.wait_ge(s("v_mm"), q + 1)
                if not isinstance(q, int) or q > 0:
                    act.wait_ge(s("pv_done"), q * 4)
                pv = PS[:, BANK_Q, :].rearrange("p (n g j d) -> p n g j d", n=8, g=2, j=4)
                for g in range(2):
                    a(vx[:, :, g, :].rearrange("p n (j w) -> p n j w", w=40)[:, :, :, 0:DH], pv[:, :, g, :, :],
                      ACT.Copy).then_inc(s("vx_ready"), 1)
                act.wait_ge(s("ktok_mm"), q + 1)
                a(ktok[:, :, :], PS[:, BANK_A, 0:4 * D].rearrange("p (b n) -> p b n", b=4), ACT.Copy
                  ).then_inc(s("ktok_ready"), 1)

            def b_output_high(q):
                act.wait_ge(s("pv_done"), q * 4 + 4)
                if not isinstance(q, int) or q > 0:
                    act.wait_ge(s("proj_mm"), q)
                for k in range(2):
                    a(ostk[0:D, :].rearrange("p (b a n) -> p b a n", b=4, a=2)[:, :, k, :],
                      PS[64 * k:64 * k + 64, BANK_O, :].rearrange("p (b n) -> p b n", b=4), ACT.Copy
                      ).then_inc(s("ohi_ready"), 1)

            def quad(q, has_n, has_a, has_c):
                for n in range(8):
                    if n == 0 and has_n:
                        a_high(q + 1)
                    if n == 1 and has_n:
                        a_evacuate(q + 1)
                    if n == 2 and has_c:
                        c_high(q - 1)
                    if n == 2 and has_a:
                        a_copies(q + 2, (0,))
                    if n == 3 and has_a:
                        a_copies(q + 2, (1,))
                    if n == 3 and has_c:
                        c_evacuate(q - 1)
                    if n in (4, 5) and has_a:
                        a_copies(q + 2, (n - 2,))
                    if n == 5 and has_c:
                        c_exp(q - 1)
                if has_n:
                    b_high(q + 1, (0, 1, 2, 3))
                b_output_high(q)
                if has_n:
                    b_high(q + 1, (4, 5, 6, 7))
                if has_c:
                    c_mask_copy(q - 1)
                if has_n:
                    b_value_copies(q + 1)

            a_copies(0, (0, 1, 2, 3))
            a_copies(1, (0, 1, 2, 3))
            a_high(0)
            a_evacuate(0)
            b_high(0, range(8))
            b_value_copies(0)
            quad(0, True, True, False)
            with act.Fori(1, NQ - 2) as q:
                quad(q, True, True, True)
            quad(NQ - 2, True, False, True)
            quad(NQ - 1, False, False, True)
            def y_high(q):
                act.wait_ge(s("y_acc"), q + 1)
                if not isinstance(q, int) or q > 0:
                    act.wait_ge(s("f_mm"), q)
                a(y_hi[:, :], yacc[:, :], ACT.Copy).then_inc(s("yhi_ready"), 1)

            def store(q):
                act.wait_ge(s("f_used"), q + 1)
                act.dma_start(out_v[bass.ds(q * P, P), :], obuf[:, :]).then_inc(s("out_done"), 16)

            def gelu(q, t):
                act.wait_ge(s("l1_done"), q * NT1 + t + 1)
                if not isinstance(q, int) or 9 * q + t // 2 - 2 > 0:
                    act.wait_ge(s("l2_done"), q * 9 + t // 2 - 2)
                a(gring[:, t % GR, :], PS[:, 2 * (t % 2):2 * (t % 2) + 2, :], ACT.Gelu,
                  bias=b1_sb[:, t:t + 1], scale=1.0 / SW).then_inc(s("gelu_done"), 1)

            def ffn(q, first, has_fold):
                for t in range(first, NT1):
                    gelu(q, t)
                    if t == 2 and has_fold:
                        y_high(q - 1)
                    if t == 8 and has_fold:
                        store(q - 1)

            act.wait_ge(s("ld_ffn"), 48)
            act.wait_ge(s("pv_done"), 4 * NQ)
            gelu(0, 0)
            gelu(0, 1)
            c_high(NQ - 1)
            c_evacuate(NQ - 1)
            gelu(0, 2)
            c_exp(NQ - 1)
            for t in range(3, 8):
                gelu(0, t)
            c_mask_copy(NQ - 1)
            ffn(0, 8, False)
            with act.Fori(1, NQ) as q:
                ffn(q, 0, True)
            y_high(NQ - 1)
            store(NQ - 1)

        @block.vector
        def _(dve):
            v = nc.vector
            ch = Steps(dve, s("dve_step"))
            tt = v.tensor_tensor

            def stats_tail(n, key, width):
                e, x = st[key], stx[key]
                ch.step(tt(x[:, 0, 0:n], e[:, 0:n, 1], e[:, 0:n, 4], ALU.subtract))
                ch.step(tt(x[:, 1, 0:n], e[:, 0:n, 2], e[:, 0:n, 5], ALU.add))
                ch.step(tt(x[:, 2, 0:n], e[:, 0:n, 1], e[:, 0:n, 4], ALU.add))
                ch.settle()
                ch.step(tt(x[:, 3, 0:n], x[:, 0, 0:n], x[:, 0, 0:n], ALU.mult))
                ch.step(v.tensor_scalar(x[:, 5, 0:n], x[:, 2, 0:n], 0.5, None, ALU.mult))
                ch.settle()
                ch.step(v.scalar_tensor_tensor(x[:, 0, 0:n], x[:, 3, 0:n], width / 4.0, x[:, 1, 0:n],
                                               ALU.mult, ALU.add))
                ch.settle()
                v.tensor_scalar(x[:, 4, 0:n], x[:, 0, 0:n], 1.0 / width, EPS, ALU.mult, ALU.add
                                ).then_inc(s("stats_" + key), 1)

            dve.wait_ge(s("ld_cst"), 16)
            v.tensor_copy(identb[:, :], ident).then_inc(s("identb_ready"), 1)
            v.tensor_copy(identh[:, :], ident).then_inc(s("identb_ready"), 1)
            dve.wait_ge(s("ld_slope"), 32)
            v.tensor_copy(slope_row[:, :, :], slope_bc[:, :].rearrange("p (h o) -> p h o", o=1)
                          .broadcast_to([P, H, DH])).then_inc(s("slope_ready"), 1)
            v.tensor_scalar(neg_slope[:, :], slope_bc[:, :], -1.0, None, ALU.mult).then_inc(s("slope_ready"), 1)
            v.tensor_copy(rt[:, 0:DT], ident).then_inc(s("rt_id"), 1)
            v.tensor_copy(pair_sum[:, :], cst[:, C_II:C_II + D]).then_inc(s("zero_ready"), 1)
            v.memset(vx[:, :, :, :], 0.0).then_inc(s("zero_ready"), 1)
            v.memset(mtok[:, :], 0.0).then_inc(s("zero_ready"), 1)
            v.memset(sbd[:, :, :], 0.0).then_inc(s("zero_ready"), 1)
            ch.step(v.memset(qdec[64:128, :, :], 0.0))
            ch.step(v.memset(table3[:, :, :], 0.0))
            dve.wait_ge(s("ld_emb"), 160)
            for k in range(4):
                tt(htab[:, k, :], embt[:, :], postab[:, k, :], ALU.add).then_inc(s("htab_ready"), 1)
            dve.wait_ge(s("htab_ready"), 4)
            for k in range(4):
                ch.step(v.bn_stats(st["t"][:, k, :], htab[:, k, :]))
            ch.settle()
            stats_tail(4, "t", DT)
            dve.wait_ge(s("rstd_t"), 1)
            for k in range(4):
                v.tensor_scalar(xt[:, k, :], htab[:, k, :], stx["t"][:, 5, k:k + 1], rstd["t"][:, k:k + 1],
                                ALU.subtract, ALU.mult).then_inc(s("xt_ready"), 1)
            dve.wait_ge(s("ld_tow"), 32)
            ch.step(v.tensor_copy(fb_bc[:, :], tb[:, B_FB:B_FB + 1].broadcast_to([P, P])))
            ch.step(v.tensor_copy(bx[:, 0:DT], tw[:, T_BC:T_BC + DT]))
            ch.settle()
            v.tensor_scalar(gh[:, :], tw[:, T_HW:T_HW + D], tb[:, B_FG:B_FG + 1], None, ALU.mult
                            ).then_inc(s("gh_ready"), 1)
            for k in range(4):
                dve.wait_ge(s(f"ld_ids{k}"), 16)
                v.tensor_scalar(onehot[:, 2 * k:2 * k + 2, :], ids_stage[:, k % 2, :],
                                cst[:, C_COL:C_COL + 1], None, ALU.is_equal).then_inc(s("onehot_ready"), 1)
            dve.wait_ge(s("loc_ready"), 1)
            v.tensor_scalar(locdb[:, :, :, :], locd[:, :, :, :], tb[:, B_BC:B_BC + 1], None, ALU.add
                            ).then_inc(s("locb_ready"), 1)
            for c in range(POS):
                dve.wait_ge(s("tab_hi"), c + 1)
                top, acc = tab_top[:, c % 2, :], PS[:, 5 + c % 2, 0:TABP]
                ch.step(v.scalar_tensor_tensor(table[:, c, :], top, cst[:, C_COL + 3:C_COL + 4], acc,
                                               ALU.mult, ALU.add))
                ch.step(tt(tab_rest[:, :], acc, top, ALU.subtract))
                ch.settle()
                v.scalar_tensor_tensor(table3[64:128, c, :], table[64:128, c, :], -1.0, tab_rest[64:128, :],
                                       ALU.mult, ALU.add).then_inc(s("tab_ready"), 1)
                dve.wait_ge(s("tab_ready"), c + 1)
            dve.wait_ge(s("decay_raw"), 8)
            tt(decay[:, :, :, :].rearrange("p j g c -> p (j g) c"), decay[:, :, :, :].rearrange("p j g c -> p (j g) c"),
               cst[:, C_CAUS:C_CAUS + CH].rearrange("p (o c) -> p o c", o=1).broadcast_to([P, H, CH]), ALU.mult
               ).then_inc(s("decay_ready"), 1)
            dve.wait_ge(s("dec_raw"), 1)
            v.tensor_scalar(dec[:, :], dec[:, :], DH ** -0.5 / SW ** 2, None, ALU.mult).then_inc(s("decay_ready"), 1)
            inv = cst[:, C_INV:C_INV + CPB].rearrange("p (o n) -> p o n", o=1).broadcast_to([P, HB, CPB])
            dve.wait_ge(s("ld_rows"), 32)

            def seqs(x):
                return x.rearrange("p (b n) -> p b n", b=HB)

            for f in range(2):
                for d in range(1, WIN + 1):
                    ch.step(v.memset(seqs(pre[:, f, d, :])[:, :, 0:d], 0.0))
            for r in range(ROUNDS):
                for f in range(2):
                    dve.wait_ge(s("t_a"), 2 * r + f + 1)
                    for d in range(WIN + 1):
                        tt(seqs(pre[:, f, d, :])[:, :, d:CPB], seqs(PS[:, 4 * f + 1, :])[:, :, 0:CPB - d],
                           seqs(a_sb[:, f, :])[:, :, d:CPB], ALU.add).then_inc(s("t_pre"), 1)
                for f in range(2):
                    base = 5 * (2 * r + f)
                    dve.wait_ge(s("t_g"), base + 2)
                    ch.step(tt(msum[:, f, :], pre[:, f, 0, :], pre[:, f, 1, :], ALU.add))
                    for d in range(2, WIN + 1):
                        dve.wait_ge(s("t_g"), base + d + 1)
                        ch.settle()
                        ch.step(tt(msum[:, f, :], msum[:, f, :], pre[:, f, d, :], ALU.add))
                    ch.settle()
                    tt(seqs(msum[:, f, :]), seqs(msum[:, f, :]), inv, ALU.mult).then_inc(s("t_sum"), 1)
                for f in range(2):
                    dve.wait_ge(s("t_r"), 2 * r + f + 1)
                    x = rtok[f]
                    ch.step(tt(x, PS[:, 4 * f, :].rearrange("p (t n) -> p t n", t=4),
                               updb2_bc[:, :].rearrange("p (o n) -> p o n", o=1).broadcast_to([P, 4, DT]), ALU.add))
                    ch.settle()
                    for t in range(4):
                        ch.step(v.bn_stats(st["t"][:, 4 * f + t, :], x[:, t, :]))
                ch.settle()
                stats_tail(8, "t", DT)
                dve.wait_ge(s("rstd_t"), r + 2)
                for f in range(2):
                    for t in range(4):
                        k = 4 * f + t
                        v.tensor_scalar(rtok[f][:, t, :], rtok[f][:, t, :], stx["t"][:, 5, k:k + 1],
                                        rstd["t"][:, k:k + 1], ALU.subtract, ALU.mult).then_inc(s("t_xc"), 1)
            dve.wait_ge(s("bc_hi"), 1)
            acc = PS[:, 0:4, 0:2 * TAB]

            def parts(k):
                return bcparts[:, k, :, :].rearrange("p (k a) n -> p k (a n)", k=4)

            rest = bc_rest.rearrange("p (k n) -> p k n", k=4)
            ch.step(tt(rest, acc, parts(0), ALU.subtract))
            ch.settle()
            ch.step(v.tensor_copy(parts(1), rest))
            ch.settle()
            tt(parts(2), rest, parts(1), ALU.subtract).then_inc(s("bc_ready"), 1)
            dve.wait_ge(s("kdec_ready"), 1)

            def bc_d(x, width):
                return x.rearrange("p (c o) -> p c o", o=1).broadcast_to([P, POS, width])

            def a_stats(q, pairs):
                for c2 in pairs:
                    dve.wait_ge(s("a_mm"), q * 4 + c2 + 1)
                    for c in (2 * c2, 2 * c2 + 1):
                        bank = BANK_A if c2 % 2 == 0 else BANK_Q
                        i = v.bn_stats(st["f"][:, c, :], PS[:, bank, (c % 2) * TAB:(c % 2) * TAB + DT])
                        if c % 2 == 0:
                            ch.step(i)
                    i.then_inc(s("a_stat"), 1)
                if pairs[-1] == 3:
                    dve.wait_ge(s("a_stat"), q * 4 + 4)
                    if not isinstance(q, int) or q > 0:
                        dve.wait_ge(s("rstd_f"), q)
                    stats_tail(8, "f", DT)

            def a_hidden_stats(q):
                dve.wait_ge(s("a_h"), q + 1)
                for c in (1, 2, 3, 4, 5, 6, 7, 0):
                    ch.step(v.bn_stats(st["a"][:, c, :], h_res[:, bass.ds(q * POS * D + c * D, D)]))
                ch.settle()
                stats_tail(8, "a", D)

            def c_stats(q):
                if not isinstance(q, int) or q >= 0:
                    dve.wait_ge(s("h2_done"), q + 1)
                for c in (1, 2, 3, 4, 5, 6, 7, 0):
                    ch.step(v.bn_stats(st["c"][:, c, :], h_res[:, bass.ds(q * POS * D + c * D, D)]))
                ch.settle()
                stats_tail(8, "c", D)

            def c_logits(q):
                dve.wait_ge(s("r_mm"), q + 1)
                ps = PS[:, BANK_T, 0:POS * E].rearrange("p (c e) -> p c e", c=POS)
                ch.step(v.tensor_reduce(rmax[:, 0, :], ps, op=ALU.max, axis=AX_X))
                ch.settle()
                tt(rlog[:, :, :], ps, bc_d(rmax[:, 0, :], E), ALU.subtract).then_inc(s("r_log"), 1)

            def c_top2(q):
                dve.wait_ge(s("r_exp"), q + 1)
                ch.step(v.tensor_reduce(rmax[:, 1, :], rexp[:, :, :], op=ALU.add, axis=AX_X))
                ch.settle()
                ch.step(v.reciprocal(rmax[:, 2, :], rmax[:, 1, :]))
                ch.settle()
                ch.step(tt(rw[:, :, :], rexp[:, :, :], bc_d(rmax[:, 2, :], E), ALU.mult))
                ch.settle()
                wj = rw[:, :, :].rearrange("p c (o j) -> p c o j", o=1).broadcast_to([P, POS, E, E])
                we = rw[:, :, :].rearrange("p c (e o) -> p c e o", o=1).broadcast_to([P, POS, E, E])
                tt(rge[:, :, :, :], wj, we, ALU.is_ge).then_inc(s("r_ge"), 1)

            def c_top2_rest(q):
                dve.wait_ge(s("r_df"), q + 1)
                ch.step(v.tensor_reduce(rank[:, :, :], rdf[:, :, :, :], op=ALU.add, axis=AX_X))
                ch.settle()
                thr = cst[:, C_THR:C_THR + E].rearrange("p (o n) -> p o n", o=1).broadcast_to([P, POS, E])
                ch.step(tt(rank[:, :, :], rank[:, :, :], thr, ALU.is_lt))
                ch.settle()
                ch.step(tt(rw[:, :, :], rw[:, :, :], rank[:, :, :], ALU.mult))
                ch.settle()
                ch.step(v.tensor_reduce(rmax[:, 1, :], rw[:, :, :], op=ALU.add, axis=AX_X))
                ch.settle()
                ch.step(v.reciprocal(rmax[:, 3, :], rmax[:, 1, :]))
                ch.settle()
                if not isinstance(q, int) or q > 0:
                    dve.wait_ge(s("m_T"), q)
                tt(mtok[:, 0:POS * E].rearrange("p (e c) -> p c e", e=E), rw[:, :, :], bc_d(rmax[:, 3, :], E),
                   ALU.mult).then_inc(s("m_ready"), 1)

            def b_split(q, uses):
                for u in uses:
                    dst, g, half = (q32, k32)[u // 4], u // 2 % 2, u % 2
                    dve.wait_ge(s("qk_hi_ready"), q * 8 + u + 1)
                    if u == 0 and (not isinstance(q, int) or q > 0):
                        dve.wait_ge(s("scores"), q * 16)
                    v.scalar_tensor_tensor(
                        dst[:, g, half * 512:(half + 1) * 512], qk_hi[:, u % 4, :],
                        cst[:, C_COL + 1 + u // 4:C_COL + 2 + u // 4], PS[:, u % 4, :], ALU.mult, ALU.add
                    ).then_inc(s("qk_split"), 1)

            def b_decayed_values(q):
                dve.wait_ge(s("vx_ready"), q * 2 + 2)
                if not isinstance(q, int) or q > 0:
                    dve.wait_ge(s("kv_mm"), q)
                pv = PS[:, BANK_Q, :].rearrange("p (b a n) -> p b a n", b=4, a=2)[:, :, 0, :]
                tt(vdec[:, :, :], pv, kdec[:, :].rearrange("p (o n) -> p o n", o=1).broadcast_to([P, 4, D]),
                   ALU.mult).then_inc(s("vdec_ready"), 1)

            def b_decayed_queries(q):
                dve.wait_ge(s("qc_mm"), q + 1)
                if not isinstance(q, int) or q > 0:
                    dve.wait_ge(s("pv_done"), q * 4)
                tt(qdec[0:D, :, :], PS[0:D, BANK_T, :].rearrange("p (b n) -> p b n", b=4),
                   dec[:, :].rearrange("p (o n) -> p o n", o=1).broadcast_to([D, 4, CH]), ALU.mult
                   ).then_inc(s("qdec_ready"), 1)

            def b_masked_state(q):
                dve.wait_ge(s("kv_mm"), q + 1)
                tt(sbd[0:D, :, :], PS[0:D, BANK_A, 256:512].rearrange("p (b n) -> p b n", b=4),
                   cst[0:D, C_BLK:C_BLK + D].rearrange("p (o n) -> p o n", o=1).broadcast_to([D, 4, D]), ALU.mult
                   ).then_inc(s("sbd_ready"), 1)

            def b_mask(q, n):
                b = n // 2
                for j in (2 * (n % 2), 2 * (n % 2) + 1):
                    dve.wait_ge(s("scores"), q * 16 + 4 * b + j + 1)
                    if j == 0 and (not isinstance(q, int) or 4 * q + b - 1 > 0):
                        dve.wait_ge(s("pv_done"), q * 4 + b - 1)
                    tt(probs[:, b % 2, j, :].rearrange("p (a n) -> p a n", a=2),
                       PS[:, j, :].rearrange("p (a n) -> p a n", a=2),
                       decay[:, j, :, :].rearrange("p (o g) c -> p o (g c)", o=1).broadcast_to([P, 2, 2 * CH]),
                       ALU.mult).then_inc(s("mask_done"), 1)

            def b_output_low(q):
                for k in range(2):
                    dve.wait_ge(s("ohi_ready"), q * 2 + k + 1)
                    hi = ostk[0:D, :].rearrange("p (b a n) -> p b a n", b=4, a=2)[:, :, k, :]
                    lo = ostk[D:P, :].rearrange("p (b a n) -> p b a n", b=4, a=2)[:, :, k, :]
                    tt(lo, PS[64 * k:64 * k + 64, BANK_O, :].rearrange("p (b n) -> p b n", b=4), hi, ALU.subtract
                       ).then_inc(s("olo_ready"), 1)

            def b_residual(q):
                hq = h_res[:, bass.ds(q * POS * D, POS * D)]
                dve.wait_ge(s("proj_mm"), q + 1)
                dve.wait_ge(s("h_bias"), q + 1)
                v.scalar_tensor_tensor(hq, PS[:, BANK_O, :], SW ** -2, hq, ALU.mult, ALU.add
                                       ).then_inc(s("h2_done"), 1)

            def quad(q, has_n, has_a, has_c):
                for n in range(8):
                    b_mask(q, n)
                    if n == 0:
                        b_masked_state(q)
                    if n == 0 and has_c:
                        c_stats(q - 1)
                    if n in (2, 3, 4, 5) and has_a:
                        a_stats(q + 2, (n - 2,))
                    if n == 5 and has_c:
                        c_logits(q - 1)
                    if n == 6 and has_c:
                        c_top2(q - 1)
                if has_a:
                    a_hidden_stats(q + 2)
                if has_n:
                    b_split(q + 1, (0, 1, 2, 3))
                if has_c:
                    c_top2_rest(q - 1)
                b_output_low(q)
                if has_n:
                    b_split(q + 1, (4, 5, 6, 7))
                    b_decayed_values(q + 1)
                b_residual(q)
                if has_n:
                    b_decayed_queries(q + 1)

            a_stats(0, (0, 1, 2, 3))
            a_stats(1, (0, 1, 2, 3))
            a_hidden_stats(0)
            dve.wait_ge(s("decay_ready"), 2)
            b_split(0, range(8))
            b_decayed_values(0)
            b_decayed_queries(0)
            a_hidden_stats(1)
            quad(0, True, True, False)
            with dve.Fori(1, NQ - 2) as q:
                ch.enter(q, 1, PER_QUAD)
                quad(q, True, True, True)
            ch.leave(NQ - 3)
            quad(NQ - 2, True, False, True)
            quad(NQ - 1, False, False, True)
            c_stats(NQ - 1)
            c_logits(NQ - 1)
            c_top2(NQ - 1)
            c_top2_rest(NQ - 1)

            def use_unit(q, unit):
                acc = PS[:, BANK_Q - 2 * (unit % 2):BANK_Q + 2 - 2 * (unit % 2), :]
                dve.wait_ge(s("l2_done"), q * 9 + 2 * unit + 1)
                y2 = yacc[:, :].rearrange("p (k n) -> p k n", k=2)
                if unit == 0:
                    if not isinstance(q, int) or q > 0:
                        dve.wait_ge(s("ylo_ready"), q)
                    v.tensor_scalar(y2, acc, b2_sb[:, 0:1], None, ALU.add).then_inc(s("y_used"), 1)
                    return
                pr = unit - 1
                dve.wait_ge(s(f"m_loaded{pr}"), q * 32 + 32)
                v.scalar_tensor_tensor(ytmp[:, :].rearrange("p (k n) -> p k n", k=2), acc, b2_sb[:, unit:unit + 1],
                                       mb[:, pr, :].rearrange("p (k n) -> p k n", k=2), ALU.add, ALU.mult
                                       ).then_inc(s("y_used"), 1)
                dve.wait_ge(s("y_used"), q * 5 + unit + 1)
                tt(yacc[:, :], yacc[:, :], ytmp[:, :], ALU.add).then_inc(s("m_used"), 1)
                dve.wait_ge(s("m_used"), q * 4 + unit)

            def y_low(q):
                dve.wait_ge(s("yhi_ready"), q + 1)
                if not isinstance(q, int) or q > 0:
                    dve.wait_ge(s("f_mm"), q)
                tt(y_lo[:, :], yacc[:, :], y_hi[:, :], ALU.subtract).then_inc(s("ylo_ready"), 1)

            def finish(q):
                dve.wait_ge(s("f_mm"), q + 1)
                if not isinstance(q, int) or q > 0:
                    dve.wait_ge(s("out_done"), q * 16)
                tt(obuf[:, :], PS[:, BANK_Q, :], h_res[:, bass.ds(q * POS * D, POS * D)], ALU.add).then_inc(s("f_used"), 1)

            def ffn(q, has_fold):
                if has_fold:
                    y_low(q - 1)
                use_unit(q, 0)
                if has_fold:
                    finish(q - 1)
                for unit in range(1, 5):
                    use_unit(q, unit)
                v.tensor_copy(rmax[:, 0, :], rmax[:, 0, :]).then_inc(s("y_acc"), 1)

            dve.wait_ge(s("ld_ffn"), 48)
            ffn(0, False)
            with dve.Fori(1, NQ) as q:
                ffn(q, True)
            y_low(NQ - 1)
            finish(NQ - 1)

        @block.gpsimd
        def _(pool):
            g = nc.gpsimd
            chp = Steps(pool, s("pool_step"))
            g.memset(minus_half[:, :], -0.5).then_inc(s("half_ready"), 1)
            pool.wait_ge(s("half_ready"), 1)

            def power(key, count, n=POS):
                pool.wait_ge(s("stats_" + key), count)
                g.tensor_tensor(rstd[key][:, 0:n], stx[key][:, 4, 0:n], minus_half[:, 0:n], ALU.pow
                                ).then_inc(s("rstd_" + key), 1)

            power("t", 1, 4)

            def split(raw, hi, lo, ready):
                chp.step(g.tensor_scalar(raw, raw, SW, 0.0, ALU.mult, ALU.add))
                chp.settle()
                chp.step(g.tensor_copy(hi, raw))
                chp.settle()
                g.tensor_tensor(lo, raw, hi, ALU.subtract).then_inc(s(ready), 1)

            pool.wait_ge(s("ld_attn"), 16)
            split(wa[:, :], wa_hi[:, :], wa_lo[:, :], "wa_ready")
            pool.wait_ge(s("ld_w1"), 16)
            split(w1_raw.rearrange("p (t n) -> p t n", t=NT1), w1_hi[:, :, :], w1_lo[:, :, :], "w1_ready")
            for r in range(ROUNDS):
                power("t", r + 2)
            def bc_d(x, width):
                return x.rearrange("p (c o) -> p c o", o=1).broadcast_to([P, POS, width])

            def bc_row(x):
                return x.rearrange("p (o n) -> p o n", o=1).broadcast_to([P, POS, D])

            def h_rows(q):
                return h_res[:, bass.ds(q * POS * D, POS * D)].rearrange("p (c n) -> p c n", c=POS)

            def a_hidden(q):
                power("f", q + 1)
                pool.wait_ge(s("rstd_f"), q + 1)
                pool.wait_ge(s("a_ucopy"), q * 4 + 4)
                g.tensor_tensor(xn[:, :, :], u_sb[:, :, :], bc_d(rstd["f"][:, :], D), ALU.mult
                                ).then_inc(s("a_u_used"), 1)
                pool.wait_ge(s("a_u_used"), q + 1)
                g.tensor_tensor(h_rows(q), xn[:, :, :], bc_row(hb[:, :]), ALU.add).then_inc(s("a_h"), 1)

            def normalize(q, key, x, x_hl):
                power(key, q + 1)
                chp.step(g.tensor_tensor(x[:, :, :], h_rows(q), bc_d(stx[key][:, 5, :], D), ALU.subtract))
                chp.settle()
                pool.wait_ge(s("rstd_" + key), q + 1)
                g.tensor_tensor(x[:, :, :], x[:, :, :], bc_d(rstd[key][:, :], D), ALU.mult
                                ).then_inc(s(key + "_xn"), 1)
                if key == "a":
                    g.tensor_tensor(h_rows(q), h_rows(q), bc_row(bproj_bc[:, :]), ALU.add).then_inc(s("h_bias"), 1)
                pool.wait_ge(s(key + "_xn"), q + 1)
                pool.wait_ge(s(key + "_hi"), q + 1)
                g.tensor_tensor(x_hl[:, :, D:2 * D], x[:, :, :], x_hl[:, :, 0:D], ALU.subtract
                                ).then_inc(s(key + "_lo"), 1)

            def c_ranks(q):
                low = cst[:, C_LOW:C_LOW + E * E].rearrange("p (o n) -> p o n", o=1).broadcast_to([P, POS, E * E])
                flat = rge[:, :, :, :].rearrange("p c e j -> p c (e j)")
                pool.wait_ge(s("r_ge"), q + 1)
                chp.step(g.tensor_tensor(flat, flat, low, ALU.mult))
                chp.settle()
                g.tensor_tensor(rdf[:, :, :, :], rge[:, :, :, :], rge[:, :, :, :].rearrange("p c e j -> p c j e"),
                                ALU.subtract).then_inc(s("r_df"), 1)

            def quad(q, has_n, has_a, has_c):
                if has_n:
                    normalize(q + 1, "a", xn, xhl)
                if has_c:
                    normalize(q - 1, "c", xn2, xhl2)
                if has_a:
                    a_hidden(q + 2)
                if has_c:
                    c_ranks(q - 1)

            pool.wait_ge(s("hb_ready"), 1)
            pool.wait_ge(s("ld_rows"), 32)
            a_hidden(0)
            normalize(0, "a", xn, xhl)
            a_hidden(1)
            quad(0, True, True, False)
            with pool.Fori(1, NQ - 2) as q:
                chp.enter(q, 1, POOL_PER_QUAD)
                quad(q, True, True, True)
            chp.leave(NQ - 3)
            quad(NQ - 2, True, False, True)
            quad(NQ - 1, False, False, True)
            normalize(NQ - 1, "c", xn2, xhl2)
            c_ranks(NQ - 1)


_INS = ["ids", "emb", "pos", "consts", "towerw", "towerb", "updb2", "attnw", "bproj", "slopes", "w1", "b1", "w2", "b2"]


def shape_constants():
    import numpy as np
    c = np.zeros((P, C_END), np.float32)
    c[:, C_ID:C_ID + P] = np.eye(P)
    c[:, C_CEN:C_CEN + P] = np.eye(P) - 1.0 / DT
    e, t = np.arange(CH)[:, None], np.arange(CH)[None, :]
    c[:, C_DIFF:C_DIFF + CH] = np.maximum(t - e, 0)
    c[:, C_CAUS:C_CAUS + CH] = (t >= e) * (DH ** -0.5 / SW ** 2)
    c[:, C_II:C_II + D] = np.vstack([np.eye(D), np.eye(D)])
    hd = np.arange(D) // DH
    c[0:D, C_BLK:C_BLK + D] = hd[:, None] == hd[None, :]
    j = np.arange(E)
    c[:, C_THR:C_THR + E] = 2.0 - (E - 1 - j)
    c[:, C_LOW:C_LOW + E * E] = (j[None, :] < j[:, None]).reshape(-1)
    p = np.arange(P)
    c[:, C_COL] = p % VOCAB
    c[:, C_COL + 1] = -1.0 * (p // 16 % 2)
    c[:, C_COL + 2] = -1.0 * (p // 8 % 2)
    c[:, C_COL + 3] = -1.0 * (p // 64)
    c[:, C_COL + 4] = -1.0 * (CH - p)
    c[:, C_INV:C_INV + CPB] = 1.0 / np.minimum(np.arange(CPB) + 1, WIN + 1)
    c[:, C_NEGC:C_NEGC + CH] = -np.arange(CH)
    return c


def laid_out(inputs):
    import numpy as np

    a = {k: np.asarray(v) for k, v in inputs.items()}
    t = {k[7:]: v for k, v in a.items() if k.startswith("L0_tok_")}
    w = {k[8:]: v for k, v in a.items() if k.startswith("L0_attn_")}
    m = {k[7:]: v for k, v in a.items() if k.startswith("L0_ffn_")}

    def tiles(x, n):
        return np.concatenate([x[P * i:P * (i + 1)] for i in range(n)], axis=1)

    def col(x):
        return x.reshape(-1, P).T

    def slots(x):
        return np.repeat(x.reshape(D, H, 1, DH), 4, axis=2).reshape(D, H * 4 * DH)

    wq, wk, wv = (w["w_qkv"][:, k * D:(k + 1) * D] for k in range(3))
    attnw = np.concatenate([slots(wq), slots(wk), wv, wk, wq, w["w_proj"], m["Wr"]], axis=1)
    w1t = [m["W1s"][:, :P], m["W1s"][:, P:]]
    b1t = [m["b1s"][:P], m["b1s"][P:]]
    w2t = [m["W2s"][:P], m["W2s"][P:]]
    for pr in range(E // 2):
        for f in range(2):
            for e in (2 * pr, 2 * pr + 1):
                w1t.append(m["W1p"][e][:, f * P:(f + 1) * P])
                b1t.append(m["b1p"][e][f * P:(f + 1) * P])
                w2t.append(m["W2p"][e][f * P:(f + 1) * P])
    w1 = np.concatenate(w1t, axis=1)
    zero = np.zeros_like(m["b2s"])
    arrays = {
        "ids": a["x"].reshape(NCHUNK, POS).T.reshape(-1),
        "emb": t["emb"], "pos": t["pos"], "consts": shape_constants(),
        "towerw": np.concatenate([t["lw1"], tiles(t["lw2"], 2), tiles(t["msg_w1"], 2), t["msg_w2"],
                                  tiles(t["upd_w1"], 2), t["upd_w2"], t["pool_w"], t["bc_w"], t["bc_w"].T,
                                  t["head_w"]], axis=1),
        "towerb": np.concatenate([col(t[k]) for k in (
            "lb1", "lb2", "lln_g", "lln_b", "pool_b", "msg_b1", "msg_b2", "upd_b1", "mln_g", "mln_b", "bc_b",
            "fln_g", "fln_b")], axis=1),
        "updb2": t["upd_b2"], "attnw": np.concatenate([attnw, attnw], axis=0), "bproj": w["b_proj"],
        "slopes": w["slopes"], "w1": np.concatenate([w1, w1], axis=0), "b1": np.stack(b1t, axis=1),
        "w2": np.concatenate(w2t, axis=1),
        "b2": np.stack([np.concatenate([m["b2s"], zero])] +
                       [m["b2p"][2 * pr:2 * pr + 2].reshape(-1) for pr in range(E // 2)], axis=1),
    }
    return {name: np.ascontiguousarray(arrays[name]) for name in _INS}


def kernel(**inputs):
    import concourse.bacc as bacc
    from concourse.bass_utils import run_bass_kernel_spmd

    arrays = laid_out(inputs)
    nc = bacc.Bacc("TRN2", target_bir_lowering=False, num_devices=1)
    args = {}
    for name in _INS:
        args[name] = nc.dram_tensor(f"in_{name}", arrays[name].shape, mybir.dt.from_np(arrays[name].dtype),
                                    kind="ExternalInput").ap()
    args["out"] = nc.dram_tensor("out_0", (NB, SEQ, D), F32, kind="ExternalOutput").ap()
    build(nc, **args)
    r = run_bass_kernel_spmd(nc, [{f"in_{k}": v for k, v in arrays.items()}], core_ids=[0])
    return r.results[0]["out_0"]
```

```python
from contextlib import ExitStack

import concourse.bass as bass
from concourse import mybir
from concourse.alu_op_type import AluOpType as ALU

ACT = mybir.ActivationFunctionType
F32 = mybir.dt.float32
F16 = mybir.dt.float16
BF16 = mybir.dt.bfloat16
I32 = mybir.dt.int32
AX_X = mybir.AxisListType.X

P = 128
VOCAB, POS, DT, ROUNDS, WIN = 64, 8, 128, 3, 4
NB, SEQ = 32, 256
CPB = SEQ // POS
NCHUNK = NB * CPB
HALF = NCHUNK // 2
HB = HALF // CPB
D, H, DH = 64, 8, 8
CH = 128
F, E = 256, 8
NT1 = 2 * (E + 1)
EPS = 1e-5
ONEHOTS_FIRST = 3
WARM = 10
PER_QUAD = 43
POOL_PER_QUAD = 3
SW = 64.0
SH = 16.0
SY = SH * SW
SPLITS = 4
NQ = NCHUNK // P
QT = P * POS
TAB = DT + D
TABP = TAB + DT

C_ID, C_CEN, C_DIFF, C_CAUS, C_II, C_BLK = 0, 128, 256, 384, 512, 576
C_THR, C_LOW, C_COL, C_INV, C_NEGC, C_END = 640, 648, 712, 720, 752, 880
W_Q, W_K, W_V, W_KC, W_QC, W_P, W_R, W_END = 0, 256, 512, 576, 640, 704, 768, 776
T_L1, T_L2, T_MA, T_MB, T_M2, T_UA, T_UB, T_U2 = 0, 256, 512, 640, 768, 896, 1024, 1152
T_PW, T_BC, T_BCT, T_HW, T_END = 1280, 1408, 1536, 1664, 1728
(B_L1, B_L2, B_LG, B_LB, B_PB, B_M1, B_M2, B_U1, B_MG, B_MB, B_BC, B_FG, B_FB, B_END) = (
    0, 2, 3, 4, 5, 6, 7, 8, 9, 10, 11, 12, 13, 14)


class Steps:

    def __init__(self, eng, sem):
        self.eng, self.sem, self.origin, self.k = eng, sem, 0, 0

    def step(self, ins):
        ins.then_inc(self.sem, 1)
        self.k += 1

    def settle(self):
        self.eng.wait_ge(self.sem, self.origin + self.k)

    def enter(self, i, first, per):
        self.start = self.origin + self.k
        self.per = per
        self.origin, self.k = self.start + (i - first) * per, 0

    def leave(self, times):
        assert self.k == self.per, ("steps in the loop's body", self.k)
        self.origin, self.k = self.start + times * self.per, 0


def build(nc, ids, emb, pos, consts, towerw, towerb, updb2, attnw, bproj, slopes, w1, b1, w2, b2, out):
    mask_rows = nc.dram_tensor("mask_rows", [NQ, E * POS, P], F32).ap()
    out_v = out.rearrange("b (j c) d -> (b j) (c d)", c=POS)

    with ExitStack() as ctx:
        def sb(name, shape, dt=F32):
            return ctx.enter_context(nc.sbuf_tensor(name, shape, dt))

        PS = ctx.enter_context(nc.psum_tensor("PS", [P, 8, 512], F32))
        BANK_A, BANK_T, BANK_Q, BANK_O = 4, 5, 6, 7

        def rows_bank(q, pair):
            return (2, 3)[pair % 2] if isinstance(q, int) and q == 0 else (BANK_A, BANK_Q)[pair % 2]

        cst = sb("cst", [P, C_END])
        ident = cst[:, C_ID:C_ID + P]
        identb = sb("identb", [P, P], BF16)
        identh = sb("identh", [P, P], F16)
        pair_sum = sb("pair_sum", [P, D], F16)
        tw = sb("tw", [P, T_END])
        tb = sb("tb", [P, B_END])
        updb2_bc = sb("updb2_bc", [P, DT])
        bproj_bc = sb("bproj_bc", [P, D])
        slope_bc = sb("slope_bc", [P, H])
        slope_row = sb("slope_row", [P, H, DH])
        neg_slope = sb("neg_slope", [P, H])
        slope_col = sb("slope_col", [D, 1])
        wa = sb("wa", [P, W_END])
        wa_hi = sb("wa_hi", [P, W_END], F16)
        wa_lo = sb("wa_lo", [P, W_END], F16)
        w1_hi = sb("w1_hi", [P, NT1, P], F16)
        w1_lo = sb("w1_lo", [P, NT1, P], F16)
        w2_sb = sb("w2_sb", [P, NT1, D])
        b1_sb = sb("b1_sb", [P, NT1])
        b2_sb = sb("b2_sb", [P, 1 + E // 2])
        minus_half = sb("minus_half", [P, POS])

        slab2 = sb("slab2", [P, POS * NCHUNK // 2])
        onehot = slab2[:, :].bitcast(BF16).rearrange("p (c n) -> p c n", c=POS)
        embt = sb("embt", [P, DT])
        postab = sb("postab", [P, 4, DT])
        htab = sb("htab", [P, 4, DT])
        table = sb("table", [P, POS, TABP], BF16)
        table3 = sb("table3", [P, POS, TABP], BF16)
        bcparts = sb("bcparts", [P, 3, NQ, TAB], BF16)
        rt = sb("rt", [P, TAB])
        bx = sb("bx", [P, TAB])
        gh = sb("gh", [P, D])
        fb_bc = sb("fb_bc", [P, P])
        hb = sb("hb", [P, D])
        hT = sb("hT", [P, 2, HALF])
        slab = sb("slab", [P, 10240])
        w1_raw = slab[:, 10240 - NT1 * P:10240]
        pre = slab[:, 0:2 * (WIN + 1) * HALF].rearrange("p (f d n) -> p f d n", f=2, d=WIN + 1)
        slab3 = sb("slab3", [P, 12 * HALF])

        def part3(k, n, dt=F32):
            x = slab3[:, k * HALF:(k + n) * HALF]
            return x if dt is F32 else x.bitcast(dt)

        lnT, g1 = part3(0, 1), part3(1, 2).rearrange("p (f n) -> p f n", f=2)
        xt = part3(3, 1).rearrange("p (t n) -> p t n", t=4)
        locd = part3(4, 2).rearrange("p (c k v) -> p c k v", c=POS, k=2)
        locdb = part3(6, 2).rearrange("p (c k v) -> p c k v", c=POS, k=2)
        tab_top = sb("tab_top", [P, 2, TABP], BF16)
        tab_rest = slab[:, 6 * NCHUNK:6 * NCHUNK + 2 * TABP].rearrange("p (k n) -> p k n", k=2)
        a_sb = part3(8, 2).rearrange("p (f n) -> p f n", f=2)
        msum = part3(10, 2).rearrange("p (f n) -> p f n", f=2)
        agg_sb = a_sb
        gu_sb = msum
        rtok = lnT.rearrange("p (t n) -> p t n", t=4), g1[:, 0, :].rearrange("p (t n) -> p t n", t=4)
        bc_rest = slab[:, 6 * NCHUNK:6 * NCHUNK + NQ * TAB // 2]
        ids_stage = slab[:, 0:6 * NCHUNK].bitcast(I32).rearrange("p (k n) -> p k n", k=3)
        psT16 = PS[:, BANK_T, :].bitcast(F16)
        GR = 6
        gring = slab[:, 0:GR * QT].rearrange("p (s n) -> p s n", s=GR)
        mb = slab[:, GR * QT:GR * QT + 4 * QT].rearrange("p (s n) -> p s n", s=4)

        h_res = sb("h_res", [P, NQ * POS * D])
        xs1 = sb("xs1", [P, QT], F16)
        xs2 = sb("xs2", [P, NQ * QT], F16)
        u_sb = part3(3, 1).rearrange("p (c n) -> p c n", c=POS)
        xn = part3(1, 1).rearrange("p (c n) -> p c n", c=POS)
        xhl = part3(4, 1, F16).rearrange("p (c n) -> p c n", c=POS)
        xn2 = part3(2, 1).rearrange("p (c n) -> p c n", c=POS)
        xhl2 = part3(5, 1, F16).rearrange("p (c n) -> p c n", c=POS)
        q32 = slab[:, 4 * QT:5 * QT].bitcast(F16).rearrange("p (g n) -> p g n", g=2)
        k32 = slab[:, 5 * QT:6 * QT].bitcast(F16).rearrange("p (g n) -> p g n", g=2)
        qk_hi = sb("qk_hi", [P, 4, 512], F16)
        vx = sb("vx", [P, POS, 2, 160])
        vdec = sb("vdec", [P, 4, D])
        ktok = sb("ktok", [P, 4, D])
        sbd = sb("sbd", [P, 4, D])
        qdec = sb("qdec", [P, 4, CH])
        probs = slab[:, 0:4 * QT].rearrange("p (s j n) -> p s j n", s=2, j=4)
        decay = sb("decay", [P, 4, 2, CH])
        kdec = sb("kdec", [P, D])
        dec = sb("dec", [D, CH])
        ostk = part3(8, 1, F16)
        st = {n: sb(f"st_{n}", [P, POS, 6]) for n in ("t", "u", "f", "a", "c")}
        stx = {n: sb(f"stx_{n}", [P, 6, POS]) for n in ("t", "u", "f", "a", "c")}
        rstd = {n: sb(f"rstd_{n}", [P, POS]) for n in ("t", "u", "f", "a", "c")}
        rmax = sb("rmax", [P, 4, POS])
        rlog = sb("rlog", [P, POS, E])
        rexp = sb("rexp", [P, POS, E])
        rw = sb("rw", [P, POS, E])
        rge = part3(6, 1).rearrange("p (c e j) -> p c e j", c=POS, e=E)
        rdf = part3(7, 1).rearrange("p (c e j) -> p c e j", c=POS, e=E)
        rank = sb("rank", [P, POS, E])
        mtok = sb("mtok", [P, P])
        top_row = sb("top_row", [P, P])
        updb1_all = sb("updb1_all", [P, 1])
        mT = sb("mT", [D, P])
        yacc = slab2[:, 0:QT]
        ytmp = slab2[:, QT:2 * QT]
        y_hi = slab2[:, 2 * QT:5 * QT // 2].bitcast(F16)
        y_lo = slab2[:, 5 * QT // 2:3 * QT].bitcast(F16)
        obuf = sb("obuf", [P, POS * D])
        w2_hi = wa[:, 0:SPLITS * D].bitcast(F16).rearrange("p (i a n) -> p i a n", i=SPLITS, a=2)
        w2_lo = wa[:, SPLITS * D:2 * SPLITS * D].bitcast(F16).rearrange("p (i a n) -> p i a n", i=SPLITS, a=2)

        def hidden_part(i, k, low):
            places = ((9, 10, 11, 8), (0, 1, 3, 4), (2, 5, 6, 7))[i % 3]
            return part3(places[2 * k + low], 1, F16)

        SEMS = {}

        def s(name):
            if name not in SEMS:
                SEMS[name] = ctx.enter_context(nc.semaphore(name))
            return SEMS[name]

        block = ctx.enter_context(nc.Block())

        @block.sync
        def _(sp):
            for k in range(2):
                sp.dma_start(embt[64 * k:64 * k + 64, :], emb).then_inc(s("ld_emb"), 16)
            for k in range(2):
                sp.dma_start(postab[64 * k:64 * k + 64, :, :],
                             pos.rearrange("(c k) d -> k c d", k=2)[k].partition_broadcast(64)
                             ).then_inc(s("ld_emb"), 16)
            for k in range(4):
                if k >= 3:
                    sp.wait_ge(s("onehot_ready"), k - 2)
                sp.dma_start(ids_stage[:, k % 3, :],
                             ids[2 * k * NCHUNK:2 * (k + 1) * NCHUNK].partition_broadcast(P)
                             ).then_inc(s(f"ld_ids{k}"), 16)
            sp.dma_start(updb2_bc[:, :], updb2.partition_broadcast(P)).then_inc(s("ld_rows"), 16)
            sp.dma_start(bproj_bc[:, :], bproj.partition_broadcast(P)).then_inc(s("ld_rows"), 16)
            sp.dma_start(wa[:, :], attnw).then_inc(s("ld_attn"), 16)
            sp.dma_start(w1_raw, w1).then_inc(s("ld_w1"), 16)
            sp.dma_start(w2_sb[:, :, :], w2.rearrange("p (t n) -> p t n", t=NT1)).then_inc(s("ld_ffn"), 16)
            sp.dma_start(b1_sb[:, :], b1).then_inc(s("ld_ffn"), 16)
            sp.dma_start(b2_sb[:, :], b2).then_inc(s("ld_ffn"), 16)
            with sp.Fori(0, NQ) as q:
                sp.wait_ge(s("mT_ready"), q + 1)
                sp.dma_start(mask_rows[bass.ds(q, 1)].rearrange("q r p -> (q r) p"), mT[:, :]
                             ).then_inc(s("m_stored"), 16)

            def load_masks(q, free):
                sp.wait_ge(s("m_stored"), q * 16 + 16)
                for pr in range(E // 2):
                    if free is not None:
                        sp.wait_ge(s("m_used"), free + pr)
                    for k in range(2):
                        e = 2 * pr + k
                        sp.dma_start(
                            mb[64 * k:64 * k + 64, pr:pr + 1, :],
                            mask_rows[bass.ds(q, 1), e * POS:(e + 1) * POS, :].rearrange("q r p -> q (r p)")
                            .partition_broadcast(64)).then_inc(s(f"m_loaded{pr}"), 16)

            sp.wait_ge(s("w1_ready"), 1)
            load_masks(0, None)
            with sp.Fori(1, NQ) as q:
                load_masks(q, q * 4 - 3)
            sp.wait_ge(s("out_done"), 16 * NQ)

        @block.tensor
        def _(pe):
            def mm(o, lhsT, rhs, start=True, stop=True):
                return nc.tensor.matmul(o, lhsT, rhs, start=start, stop=stop, skip_group_check=True)

            pe.wait_ge(s("xt_ready"), 4)
            for k in range(4):
                i = nc.tensor.transpose(PS[:, 0, k * P:(k + 1) * P], xt[:, k, :], ident)
            i.then_inc(s("xtT"), 1)
            pe.wait_ge(s("ld_tow"), 32)
            pe.wait_ge(s("lnT_ready"), 1)
            for f in range(2):
                mm(PS[:, 1 + f, :], tw[:, T_L1 + f * P:T_L1 + (f + 1) * P], lnT[:, :]).then_inc(s("mlp1"), 1)
            for f in range(2):
                pe.wait_ge(s("g1_ready"), f + 1)
                mm(PS[:, 3, :], tw[:, T_L2 + f * P:T_L2 + (f + 1) * P], g1[:, f, :], start=f == 0, stop=False)
            for k in range(4):
                i = mm(PS[:, 3, k * P:(k + 1) * P], htab[:, k, :], ident, start=False, stop=True)
            i.then_inc(s("mlp2"), 1)
            pe.wait_ge(s("gh_ready"), 1)
            mm(PS[:, 4, 0:D], cst[:, C_CEN:C_CEN + P], gh[:, :]).then_inc(s("ghc"), 1)
            pe.wait_ge(s("rt_ready"), 1)
            mm(PS[:, 4, 192:193], tw[:, T_UB:T_UB + P], tb[:, B_M2:B_M2 + 1])
            mm(PS[:, 4, 64:64 + D], fb_bc[:, :], tw[:, T_HW:T_HW + D]).then_inc(s("hb_mm"), 1)
            pe.wait_ge(s("hb_ready"), 1)
            mm(PS[:, 4, 128:128 + D], tw[:, T_BCT:T_BCT + P], rt[:, DT:TAB]).then_inc(s("bx_mm"), 1)
            pe.wait_ge(s("locb_ready"), 1)
            pe.wait_ge(s("bx_ready"), 1)
            for c in range(POS + 2):
                bank = 5 + c % 3
                if c < POS:
                    if c >= 3:
                        pe.wait_ge(s("tab_mid"), c - 2)
                    mm(PS[:, bank, 0:TAB], locdb[:, c, :, :], rt[:, :])
                    mm(PS[:, bank, TAB:TABP], locd[:, c, :, :], tw[:, T_PW:T_PW + P]).then_inc(s("tab_mm"), 1)
                if c >= 2:
                    b = c - 2
                    if b % 2 == 0:
                        pe.wait_ge(s("onehot_ready"), b // 2 + 1)
                    pe.wait_ge(s("tab_ready"), b + 1)
                    for f in range(2):
                        oh = onehot[:, b, f * HALF:(f + 1) * HALF]
                        mm(PS[:, 4 * f, :], table[:, b, TAB:TABP], oh, start=b == 0, stop=False)
                        i = mm(PS[:, 4 * f, :], table3[:, b, TAB:TABP], oh, start=False, stop=b == POS - 1)
                        if b == POS - 1:
                            i.then_inc(s("summ"), 1)

            def a_rows(q, pair, free):
                bank = rows_bank(q, pair)
                if pair >= 2:
                    pe.wait_ge(s("a_ucopy"), q * 4 + pair - 1)
                elif free is not None:
                    pe.wait_ge(s(free[0]), free[1])
                for c in (2 * pair, 2 * pair + 1):
                    o = PS[:, bank, (c % 2) * TAB:(c % 2 + 1) * TAB]
                    oh = onehot[:, c:c + 1, bass.ds(q * P, P)]
                    for part in range(3):
                        mm(o, identb[:, :], bcparts[:, part:part + 1, bass.ds(q, 1), :], start=part == 0, stop=False)
                    mm(o, oh, table[:, c, 0:TAB], start=False, stop=False)
                    i = mm(o, oh, table3[:, c, 0:TAB], start=False, stop=True)
                i.then_inc(s("a_mm"), 1)

            def chunk_adds(f):
                pe.wait_ge(s(f"h_ready{f}"), ROUNDS + 1)
                if f == 1:
                    pe.wait_ge(s("bc_ready"), 1)
                for k in range(4):
                    o = PS[:, k // 2, (k % 2) * TAB:(k % 2 + 1) * TAB]
                    i = mm(o, hT[:, f, k * P:(k + 1) * P], bx[:, :])
                i.then_inc(s("bc_mm"), 1)

            def t_first(f, k):
                pe.wait_ge(s(f"h_ready{f}"), k)
                mm(PS[:, 4 * f, :], tw[:, T_MA:T_MA + P], hT[:, f, :]).then_inc(s(f"t_self{f}"), 1)
                mm(PS[:, 4 * f + 1, :], tw[:, T_MB:T_MB + P], hT[:, f, :]).then_inc(s(f"t_nbr{f}"), 1)

            def keep_warm(bank, n):
                for _ in range(n):
                    mm(PS[:, bank, :], identb[:, :], onehot[:, 0, 0:HALF])

            t_first(0, 1)
            pe.wait_ge(s("top_ready"), 1)
            pe.wait_ge(s("ld_rows"), 32)
            for w in range(2 * ROUNDS + 1):
                x, y, rx, ry = w % 2, (w + 1) % 2, w // 2, (w - 1) // 2
                if w >= 1:
                    pe.wait_ge(s(f"t_gu{y}"), ry + 1)
                    for t in range(4):
                        i = mm(PS[:, 4 * y, t * P:(t + 1) * P], gu_sb[:, y, t * P:(t + 1) * P],
                               tw[:, T_U2:T_U2 + P], start=False, stop=True)
                    i.then_inc(s(f"t_r{y}"), 1)
                if w < 2 * ROUNDS:
                    if w == 1:
                        pe.wait_ge(s("h_ready1"), 1)
                    mm(PS[:, 4 * x + 3, :], tw[:, T_UA:T_UA + P], hT[:, x, :], start=True, stop=False)
                    pe.wait_ge(s(f"t_a{x}"), rx + 1)
                    mm(PS[:, 4 * x, :], top_row[:, :],
                       updb2_bc[:, :].rearrange("p (o n) -> p o n", o=1).broadcast_to([P, 4, DT]), start=True, stop=False)
                    for t in range(4):
                        mm(PS[:, 4 * x, t * P:(t + 1) * P], hT[:, x, t * P:(t + 1) * P], ident, start=False, stop=False)
                if w == 2 * ROUNDS:
                    pe.wait_ge(s("identb_ready"), 2)
                    pe.wait_ge(s("bc_ready"), 1)
                    a_rows(0, 0, None)
                    a_rows(0, 1, None)
                elif w >= 1:
                    keep_warm(4 * y + 3, WARM)
                if w >= 1:
                    pe.wait_ge(s(f"t_xc{y}"), 4 * ry + 4)
                    for t in range(4):
                        i = nc.tensor.transpose(PS[:, 4 * y + 1, t * P:(t + 1) * P], rtok[y][:, t, :], ident)
                    i.then_inc(s(f"t_T{y}"), 1)
                if w < 2 * ROUNDS:
                    pe.wait_ge(s(f"t_sum{x}"), rx + 1)
                    mm(PS[:, 4 * x + 2, :], tw[:, T_M2:T_M2 + P], msum[:, x, :]).then_inc(s(f"t_agg{x}"), 1)
                if w + 1 < 2 * ROUNDS:
                    t_first(y, (w + 1) // 2 + 1)
                if w < 2 * ROUNDS:
                    if w == 2 * ROUNDS - 1:
                        chunk_adds(0)
                    pe.wait_ge(s(f"t_aggs{x}"), rx + 1)
                    mm(PS[:, 4 * x + 3, :], tw[:, T_UB:T_UB + P], agg_sb[:, x, :], start=False, stop=True
                       ).then_inc(s(f"t_u{x}"), 1)
            def a_transposes(q):
                pe.wait_ge(s("a_lo"), q + 1)
                pe.wait_ge(s("a_hi"), q + 1)
                for c in range(POS):
                    i = nc.tensor.transpose(psT16[:, c * P:(c + 1) * P], xhl[:, c, :], identh[:, :])
                i.then_inc(s("a_T"), 1)

            def c_transposes(q):
                pe.wait_ge(s("c_lo"), q + 1)
                pe.wait_ge(s("c_hi"), q + 1)
                for c in range(POS):
                    i = nc.tensor.transpose(psT16[:, c * P:(c + 1) * P], xhl2[:, c, :], identh[:, :])
                i.then_inc(s("c_T"), 1)

            def c_router(q):
                pe.wait_ge(s("xs2_ready"), q + 1)
                for c in range(POS):
                    x = xs2[:, bass.ds(q * QT + c * P, P)]
                    o = PS[:, BANK_T, c * E:(c + 1) * E]
                    mm(o, x, wa_hi[:, W_R:W_R + E], start=True, stop=False)
                    i = mm(o, x, wa_lo[:, W_R:W_R + E], start=False, stop=True)
                i.then_inc(s("r_mm"), 1)

            def c_mask_transpose(q):
                pe.wait_ge(s("m_ready"), q + 1)
                nc.tensor.transpose(PS[:, BANK_T, 0:P], mtok[:, :], ident).then_inc(s("m_T"), 1)

            def b_queries_keys(q, uses):
                for u in uses:
                    w, g, half = (W_Q, W_K)[u // 4], u // 2 % 2, u % 2
                    if u >= 4:
                        pe.wait_ge(s("qk_split"), q * 8 + u - 3)
                    elif not isinstance(q, int) or q > 0:
                        pe.wait_ge(s("mask_done"), q * 16 - 3 + u)
                    x = xs1[:, half * 512:(half + 1) * 512]
                    mm(PS[:, u % 4, :], wa_hi[:, w + g * P:w + (g + 1) * P], x, start=True, stop=False)
                    mm(PS[:, u % 4, :], wa_lo[:, w + g * P:w + (g + 1) * P], x, start=False, stop=True
                       ).then_inc(s("qk_mm"), 1)

            def b_values(q):
                pe.wait_ge(s("a_ucopy"), q * 4 + 8 if not isinstance(q, int) else min(q * 4 + 8, 4 * NQ))
                for n in range(8):
                    o = PS[:, BANK_Q, n * D:(n + 1) * D]
                    x = xs1[:, n * CH:(n + 1) * CH]
                    mm(o, x, wa_hi[:, W_V:W_V + D], start=True, stop=False)
                    i = mm(o, x, wa_lo[:, W_V:W_V + D], start=False, stop=True)
                i.then_inc(s("v_mm"), 1)
                for b in range(4):
                    o = PS[:, BANK_A, b * D:(b + 1) * D]
                    x = xs1[:, 2 * b * CH:(2 * b + 1) * CH]
                    mm(o, x, wa_hi[:, W_KC:W_KC + D], start=True, stop=False)
                    i = mm(o, x, wa_lo[:, W_KC:W_KC + D], start=False, stop=True)
                i.then_inc(s("ktok_mm"), 1)

            def b_chunk_queries(q):
                x = xs1[:, :].rearrange("p (b a n) -> p b a n", b=4, a=2)[:, :, 1, :]
                mm(PS[0:D, BANK_T, :], wa_hi[:, W_QC:W_QC + D], x, start=True, stop=False)
                mm(PS[0:D, BANK_T, :], wa_lo[:, W_QC:W_QC + D], x, start=False, stop=True).then_inc(s("qc_mm"), 1)

            def b_state(q):
                pe.wait_ge(s("ktok_ready"), q + 1)
                pe.wait_ge(s("vdec_ready"), q + 1)
                for b in range(4):
                    i = mm(PS[0:D, BANK_A, 256 + b * D:256 + (b + 1) * D], ktok[:, b, :], vdec[:, b, :])
                i.then_inc(s("kv_mm"), 1)

            def b_scores(q, n):
                b = n // 2
                for j in (2 * (n % 2), 2 * (n % 2) + 1):
                    if not isinstance(q, int) or 16 * q + 4 * b + j - 3 > 0:
                        pe.wait_ge(s("mask_done"), q * 16 + 4 * b + j - 3)
                    for a in range(2):
                        chunk = slice((2 * b + a) * CH, (2 * b + a + 1) * CH)
                        for g in range(2):
                            i = mm(PS[:, j, (2 * a + g) * CH:(2 * a + g + 1) * CH],
                                   k32[32 * j:32 * j + 32, g, chunk], q32[32 * j:32 * j + 32, g, chunk])
                    i.then_inc(s("scores"), 1)

            def b_outputs(q, b):
                pe.wait_ge(s("mask_done"), q * 16 + 4 * b + 4)
                if b == 0:
                    pe.wait_ge(s("sbd_ready"), q + 1)
                    pe.wait_ge(s("qdec_ready"), q + 1)
                cols = slice(b * CH, (b + 1) * CH)
                mm(PS[64:128, BANK_O, cols], sbd[:, b, :], qdec[:, b, :], start=True, stop=False)
                for j in range(4):
                    for a in range(2):
                        for g in range(2):
                            n = 2 * b + a
                            r0 = 64 * a + 32 * g
                            i = mm(PS[r0:r0 + 32, BANK_O, cols], vx[:, n, g, 32 * j:32 * j + 32],
                                   probs[:, b % 2, j, (2 * a + g) * CH:(2 * a + g + 1) * CH],
                                   start=(a == 0 and j == 0), stop=j == 3)
                i.then_inc(s("pv_done"), 1)

            def b_project(q):
                pe.wait_ge(s("olo_ready"), q * 2 + 2)
                for c in range(POS):
                    o = PS[:, BANK_O, c * D:(c + 1) * D]
                    x = ostk[:, c:QT:POS]
                    mm(o, x, wa_hi[:, W_P:W_P + D], start=True, stop=False)
                    i = mm(o, x, wa_lo[:, W_P:W_P + D], start=False, stop=True)
                i.then_inc(s("proj_mm"), 1)

            def quad(q, has_n, has_a, has_c):
                pe.wait_ge(s("qk_split"), q * 8 + 8)
                for n in range(8):
                    if n == 0:
                        b_scores(q, 0)
                    if n < 7:
                        b_scores(q, n + 1)
                    if n == 0:
                        b_state(q)
                    if n == 4 and has_a:
                        a_rows(q + 2, 3, None)
                    if n in (2, 4, 6):
                        b_outputs(q, n // 2 - 1)
                    if n == 1 and has_a:
                        a_rows(q + 2, 0, ("sbd_ready", q + 1))
                        a_rows(q + 2, 1, ("vdec_ready", q + 1))
                    if n == 1:
                        pe.wait_ge(s("qdec_ready"), q + 1)
                        if has_n:
                            a_transposes(q + 1)
                    if n == 3 and has_a:
                        a_rows(q + 2, 2, None)
                    if n == 4 and has_c:
                        if has_n:
                            pe.wait_ge(s("xs1_ready"), q + 2)
                        c_transposes(q - 1)
                    if n == 5 and has_c:
                        c_router(q - 1)
                if has_n:
                    pe.wait_ge(s("xs1_ready"), q + 2)
                    b_queries_keys(q + 1, (0, 1, 2, 3))
                b_outputs(q, 3)
                if has_n:
                    b_queries_keys(q + 1, (4, 5, 6, 7))
                    b_values(q + 1)
                if has_c and has_n:
                    pe.wait_ge(s("r_log"), q)
                    c_mask_transpose(q - 1)
                b_project(q)
                if has_n:
                    if has_c:
                        pe.wait_ge(s("mT_ready"), q)
                    b_chunk_queries(q + 1)

            a_rows(0, 2, None)
            a_rows(0, 3, None)
            chunk_adds(1)
            for pair in range(4):
                a_rows(1, pair, None)
            a_transposes(0)
            pe.wait_ge(s("bc_ready"), 2)
            pe.wait_ge(s("wa_ready"), 1)
            pe.wait_ge(s("zero_ready"), 5)
            pe.wait_ge(s("xs1_ready"), 1)
            b_queries_keys(0, range(8))
            b_values(0)
            b_chunk_queries(0)
            quad(0, True, True, False)
            with pe.Fori(1, NQ - 2) as q:
                quad(q, True, True, True)
            quad(NQ - 2, True, False, True)
            quad(NQ - 1, False, False, True)
            def l1(q, t):
                if not isinstance(q, int) or q > 0 or t >= 2:
                    pe.wait_ge(s("gelu_done"), q * NT1 + t - 1)
                for w, first in ((w1_hi, True), (w1_lo, False)):
                    for half in range(2):
                        i = mm(PS[:, 2 * (t % 2) + half, :], w[:, t, :],
                               xs2[:, bass.ds(q * QT + half * 512, 512)], start=first, stop=not first)
                i.then_inc(s("l1_done"), 1)

            def l2(q, u):
                unit = (u + 1) // 2
                first = u == 0 or u % 2 == 1
                last = u % 2 == 0
                banks = BANK_Q - 2 * (unit % 2)
                if first:
                    need = {0: 0, 1: -1, 2: 1, 3: 2, 4: 3}[unit]
                    if not isinstance(q, int) or 5 * q + need > 0:
                        pe.wait_ge(s("y_used"), q * 5 + need)
                    if unit == 2 and (not isinstance(q, int) or q > 0):
                        pe.wait_ge(s("f_used"), q)
                if u % 2 == 0 and u // 2 < SPLITS:
                    pe.wait_ge(s("hid_lo"), q * 2 * SPLITS + u + 2)
                    parts = [(w, low) for w, low in ((w2_hi, 0), (w2_lo, 0), (w2_hi, 1))]
                    for n, (w, low) in enumerate(parts):
                        for half in range(2):
                            for k in range(2):
                                i = mm(PS[64 * k:64 * k + 64, banks + half, :], w[:, u // 2, k, :],
                                       hidden_part(u // 2, k, low)[:, half * 512:(half + 1) * 512],
                                       start=first and n == 0, stop=last and n == 2)
                else:
                    pe.wait_ge(s("gelu_done"), q * NT1 + 2 * u + 2)
                    for half in range(2):
                        for k in range(2):
                            i = mm(PS[64 * k:64 * k + 64, banks + half, :], w2_sb[:, 2 * u + k, :],
                                   gring[:, (2 * u + k) % GR, half * 512:(half + 1) * 512], start=first, stop=last)
                i.then_inc(s("l2_done"), 1)

            def fold(q):
                pe.wait_ge(s("ylo_ready"), q + 1)
                for c in range(POS):
                    o = PS[:, BANK_Q, c * D:(c + 1) * D]
                    mm(o, y_hi[:, c * P:(c + 1) * P], pair_sum[:, :], start=True, stop=False)
                    i = mm(o, y_lo[:, c * P:(c + 1) * P], pair_sum[:, :], start=False, stop=True)
                i.then_inc(s("f_mm"), 1)

            def l1_ahead(q, u, has_next):
                n = u + 2
                if n < NT1 // 2:
                    l1(q, 2 * n)
                    l1(q, 2 * n + 1)
                elif has_next:
                    l1(q + 1, 2 * n - NT1)
                    l1(q + 1, 2 * n - NT1 + 1)

            def ffn(q, has_fold, has_next):
                for u in range(NT1 // 2):
                    l1_ahead(q, u, has_next)
                    l2(q, u)
                    if u == 1 and has_fold:
                        pe.wait_ge(s("y_used"), q * 5 + 1)
                        fold(q - 1)

            pe.wait_ge(s("w1_ready"), 1)
            pe.wait_ge(s("mask_done"), 16 * NQ)
            l1(0, 0)
            l1(0, 1)
            pe.wait_ge(s("r_log"), NQ - 1)
            c_mask_transpose(NQ - 2)
            pe.wait_ge(s("mT_ready"), NQ - 1)
            c_transposes(NQ - 1)
            l1(0, 2)
            c_router(NQ - 1)
            l1(0, 3)
            pe.wait_ge(s("w2_ready"), 1)
            pe.wait_ge(s("h2_done"), NQ)
            l2(0, 0)
            for t in range(4, 8):
                l1(0, t)
            pe.wait_ge(s("r_log"), NQ)
            c_mask_transpose(NQ - 1)
            pe.wait_ge(s("mT_ready"), NQ)
            l2(0, 1)
            for u in range(2, NT1 // 2):
                l1_ahead(0, u, True)
                l2(0, u)
            with pe.Fori(1, NQ - 1) as q:
                ffn(q, True, True)
            ffn(NQ - 1, True, False)
            pe.wait_ge(s("y_used"), 5 * NQ)
            fold(NQ - 1)

        @block.scalar
        def _(act):
            def a(o, i, f=ACT.Identity, **kw):
                return nc.scalar.activation(o, i, f, **kw)

            act.dma_start(cst[:, :], consts).then_inc(s("ld_cst"), 16)
            act.dma_start(slope_bc[:, :], slopes.partition_broadcast(P)).then_inc(s("ld_slope"), 16)
            act.dma_start(slope_col[:, :], bass.AP(tensor=slopes.tensor, offset=slopes.offset,
                                                   ap=[[1, H], [0, DH], [1, 1]])).then_inc(s("ld_slope"), 16)
            act.dma_start(tb[:, :], towerb).then_inc(s("ld_tow"), 16)
            act.dma_start(tw[:, :], towerw).then_inc(s("ld_tow"), 16)
            act.wait_ge(s("slope_ready"), 2)
            for j in range(4):
                for g in range(2):
                    a(decay[:, j, g, :], cst[:, C_DIFF:C_DIFF + P], ACT.Exp,
                      scale=neg_slope[:, 4 * g + j:4 * g + j + 1]).then_inc(s("decay_raw"), 1)
            a(kdec[:, :], slope_row[:, :, :], ACT.Exp, scale=cst[:, C_COL + 4:C_COL + 5]).then_inc(s("kdec_ready"), 1)
            a(dec[:, :], cst[0:D, C_NEGC:C_NEGC + CH], ACT.Exp, scale=slope_col[:, :]).then_inc(s("dec_raw"), 1)
            act.wait_ge(s("ld_tow"), 32)
            act.wait_ge(s("xtT"), 1)
            a(lnT[:, :], PS[:, 0, :], bias=tb[:, B_LB:B_LB + 1], scale=tb[:, B_LG:B_LG + 1]).then_inc(s("lnT_ready"), 1)
            for f in range(2):
                act.wait_ge(s("mlp1"), f + 1)
                a(g1[:, f, :], PS[:, 1 + f, :], ACT.Gelu, bias=tb[:, B_L1 + f:B_L1 + f + 1]).then_inc(s("g1_ready"), 1)
            act.wait_ge(s("mlp2"), 1)
            a(locd[:, :, :, :], PS[:, 3, :].rearrange("p (c o v) -> p c o v", o=1, v=VOCAB)
              .broadcast_to([P, POS, 2, VOCAB]), bias=tb[:, B_L2:B_L2 + 1]).then_inc(s("loc_ready"), 1)
            act.wait_ge(s("ghc"), 1)
            a(rt[:, DT:TAB], PS[:, 4, 0:D]).then_inc(s("rt_ready"), 1)
            act.wait_ge(s("hb_mm"), 1)
            a(updb1_all[:, :], PS[:, 4, 192:193], bias=tb[:, B_U1:B_U1 + 1]).then_inc(s("updb1_ready"), 1)
            a(hb[:, :], PS[:, 4, 64:64 + D]).then_inc(s("hb_ready"), 1)
            act.wait_ge(s("bx_mm"), 1)
            a(bx[:, DT:TAB], PS[:, 4, 128:128 + D]).then_inc(s("bx_ready"), 1)
            for c in range(POS):
                act.wait_ge(s("tab_mm"), c + 1)
                if c >= 2:
                    act.wait_ge(s("tab_mid"), c - 1)
                a(tab_top[:, c % 2, :], PS[:, 5 + c % 3, 0:TABP], ACT.Copy).then_inc(s("tab_hi"), 1)
            for f in range(2):
                act.wait_ge(s("summ"), f + 1)
                a(hT[:, f, :], PS[:, 4 * f, :], bias=tb[:, B_PB:B_PB + 1], scale=1.0 / POS
                  ).then_inc(s(f"h_ready{f}"), 1)
            def a_copies(q, pairs):
                for c2 in pairs:
                    act.wait_ge(s("a_stat"), q * 4 + c2 + 1)
                    if c2 == 0 and (not isinstance(q, int) or q > 0):
                        act.wait_ge(s("a_u_used"), q)
                    src = PS[:, rows_bank(q, c2), 0:2 * TAB].rearrange("p (c n) -> p c n", c=2)[:, :, DT:TAB]
                    a(u_sb[:, 2 * c2:2 * c2 + 2, :], src, ACT.Copy).then_inc(s("a_ucopy"), 1)

            def chunk_high(f):
                act.wait_ge(s("bc_mm"), f + 1)
                a(bcparts[:, 0, 4 * f:4 * f + 4, :].rearrange("p (k a) n -> p k (a n)", k=2),
                  PS[:, 0:2, 0:2 * TAB], ACT.Copy).then_inc(s("bc_hi"), 1)

            act.wait_ge(s("updb1_ready"), 1)
            for w in range(2 * ROUNDS + 1):
                x, y, rx, ry = w % 2, (w + 1) % 2, w // 2, (w - 1) // 2
                if w == 2 * ROUNDS:
                    chunk_high(0)
                if w < 2 * ROUNDS:
                    act.wait_ge(s(f"t_self{x}"), rx + 1)
                    a(a_sb[:, x, :], PS[:, 4 * x, :], bias=tb[:, B_M1:B_M1 + 1]).then_inc(s(f"t_a{x}"), 1)
                if w >= 1:
                    act.wait_ge(s(f"t_u{y}"), ry + 1)
                    a(gu_sb[:, y, :], PS[:, 4 * y + 3, :], ACT.Gelu, bias=updb1_all[:, :]).then_inc(s(f"t_gu{y}"), 1)
                if w < 2 * ROUNDS:
                    for d in range(WIN + 1):
                        act.wait_ge(s(f"t_pre{x}"), 5 * rx + d + 1)
                        v = pre[:, x, d, :].rearrange("p (b n) -> p b n", b=HB)[:, :, d:CPB]
                        a(v, v, ACT.Gelu).then_inc(s(f"t_g{x}"), 1)
                if w == 2 * ROUNDS:
                    a_copies(0, (0, 1))
                if w >= 1:
                    act.wait_ge(s(f"t_T{y}"), ry + 1)
                    a(hT[:, y, :], PS[:, 4 * y + 1, :], bias=tb[:, B_MB:B_MB + 1], scale=tb[:, B_MG:B_MG + 1]
                      ).then_inc(s(f"h_ready{y}"), 1)
            def a_high(q):
                act.wait_ge(s("a_xn"), q + 1)
                if not isinstance(q, int) or q > 0:
                    act.wait_ge(s("a_T"), q)
                a(xhl[:, :, 0:D], xn[:, :, :], ACT.Copy).then_inc(s("a_hi"), 1)

            def a_evacuate(q):
                act.wait_ge(s("a_T"), q + 1)
                if not isinstance(q, int) or q > 0:
                    act.wait_ge(s("qc_mm"), q)
                    act.wait_ge(s("ktok_mm"), q)
                a(xs1[:, :].rearrange("p (n c) -> p c n", c=POS), psT16.rearrange("p (c n) -> p c n", c=POS),
                  ACT.Copy).then_inc(s("xs1_ready"), 1)

            def c_high(q):
                act.wait_ge(s("c_xn"), q + 1)
                if not isinstance(q, int) or q > 0:
                    act.wait_ge(s("c_T"), q)
                a(xhl2[:, :, 0:D], xn2[:, :, :], ACT.Copy).then_inc(s("c_hi"), 1)

            def c_evacuate(q):
                act.wait_ge(s("c_T"), q + 1)
                a(xs2[:, bass.ds(q * QT, QT)], psT16, ACT.Copy).then_inc(s("xs2_ready"), 1)

            def c_exp(q):
                act.wait_ge(s("r_log"), q + 1)
                a(rexp[:, :, :], rlog[:, :, :], ACT.Exp, scale=1.0 / SW).then_inc(s("r_exp"), 1)

            def c_mask_copy(q):
                act.wait_ge(s("m_T"), q + 1)
                if not isinstance(q, int) or q > 0:
                    act.wait_ge(s("m_stored"), q * 16)
                a(mT[:, :], PS[0:D, BANK_T, 0:P], ACT.Copy).then_inc(s("mT_ready"), 1)

            def b_high(q, uses):
                for u in uses:
                    act.wait_ge(s("qk_mm"), q * 8 + u + 1)
                    if not isinstance(q, int) or q > 0 or u >= 4:
                        act.wait_ge(s("qk_split"), q * 8 + u - 3)
                    a(qk_hi[:, u % 4, :], PS[:, u % 4, :], ACT.Copy).then_inc(s("qk_hi_ready"), 1)

            def b_value_copies(q):
                act.wait_ge(s("v_mm"), q + 1)
                if not isinstance(q, int) or q > 0:
                    act.wait_ge(s("pv_done"), q * 4)
                pv = PS[:, BANK_Q, :].rearrange("p (n g j d) -> p n g j d", n=8, g=2, j=4)
                for g in range(2):
                    a(vx[:, :, g, :].rearrange("p n (j w) -> p n j w", w=40)[:, :, :, 0:DH], pv[:, :, g, :, :],
                      ACT.Copy).then_inc(s("vx_ready"), 1)
                act.wait_ge(s("ktok_mm"), q + 1)
                a(ktok[:, :, :], PS[:, BANK_A, 0:4 * D].rearrange("p (b n) -> p b n", b=4), ACT.Copy
                  ).then_inc(s("ktok_ready"), 1)

            def b_output_high(q):
                act.wait_ge(s("pv_done"), q * 4 + 4)
                if not isinstance(q, int) or q > 0:
                    act.wait_ge(s("proj_mm"), q)
                for k in range(2):
                    a(ostk[0:D, :].rearrange("p (b a n) -> p b a n", b=4, a=2)[:, :, k, :],
                      PS[64 * k:64 * k + 64, BANK_O, :].rearrange("p (b n) -> p b n", b=4), ACT.Copy
                      ).then_inc(s("ohi_ready"), 1)

            def quad(q, has_n, has_a, has_c):
                for n in range(8):
                    if n == 0 and has_n:
                        a_high(q + 1)
                    if n == 1 and has_n:
                        a_evacuate(q + 1)
                    if n == 2 and has_c:
                        c_high(q - 1)
                    if n == 2 and has_a:
                        a_copies(q + 2, (0,))
                    if n == 3 and has_a:
                        a_copies(q + 2, (1,))
                    if n in (4, 5) and has_a:
                        a_copies(q + 2, (n - 2,))
                    if n == 4 and has_c:
                        c_evacuate(q - 1)
                    if n == 6 and has_c:
                        c_exp(q - 1)
                if has_n:
                    b_high(q + 1, (0, 1, 2, 3))
                b_output_high(q)
                if has_n:
                    b_high(q + 1, (4, 5, 6, 7))
                if has_c and has_n:
                    c_mask_copy(q - 1)
                if has_n:
                    b_value_copies(q + 1)

            a_copies(0, (2, 3))
            chunk_high(1)
            a_copies(1, (0, 1, 2, 3))
            a_high(0)
            a_evacuate(0)
            b_high(0, range(8))
            b_value_copies(0)
            quad(0, True, True, False)
            with act.Fori(1, NQ - 2) as q:
                quad(q, True, True, True)
            quad(NQ - 2, True, False, True)
            quad(NQ - 1, False, False, True)
            def store(q):
                act.wait_ge(s("f_used"), q + 1)
                act.dma_start(out_v[bass.ds(q * P, P), :], obuf[:, :]).then_inc(s("out_done"), 16)

            def gelu(q, t):
                act.wait_ge(s("l1_done"), q * NT1 + t + 1)
                if not isinstance(q, int) or 9 * q + t // 2 - 2 > 0:
                    act.wait_ge(s("l2_done"), q * 9 + t // 2 - 2)
                a(gring[:, t % GR, :], PS[:, 2 * (t % 2):2 * (t % 2) + 2, :], ACT.Gelu,
                  bias=b1_sb[:, t:t + 1], scale=1.0 / SW).then_inc(s("gelu_done"), 1)

            def hidden_high(q, i):
                for k in range(2):
                    t = 4 * i + k
                    act.wait_ge(s("gelu_done"), q * NT1 + t + 1)
                    a(hidden_part(i, k, 0), gring[:, t % GR, :], ACT.Copy, scale=SH).then_inc(s("hid_hi"), 1)

            def ffn(q, first, has_fold):
                for t in range(first, NT1):
                    gelu(q, t)
                    if t % 4 == 1 and t // 4 < SPLITS:
                        hidden_high(q, t // 4)
                    if t == 8 and has_fold:
                        store(q - 1)

            act.wait_ge(s("ld_ffn"), 48)
            act.wait_ge(s("pv_done"), 4 * NQ)
            gelu(0, 0)
            gelu(0, 1)
            c_mask_copy(NQ - 2)
            c_high(NQ - 1)
            hidden_high(0, 0)
            c_evacuate(NQ - 1)
            c_exp(NQ - 1)
            for t in range(2, 8):
                gelu(0, t)
                if t == 5:
                    hidden_high(0, 1)
            c_mask_copy(NQ - 1)
            ffn(0, 8, False)
            with act.Fori(1, NQ) as q:
                ffn(q, 0, True)
            store(NQ - 1)

        @block.vector
        def _(dve):
            v = nc.vector
            ch = Steps(dve, s("dve_step"))
            tt = v.tensor_tensor

            def stats_tail(n, key, width):
                e, x = st[key], stx[key]
                ch.step(tt(x[:, 0, 0:n], e[:, 0:n, 1], e[:, 0:n, 4], ALU.subtract))
                ch.step(tt(x[:, 1:3, 0:n], e[:, 0:n, 1:3].rearrange("p n k -> p k n"),
                           e[:, 0:n, 4:6].rearrange("p n k -> p k n"), ALU.add))
                ch.settle()
                ch.step(tt(x[:, 3, 0:n], x[:, 0, 0:n], x[:, 0, 0:n], ALU.mult))
                if key != "f":
                    ch.step(v.tensor_scalar(x[:, 5, 0:n], x[:, 1, 0:n], 0.5, None, ALU.mult))
                ch.settle()
                ch.step(v.scalar_tensor_tensor(x[:, 0, 0:n], x[:, 3, 0:n], width / 4.0, x[:, 2, 0:n],
                                               ALU.mult, ALU.add))
                ch.settle()
                v.tensor_scalar(x[:, 4, 0:n], x[:, 0, 0:n], 1.0 / width, EPS, ALU.mult, ALU.add
                                ).then_inc(s("stats_" + key), 1)

            dve.wait_ge(s("ld_cst"), 16)
            v.tensor_copy(identb[:, :], ident).then_inc(s("identb_ready"), 1)
            v.tensor_copy(identh[:, :], ident).then_inc(s("identb_ready"), 1)
            dve.wait_ge(s("ld_slope"), 32)
            v.tensor_copy(slope_row[:, :, :], slope_bc[:, :].rearrange("p (h o) -> p h o", o=1)
                          .broadcast_to([P, H, DH])).then_inc(s("slope_ready"), 1)
            v.tensor_scalar(neg_slope[:, :], slope_bc[:, :], -1.0, None, ALU.mult).then_inc(s("slope_ready"), 1)
            v.tensor_copy(rt[:, 0:DT], ident).then_inc(s("rt_id"), 1)
            v.tensor_copy(pair_sum[:, :], cst[:, C_II:C_II + D]).then_inc(s("zero_ready"), 1)
            dve.wait_ge(s("ld_emb"), 64)
            for k in range(4):
                tt(htab[:, k, :], embt[:, :], postab[:, k, :], ALU.add).then_inc(s("htab_ready"), 1)
            dve.wait_ge(s("htab_ready"), 4)
            for k in range(4):
                ch.step(v.bn_stats(st["t"][:, k, :], htab[:, k, :]))
            ch.settle()
            stats_tail(4, "t", DT)
            dve.wait_ge(s("rstd_t"), 1)
            for k in range(4):
                v.tensor_scalar(xt[:, k, :], htab[:, k, :], stx["t"][:, 5, k:k + 1], rstd["t"][:, k:k + 1],
                                ALU.subtract, ALU.mult).then_inc(s("xt_ready"), 1)
            dve.wait_ge(s("ld_tow"), 32)
            ch.step(v.tensor_copy(fb_bc[:, :], tb[:, B_FB:B_FB + 1].broadcast_to([P, P])))
            ch.step(v.tensor_copy(bx[:, 0:DT], tw[:, T_BC:T_BC + DT]))
            ch.settle()
            v.tensor_scalar(gh[:, :], tw[:, T_HW:T_HW + D], tb[:, B_FG:B_FG + 1], None, ALU.mult
                            ).then_inc(s("gh_ready"), 1)
            for k in range(4):
                if k == ONEHOTS_FIRST:
                    dve.wait_ge(s("loc_ready"), 1)
                    v.tensor_scalar(locdb[:, :, :, :], locd[:, :, :, :], tb[:, B_BC:B_BC + 1], None, ALU.add
                                    ).then_inc(s("locb_ready"), 1)
                dve.wait_ge(s(f"ld_ids{k}"), 16)
                v.tensor_scalar(onehot[:, 2 * k:2 * k + 2, :], ids_stage[:, k % 3, :],
                                cst[:, C_COL:C_COL + 1], None, ALU.is_equal).then_inc(s("onehot_ready"), 1)
            for c in range(POS):
                dve.wait_ge(s("tab_hi"), c + 1)
                top, acc = tab_top[:, c % 2, :], PS[:, 5 + c % 3, 0:TABP]
                ch.step(v.scalar_tensor_tensor(table[:, c, :], top, cst[:, C_COL + 3:C_COL + 4], acc,
                                               ALU.mult, ALU.add))
                if c >= 2:
                    dve.wait_ge(s("tab_ready"), c - 1)
                tt(tab_rest[:, c % 2, :], acc, top, ALU.subtract).then_inc(s("tab_mid"), 1)
            dve.wait_ge(s("decay_raw"), 8)
            tt(decay[:, :, :, :].rearrange("p j g c -> p (j g) c"), decay[:, :, :, :].rearrange("p j g c -> p (j g) c"),
               cst[:, C_CAUS:C_CAUS + CH].rearrange("p (o c) -> p o c", o=1).broadcast_to([P, H, CH]), ALU.mult
               ).then_inc(s("decay_ready"), 1)
            dve.wait_ge(s("dec_raw"), 1)
            v.tensor_scalar(dec[:, :], dec[:, :], DH ** -0.5 / SW ** 2, None, ALU.mult).then_inc(s("decay_ready"), 1)
            inv = cst[:, C_INV:C_INV + CPB].rearrange("p (o n) -> p o n", o=1).broadcast_to([P, HB, CPB])

            def seqs(x):
                return x.rearrange("p (b n) -> p b n", b=HB)

            for f in range(2):
                for d in range(1, WIN + 1):
                    ch.step(v.memset(seqs(pre[:, f, d, :])[:, :, 0:d], 0.0))
            def messages(f, r, lags):
                for d in lags:
                    if d == 0:
                        dve.wait_ge(s(f"t_nbr{f}"), r + 1)
                        dve.wait_ge(s(f"t_a{f}"), r + 1)
                    tt(seqs(pre[:, f, d, :])[:, :, d:CPB], seqs(PS[:, 4 * f + 1, :])[:, :, 0:CPB - d],
                       seqs(a_sb[:, f, :])[:, :, d:CPB], ALU.add).then_inc(s(f"t_pre{f}"), 1)

            def message_sum(f, r):
                dve.wait_ge(s(f"t_g{f}"), 5 * r + 5)
                ch.step(tt(msum[:, f, :], pre[:, f, 3, :], pre[:, f, 4, :], ALU.add))
                ch.settle()
                dve.wait_ge(s(f"t_p{f}"), 2 * r + 2)
                tt(msum[:, f, :], msum[:, f, :], pre[:, f, 0, :], ALU.add).then_inc(s(f"t_sum{f}"), 1)

            def a_stats(q, pairs):
                for c2 in pairs:
                    dve.wait_ge(s("a_mm"), q * 4 + c2 + 1)
                    for c in (2 * c2, 2 * c2 + 1):
                        bank = rows_bank(q, c2)
                        i = v.bn_stats(st["f"][:, c, :], PS[:, bank, (c % 2) * TAB:(c % 2) * TAB + DT])
                        if c % 2 == 0:
                            ch.step(i)
                    i.then_inc(s("a_stat"), 1)
                if pairs[-1] == 3:
                    dve.wait_ge(s("a_stat"), q * 4 + 4)
                    if not isinstance(q, int) or q > 0:
                        dve.wait_ge(s("rstd_f"), q)
                    stats_tail(8, "f", DT)

            rest = bc_rest.rearrange("p (k n) -> p k n", k=2)

            def bc_split(f):
                dve.wait_ge(s("bc_hi"), f + 1)
                parts = [bcparts[:, k, 4 * f:4 * f + 4, :].rearrange("p (k a) n -> p k (a n)", k=2) for k in range(3)]
                ch.step(tt(rest, PS[:, 0:2, 0:2 * TAB], parts[0], ALU.subtract))
                ch.settle()
                ch.step(v.tensor_copy(parts[1], rest))
                ch.settle()
                tt(parts[2], rest, parts[1], ALU.subtract).then_inc(s("bc_ready"), 1)
                dve.wait_ge(s("bc_ready"), f + 1)

            for w in range(2 * ROUNDS + 1):
                x, y, rx, ry = w % 2, (w + 1) % 2, w // 2, (w - 1) // 2
                key = "tu"[y]
                if w >= 1:
                    dve.wait_ge(s(f"t_agg{y}"), ry + 1)
                    tt(seqs(agg_sb[:, y, :]), seqs(PS[:, 4 * y + 2, :]), inv, ALU.mult).then_inc(s(f"t_aggs{y}"), 1)
                if w < 2 * ROUNDS:
                    messages(x, rx, (0, 1, 2))
                else:
                    bc_split(0)
                if w >= 1:
                    dve.wait_ge(s(f"t_r{y}"), ry + 1)
                    for t in range(4):
                        ch.step(v.bn_stats(st[key][:, t, :], PS[:, 4 * y, t * P:(t + 1) * P]))
                    ch.settle()
                    stats_tail(4, key, DT)
                if w < 2 * ROUNDS:
                    messages(x, rx, (3, 4))
                else:
                    a_stats(0, (0, 1))
                if w >= 1:
                    dve.wait_ge(s("rstd_" + key), ry + 1 + (y == 0))
                    for t in range(4):
                        v.tensor_scalar(rtok[y][:, t, :], PS[:, 4 * y, t * P:(t + 1) * P], stx[key][:, 5, t:t + 1],
                                        rstd[key][:, t:t + 1], ALU.subtract, ALU.mult).then_inc(s(f"t_xc{y}"), 1)
                if w < 2 * ROUNDS:
                    message_sum(x, rx)

            dve.wait_ge(s("kdec_ready"), 1)

            def bc_d(x, width):
                return x.rearrange("p (c o) -> p c o", o=1).broadcast_to([P, POS, width])

            def a_hidden_stats(q):
                dve.wait_ge(s("a_h"), q + 1)
                for c in (1, 2, 3, 4, 5, 6, 7, 0):
                    ch.step(v.bn_stats(st["a"][:, c, :], h_res[:, bass.ds(q * POS * D + c * D, D)]))
                ch.settle()
                stats_tail(8, "a", D)

            def c_stats(q):
                if not isinstance(q, int) or q >= 0:
                    dve.wait_ge(s("h2_done"), q + 1)
                for c in (1, 2, 3, 4, 5, 6, 7, 0):
                    ch.step(v.bn_stats(st["c"][:, c, :], h_res[:, bass.ds(q * POS * D + c * D, D)]))
                ch.settle()
                stats_tail(8, "c", D)

            def c_logits(q):
                dve.wait_ge(s("r_mm"), q + 1)
                ps = PS[:, BANK_T, 0:POS * E].rearrange("p (c e) -> p c e", c=POS)
                ch.step(v.tensor_reduce(rmax[:, 0, :], ps, op=ALU.max, axis=AX_X))
                ch.settle()
                tt(rlog[:, :, :], ps, bc_d(rmax[:, 0, :], E), ALU.subtract).then_inc(s("r_log"), 1)

            def c_top2(q):
                dve.wait_ge(s("r_exp"), q + 1)
                ch.step(v.tensor_reduce(rmax[:, 1, :], rexp[:, :, :], op=ALU.add, axis=AX_X))
                ch.settle()
                ch.step(v.reciprocal(rmax[:, 2, :], rmax[:, 1, :]))
                ch.settle()
                ch.step(tt(rw[:, :, :], rexp[:, :, :], bc_d(rmax[:, 2, :], E), ALU.mult))
                ch.settle()
                wj = rw[:, :, :].rearrange("p c (o j) -> p c o j", o=1).broadcast_to([P, POS, E, E])
                we = rw[:, :, :].rearrange("p c (e o) -> p c e o", o=1).broadcast_to([P, POS, E, E])
                tt(rge[:, :, :, :], wj, we, ALU.is_ge).then_inc(s("r_ge"), 1)

            def c_top2_rest(q):
                dve.wait_ge(s("r_df"), q + 1)
                ch.step(v.tensor_reduce(rank[:, :, :], rdf[:, :, :, :], op=ALU.add, axis=AX_X))
                ch.settle()
                thr = cst[:, C_THR:C_THR + E].rearrange("p (o n) -> p o n", o=1).broadcast_to([P, POS, E])
                ch.step(tt(rank[:, :, :], rank[:, :, :], thr, ALU.is_lt))
                ch.settle()
                ch.step(tt(rw[:, :, :], rw[:, :, :], rank[:, :, :], ALU.mult))
                ch.settle()
                ch.step(v.tensor_reduce(rmax[:, 1, :], rw[:, :, :], op=ALU.add, axis=AX_X))
                ch.settle()
                ch.step(v.reciprocal(rmax[:, 3, :], rmax[:, 1, :]))
                ch.settle()
                if not isinstance(q, int) or q > 0:
                    dve.wait_ge(s("m_T"), q)
                tt(mtok[:, 0:POS * E].rearrange("p (e c) -> p c e", e=E), rw[:, :, :], bc_d(rmax[:, 3, :], E),
                   ALU.mult).then_inc(s("m_ready"), 1)

            def b_split(q, uses):
                for u in uses:
                    dst, g, half = (q32, k32)[u // 4], u // 2 % 2, u % 2
                    dve.wait_ge(s("qk_hi_ready"), q * 8 + u + 1)
                    if u == 0 and (not isinstance(q, int) or q > 0):
                        dve.wait_ge(s("scores"), q * 16)
                    v.scalar_tensor_tensor(
                        dst[:, g, half * 512:(half + 1) * 512], qk_hi[:, u % 4, :],
                        cst[:, C_COL + 1 + u // 4:C_COL + 2 + u // 4], PS[:, u % 4, :], ALU.mult, ALU.add
                    ).then_inc(s("qk_split"), 1)

            def b_decayed_values(q):
                dve.wait_ge(s("vx_ready"), q * 2 + 2)
                if not isinstance(q, int) or q > 0:
                    dve.wait_ge(s("kv_mm"), q)
                pv = PS[:, BANK_Q, :].rearrange("p (b a n) -> p b a n", b=4, a=2)[:, :, 0, :]
                tt(vdec[:, :, :], pv, kdec[:, :].rearrange("p (o n) -> p o n", o=1).broadcast_to([P, 4, D]),
                   ALU.mult).then_inc(s("vdec_ready"), 1)

            def b_decayed_queries(q):
                dve.wait_ge(s("qc_mm"), q + 1)
                if not isinstance(q, int) or q > 0:
                    dve.wait_ge(s("pv_done"), q * 4)
                tt(qdec[0:D, :, :], PS[0:D, BANK_T, :].rearrange("p (b n) -> p b n", b=4),
                   dec[:, :].rearrange("p (o n) -> p o n", o=1).broadcast_to([D, 4, CH]), ALU.mult
                   ).then_inc(s("qdec_ready"), 1)

            def b_masked_state(q):
                dve.wait_ge(s("kv_mm"), q + 1)
                tt(sbd[0:D, :, :], PS[0:D, BANK_A, 256:512].rearrange("p (b n) -> p b n", b=4),
                   cst[0:D, C_BLK:C_BLK + D].rearrange("p (o n) -> p o n", o=1).broadcast_to([D, 4, D]), ALU.mult
                   ).then_inc(s("sbd_ready"), 1)

            def b_mask(q, n):
                b = n // 2
                for j in (2 * (n % 2), 2 * (n % 2) + 1):
                    dve.wait_ge(s("scores"), q * 16 + 4 * b + j + 1)
                    if j == 0 and (not isinstance(q, int) or 4 * q + b - 1 > 0):
                        dve.wait_ge(s("pv_done"), q * 4 + b - 1)
                    tt(probs[:, b % 2, j, :].rearrange("p (a n) -> p a n", a=2),
                       PS[:, j, :].rearrange("p (a n) -> p a n", a=2),
                       decay[:, j, :, :].rearrange("p (o g) c -> p o (g c)", o=1).broadcast_to([P, 2, 2 * CH]),
                       ALU.mult).then_inc(s("mask_done"), 1)

            def b_output_low(q):
                for k in range(2):
                    dve.wait_ge(s("ohi_ready"), q * 2 + k + 1)
                    hi = ostk[0:D, :].rearrange("p (b a n) -> p b a n", b=4, a=2)[:, :, k, :]
                    lo = ostk[D:P, :].rearrange("p (b a n) -> p b a n", b=4, a=2)[:, :, k, :]
                    tt(lo, PS[64 * k:64 * k + 64, BANK_O, :].rearrange("p (b n) -> p b n", b=4), hi, ALU.subtract
                       ).then_inc(s("olo_ready"), 1)

            def b_residual(q):
                hq = h_res[:, bass.ds(q * POS * D, POS * D)]
                dve.wait_ge(s("proj_mm"), q + 1)
                dve.wait_ge(s("h_bias"), q + 1)
                v.scalar_tensor_tensor(hq, PS[:, BANK_O, :], SW ** -2, hq, ALU.mult, ALU.add
                                       ).then_inc(s("h2_done"), 1)

            def quad(q, has_n, has_a, has_c):
                for n in range(8):
                    b_mask(q, n)
                    if n == 0:
                        b_masked_state(q)
                    if n == 0 and has_c:
                        c_stats(q - 1)
                    if n in (2, 3, 4, 5) and has_a:
                        a_stats(q + 2, (n - 2,))
                    if n == 6 and has_c:
                        c_logits(q - 1)
                    if n == 7 and has_c:
                        c_top2(q - 1)
                if has_a:
                    a_hidden_stats(q + 2)
                if has_n:
                    b_split(q + 1, (0, 1, 2, 3))
                if has_n:
                    if has_c:
                        c_top2_rest(q - 1)
                    b_output_low(q)
                    b_split(q + 1, (4, 5, 6, 7))
                    b_decayed_values(q + 1)
                    b_residual(q)
                    b_decayed_queries(q + 1)
                else:
                    b_output_low(q)
                    b_residual(q)

            a_stats(0, (2, 3))
            bc_split(1)
            a_hidden_stats(0)
            a_stats(1, (0, 1, 2, 3))
            dve.wait_ge(s("decay_ready"), 2)
            dve.wait_ge(s("ld_ffn"), 48)
            dve.wait_ge(s("wa_ready"), 1)
            ch.step(v.tensor_scalar(w2_sb[:, :, :], w2_sb[:, :, :], SW, None, ALU.mult))
            ch.step(v.tensor_scalar(b2_sb[:, :], b2_sb[:, :], SY, None, ALU.mult))
            ch.settle()
            for i in range(SPLITS):
                ch.step(v.tensor_copy(w2_hi[:, i, :, :], w2_sb[:, 4 * i:4 * i + 2, :]))
            ch.settle()
            for i in range(SPLITS):
                ch.step(tt(w2_lo[:, i, :, :], w2_sb[:, 4 * i:4 * i + 2, :], w2_hi[:, i, :, :], ALU.subtract))
            ch.settle()
            v.tensor_scalar(w2_sb[:, :, :], w2_sb[:, :, :], SH, None, ALU.mult).then_inc(s("w2_ready"), 1)
            b_split(0, range(4))
            a_hidden_stats(1)
            b_split(0, range(4, 8))
            b_decayed_values(0)
            b_decayed_queries(0)
            quad(0, True, True, False)
            with dve.Fori(1, NQ - 2) as q:
                ch.enter(q, 1, PER_QUAD)
                quad(q, True, True, True)
            ch.leave(NQ - 3)
            quad(NQ - 2, True, False, True)
            quad(NQ - 1, False, False, True)

            def split_hidden(q, i):
                for k in range(2):
                    dve.wait_ge(s("hid_hi"), q * 2 * SPLITS + 2 * i + k + 1)
                    v.scalar_tensor_tensor(hidden_part(i, k, 1), gring[:, (4 * i + k) % GR, :], SH,
                                           hidden_part(i, k, 0), ALU.mult, ALU.subtract).then_inc(s("hid_lo"), 1)

            c_stats(NQ - 1)
            c_top2_rest(NQ - 2)
            hq = h_res[:, (NQ - 1) * POS * D:NQ * POS * D].rearrange("p (c n) -> p c n", c=POS)
            dve.wait_ge(s("rstd_c"), NQ)
            ch.step(tt(xn2[:, :, :], hq, bc_d(stx["c"][:, 5, :], D), ALU.subtract))
            ch.settle()
            tt(xn2[:, :, :], xn2[:, :, :], bc_d(rstd["c"][:, :], D), ALU.mult).then_inc(s("c_xn"), 1)
            dve.wait_ge(s("c_xn"), NQ)
            dve.wait_ge(s("c_hi"), NQ)
            tt(xhl2[:, :, D:2 * D], xn2[:, :, :], xhl2[:, :, 0:D], ALU.subtract).then_inc(s("c_lo"), 1)
            split_hidden(0, 0)
            c_logits(NQ - 1)
            c_top2(NQ - 1)
            dve.wait_ge(s("r_ge"), NQ)
            flat = rge[:, :, :, :].rearrange("p c e j -> p c (e j)")
            low = cst[:, C_LOW:C_LOW + E * E].rearrange("p (o n) -> p o n", o=1).broadcast_to([P, POS, E * E])
            ch.step(tt(flat, flat, low, ALU.mult))
            ch.settle()
            tt(rdf[:, :, :, :], rge[:, :, :, :], rge[:, :, :, :].rearrange("p c e j -> p c j e"),
               ALU.subtract).then_inc(s("r_df"), 1)
            c_top2_rest(NQ - 1)

            def use_unit(q, unit):
                acc = PS[:, BANK_Q - 2 * (unit % 2):BANK_Q + 2 - 2 * (unit % 2), :]
                dve.wait_ge(s("l2_done"), q * 9 + 2 * unit + 1)
                y2 = yacc[:, :].rearrange("p (k n) -> p k n", k=2)
                if unit == 0:
                    if not isinstance(q, int) or q > 0:
                        dve.wait_ge(s("ylo_ready"), q)
                    v.tensor_scalar(y2, acc, b2_sb[:, 0:1], None, ALU.add).then_inc(s("y_used"), 1)
                    return
                pr = unit - 1
                dve.wait_ge(s(f"m_loaded{pr}"), q * 32 + 32)
                v.scalar_tensor_tensor(ytmp[:, :].rearrange("p (k n) -> p k n", k=2), acc, b2_sb[:, unit:unit + 1],
                                       mb[:, pr, :].rearrange("p (k n) -> p k n", k=2), ALU.add, ALU.mult
                                       ).then_inc(s("y_used"), 1)
                dve.wait_ge(s("y_used"), q * 5 + unit + 1)
                tt(yacc[:, :], yacc[:, :], ytmp[:, :], ALU.add).then_inc(s("m_used"), 1)
                dve.wait_ge(s("m_used"), q * 4 + unit)

            def y_split(q):
                if not isinstance(q, int) or q > 0:
                    dve.wait_ge(s("f_mm"), q)
                v.tensor_scalar(y_hi[:, :], yacc[:, :], 1.0 / SY, None, ALU.mult).then_inc(s("yhi_ready"), 1)
                dve.wait_ge(s("yhi_ready"), q + 1)
                v.scalar_tensor_tensor(y_lo[:, :], yacc[:, :], 1.0 / SY, y_hi[:, :], ALU.mult, ALU.subtract
                                       ).then_inc(s("ylo_ready"), 1)

            def finish(q):
                dve.wait_ge(s("f_mm"), q + 1)
                if not isinstance(q, int) or q > 0:
                    dve.wait_ge(s("out_done"), q * 16)
                tt(obuf[:, :], PS[:, BANK_Q, :], h_res[:, bass.ds(q * POS * D, POS * D)], ALU.add).then_inc(s("f_used"), 1)

            def ffn(q, has_fold, has_next):
                use_unit(q, 0)
                split_hidden(q, 1)
                if has_fold:
                    finish(q - 1)
                for unit in range(1, 5):
                    if unit + 1 < SPLITS:
                        split_hidden(q, unit + 1)
                    if unit == 4 and has_next:
                        split_hidden(q + 1, 0)
                    use_unit(q, unit)
                y_split(q)

            ffn(0, False, True)
            with dve.Fori(1, NQ - 1) as q:
                ffn(q, True, True)
            ffn(NQ - 1, True, False)
            finish(NQ - 1)

        @block.gpsimd
        def _(pool):
            g = nc.gpsimd
            chp = Steps(pool, s("pool_step"))
            g.memset(minus_half[:, :], -0.5).then_inc(s("half_ready"), 1)
            pool.wait_ge(s("half_ready"), 1)
            g.memset(table3[:, :, :], 0.0).then_inc(s("table3_zero"), 1)
            pool.wait_ge(s("table3_zero"), 1)

            def power(key, count, n=POS):
                pool.wait_ge(s("stats_" + key), count)
                g.tensor_tensor(rstd[key][:, 0:n], stx[key][:, 4, 0:n], minus_half[:, 0:n], ALU.pow
                                ).then_inc(s("rstd_" + key), 1)

            power("t", 1, 4)

            def split(raw, hi, lo, ready):
                chp.step(g.tensor_scalar(raw, raw, SW, 0.0, ALU.mult, ALU.add))
                chp.settle()
                chp.step(g.tensor_copy(hi, raw))
                chp.settle()
                g.tensor_tensor(lo, raw, hi, ALU.subtract).then_inc(s(ready), 1)

            g.memset(vx[:, :, :, :], 0.0).then_inc(s("zero_ready"), 1)
            g.memset(mtok[:, :], 0.0).then_inc(s("zero_ready"), 1)
            g.memset(sbd[:, :, :], 0.0).then_inc(s("zero_ready"), 1)
            chp.step(g.memset(top_row[:, :], 0.0))
            chp.settle()
            g.memset(top_row[0:1, :], 1.0).then_inc(s("top_ready"), 1)
            pool.wait_ge(s("top_ready"), 1)
            g.memset(qdec[64:128, :, :], 0.0).then_inc(s("zero_ready"), 1)
            pool.wait_ge(s("zero_ready"), 5)
            for c in range(POS):
                pool.wait_ge(s("tab_mid"), c + 1)
                g.tensor_tensor(table3[64:128, c, :], tab_rest[64:128, c % 2, :], table[64:128, c, :], ALU.subtract
                                ).then_inc(s("tab_ready"), 1)
            pool.wait_ge(s("tab_ready"), POS)
            pool.wait_ge(s("ld_attn"), 16)
            split(wa[:, :], wa_hi[:, :], wa_lo[:, :], "wa_ready")
            pool.wait_ge(s("wa_ready"), 1)
            def lag_sum(f, r, d):
                pool.wait_ge(s(f"t_g{f}"), 5 * r + d + 1)
                if d > 1:
                    pool.wait_ge(s(f"t_p{f}"), 2 * r + d - 1)
                g.tensor_tensor(pre[:, f, 0, :], pre[:, f, 0, :], pre[:, f, d, :], ALU.add).then_inc(s(f"t_p{f}"), 1)

            for w in range(2 * ROUNDS + 1):
                x, y, rx, ry = w % 2, (w + 1) % 2, w // 2, (w - 1) // 2
                if w < 2 * ROUNDS:
                    lag_sum(x, rx, 1)
                    pool.wait_ge(s(f"t_p{x}"), 2 * rx + 1)
                if w >= 1:
                    power("tu"[y], ry + 1 + (y == 0), 4)
                    if w < 2 * ROUNDS:
                        pool.wait_ge(s("rstd_" + "tu"[y]), ry + 1 + (y == 0))
                if w < 2 * ROUNDS:
                    lag_sum(x, rx, 2)
                    pool.wait_ge(s(f"t_p{x}"), 2 * rx + 2)
            def bc_d(x, width):
                return x.rearrange("p (c o) -> p c o", o=1).broadcast_to([P, POS, width])

            def bc_row(x):
                return x.rearrange("p (o n) -> p o n", o=1).broadcast_to([P, POS, D])

            def h_rows(q):
                return h_res[:, bass.ds(q * POS * D, POS * D)].rearrange("p (c n) -> p c n", c=POS)

            def a_hidden(q):
                power("f", q + 1)
                pool.wait_ge(s("rstd_f"), q + 1)
                pool.wait_ge(s("a_ucopy"), q * 4 + 4)
                g.tensor_tensor(xn[:, :, :], u_sb[:, :, :], bc_d(rstd["f"][:, :], D), ALU.mult
                                ).then_inc(s("a_u_used"), 1)
                pool.wait_ge(s("a_u_used"), q + 1)
                g.tensor_tensor(h_rows(q), xn[:, :, :], bc_row(hb[:, :]), ALU.add).then_inc(s("a_h"), 1)

            def normalize(q, key, x, x_hl):
                power(key, q + 1)
                chp.step(g.tensor_tensor(x[:, :, :], h_rows(q), bc_d(stx[key][:, 5, :], D), ALU.subtract))
                chp.settle()
                pool.wait_ge(s("rstd_" + key), q + 1)
                g.tensor_tensor(x[:, :, :], x[:, :, :], bc_d(rstd[key][:, :], D), ALU.mult
                                ).then_inc(s(key + "_xn"), 1)
                if key == "a":
                    g.tensor_tensor(h_rows(q), h_rows(q), bc_row(bproj_bc[:, :]), ALU.add).then_inc(s("h_bias"), 1)
                pool.wait_ge(s(key + "_xn"), q + 1)
                pool.wait_ge(s(key + "_hi"), q + 1)
                g.tensor_tensor(x_hl[:, :, D:2 * D], x[:, :, :], x_hl[:, :, 0:D], ALU.subtract
                                ).then_inc(s(key + "_lo"), 1)

            def c_ranks(q):
                low = cst[:, C_LOW:C_LOW + E * E].rearrange("p (o n) -> p o n", o=1).broadcast_to([P, POS, E * E])
                flat = rge[:, :, :, :].rearrange("p c e j -> p c (e j)")
                pool.wait_ge(s("r_ge"), q + 1)
                chp.step(g.tensor_tensor(flat, flat, low, ALU.mult))
                chp.settle()
                g.tensor_tensor(rdf[:, :, :, :], rge[:, :, :, :], rge[:, :, :, :].rearrange("p c e j -> p c j e"),
                                ALU.subtract).then_inc(s("r_df"), 1)

            def quad(q, has_n, has_a, has_c):
                if has_n:
                    normalize(q + 1, "a", xn, xhl)
                if has_c:
                    normalize(q - 1, "c", xn2, xhl2)
                if has_a:
                    a_hidden(q + 2)
                if has_c:
                    c_ranks(q - 1)

            pool.wait_ge(s("hb_ready"), 1)
            pool.wait_ge(s("ld_rows"), 32)
            a_hidden(0)
            normalize(0, "a", xn, xhl)
            a_hidden(1)
            normalize(1, "a", xn, xhl)
            pool.wait_ge(s("ld_w1"), 16)
            pool.wait_ge(s("a_lo"), 2)
            w1_f = w1_raw.rearrange("p (t n) -> p t n", t=NT1)
            chp.step(g.tensor_scalar(w1_f, w1_f, SW, 0.0, ALU.mult, ALU.add))
            chp.settle()
            chp.step(g.tensor_copy(w1_hi[:, :, :], w1_f))
            chp.settle()
            a_hidden(2)
            pool.wait_ge(s("a_h"), 3)
            g.tensor_tensor(w1_lo[:, :, :], w1_f, w1_hi[:, :, :], ALU.subtract).then_inc(s("w1_ready"), 1)
            pool.wait_ge(s("w1_ready"), 1)
            with pool.Fori(1, NQ - 2) as q:
                chp.enter(q, 1, POOL_PER_QUAD)
                quad(q, True, True, True)
            chp.leave(NQ - 3)
            quad(NQ - 2, True, False, True)
            quad(NQ - 1, False, False, True)
            power("c", NQ)


_INS = ["ids", "emb", "pos", "consts", "towerw", "towerb", "updb2", "attnw", "bproj", "slopes", "w1", "b1", "w2", "b2"]


def shape_constants():
    import numpy as np
    c = np.zeros((P, C_END), np.float32)
    c[:, C_ID:C_ID + P] = np.eye(P)
    c[:, C_CEN:C_CEN + P] = np.eye(P) - 1.0 / DT
    e, t = np.arange(CH)[:, None], np.arange(CH)[None, :]
    c[:, C_DIFF:C_DIFF + CH] = np.maximum(t - e, 0)
    c[:, C_CAUS:C_CAUS + CH] = (t >= e) * (DH ** -0.5 / SW ** 2)
    c[:, C_II:C_II + D] = np.vstack([np.eye(D), np.eye(D)])
    hd = np.arange(D) // DH
    c[0:D, C_BLK:C_BLK + D] = hd[:, None] == hd[None, :]
    j = np.arange(E)
    c[:, C_THR:C_THR + E] = 2.0 - (E - 1 - j)
    c[:, C_LOW:C_LOW + E * E] = (j[None, :] < j[:, None]).reshape(-1)
    p = np.arange(P)
    c[:, C_COL] = p % VOCAB
    c[:, C_COL + 1] = -1.0 * (p // 16 % 2)
    c[:, C_COL + 2] = -1.0 * (p // 8 % 2)
    c[:, C_COL + 3] = -1.0 * (p // 64)
    c[:, C_COL + 4] = -1.0 * (CH - p)
    c[:, C_INV:C_INV + CPB] = 1.0 / np.minimum(np.arange(CPB) + 1, WIN + 1)
    c[:, C_NEGC:C_NEGC + CH] = -np.arange(CH)
    return c


def laid_out(inputs):
    import numpy as np

    a = {k: np.asarray(v) for k, v in inputs.items()}
    t = {k[7:]: v for k, v in a.items() if k.startswith("L0_tok_")}
    w = {k[8:]: v for k, v in a.items() if k.startswith("L0_attn_")}
    m = {k[7:]: v for k, v in a.items() if k.startswith("L0_ffn_")}

    def tiles(x, n):
        return np.concatenate([x[P * i:P * (i + 1)] for i in range(n)], axis=1)

    def col(x):
        return x.reshape(-1, P).T

    def slots(x):
        return np.repeat(x.reshape(D, H, 1, DH), 4, axis=2).reshape(D, H * 4 * DH)

    wq, wk, wv = (w["w_qkv"][:, k * D:(k + 1) * D] for k in range(3))
    attnw = np.concatenate([slots(wq), slots(wk), wv, wk, wq, w["w_proj"], m["Wr"]], axis=1)
    w1t = [m["W1s"][:, :P], m["W1s"][:, P:]]
    b1t = [m["b1s"][:P], m["b1s"][P:]]
    w2t = [m["W2s"][:P], m["W2s"][P:]]
    for pr in range(E // 2):
        for f in range(2):
            for e in (2 * pr, 2 * pr + 1):
                w1t.append(m["W1p"][e][:, f * P:(f + 1) * P])
                b1t.append(m["b1p"][e][f * P:(f + 1) * P])
                w2t.append(m["W2p"][e][f * P:(f + 1) * P])
    w1 = np.concatenate(w1t, axis=1)
    zero = np.zeros_like(m["b2s"])
    arrays = {
        "ids": a["x"].reshape(NCHUNK, POS).T.reshape(-1),
        "emb": t["emb"], "pos": t["pos"], "consts": shape_constants(),
        "towerw": np.concatenate([t["lw1"], tiles(t["lw2"], 2), tiles(t["msg_w1"], 2), t["msg_w2"],
                                  tiles(t["upd_w1"], 2), t["upd_w2"], t["pool_w"], t["bc_w"], t["bc_w"].T,
                                  t["head_w"]], axis=1),
        "towerb": np.concatenate([col(t[k]) for k in (
            "lb1", "lb2", "lln_g", "lln_b", "pool_b", "msg_b1", "msg_b2", "upd_b1", "mln_g", "mln_b", "bc_b",
            "fln_g", "fln_b")], axis=1),
        "updb2": t["upd_b2"], "attnw": np.concatenate([attnw, attnw], axis=0), "bproj": w["b_proj"],
        "slopes": w["slopes"], "w1": np.concatenate([w1, w1], axis=0), "b1": np.stack(b1t, axis=1),
        "w2": np.concatenate(w2t, axis=1),
        "b2": np.stack([np.concatenate([m["b2s"], zero])] +
                       [m["b2p"][2 * pr:2 * pr + 2].reshape(-1) for pr in range(E // 2)], axis=1),
    }
    return {name: np.ascontiguousarray(arrays[name]) for name in _INS}


def kernel(**inputs):
    import concourse.bacc as bacc
    from concourse.bass_utils import run_bass_kernel_spmd

    arrays = laid_out(inputs)
    nc = bacc.Bacc("TRN2", target_bir_lowering=False, num_devices=1)
    args = {}
    for name in _INS:
        args[name] = nc.dram_tensor(f"in_{name}", arrays[name].shape, mybir.dt.from_np(arrays[name].dtype),
                                    kind="ExternalInput").ap()
    args["out"] = nc.dram_tensor("out_0", (NB, SEQ, D), F32, kind="ExternalOutput").ap()
    build(nc, **args)
    r = run_bass_kernel_spmd(nc, [{f"in_{k}": v for k, v in arrays.items()}], core_ids=[0])
    return r.results[0]["out_0"]
```
